# Optimizing a Trainium2 kernel written in Bass

```python
import numpy as np
import jax
import jax.numpy as jnp

def _softmax(x, axis=-1):
    return jax.nn.softmax(x, axis=axis)

def _gelu(x):
    return jax.nn.gelu(x, approximate=True)

def _silu(x):
    return jax.nn.silu(x)

def _sigmoid(x):
    return jax.nn.sigmoid(x)

def _layernorm(x, axis=-1, eps=1e-05):
    m = jnp.mean(x, axis=axis, keepdims=True)
    v = jnp.var(x, axis=axis, keepdims=True)
    return (x - m) / jnp.sqrt(v + eps)

def _scatter_add(tgt, idx, src, axis=0):
    return tgt.at[idx].add(src)

def _segment_sum(src, seg, n):
    return jax.ops.segment_sum(src, seg, n)
kernel_name = 'mk_seq_preln_d2_jaxref_r8_5f078e'

def setup_inputs(seed: int=0):
    np.random.seed(seed)
    _w = jnp.asarray

    def _L0_attn_setup():
        import jax, jax.numpy as jnp
        import numpy as np
        B, N, D = (2, 256, 128)
        H, DH = (16, 64)
        SOFTCLAMP = 50.0
        SCALE = DH ** (-0.5)
        key = jax.random.key(seed)
        ks = jax.random.split(key, 5)
        std = D ** (-0.5)
        return {'x': jax.random.normal(ks[0], (B, N, D), dtype=jnp.float32), 'Wq': jax.random.normal(ks[1], (H * DH, D), dtype=jnp.float32) * std, 'Wk': jax.random.normal(ks[2], (H * DH, D), dtype=jnp.float32) * std, 'Wv': jax.random.normal(ks[3], (H * DH, D), dtype=jnp.float32) * std, 'Wo': jax.random.normal(ks[4], (D, H * DH), dtype=jnp.float32) * std}
    _L0_attn_in = _L0_attn_setup()

    def _L0_ffn_setup():
        import jax, jax.numpy as jnp
        import numpy as np
        D_MODEL = 128
        D_FF = 512
        NUM_EXPERTS = 8
        key = jax.random.key(seed)
        ks = jax.random.split(key, 8)
        scale_in = 1.0 / np.sqrt(D_MODEL)
        scale_ff = 1.0 / np.sqrt(D_FF)
        x = jax.random.normal(ks[0], (4, 256, D_MODEL), dtype=jnp.float32)
        gate_w = jax.random.uniform(ks[1], (NUM_EXPERTS, D_MODEL), jnp.float32, -scale_in, scale_in)
        gate_b = jax.random.uniform(ks[2], (NUM_EXPERTS,), jnp.float32, -scale_in, scale_in)
        expert_bias = jnp.zeros((NUM_EXPERTS,), dtype=jnp.float32)
        w1 = jax.random.uniform(ks[3], (NUM_EXPERTS, D_MODEL, D_FF), jnp.float32, -scale_in, scale_in)
        b1 = jax.random.uniform(ks[4], (NUM_EXPERTS, D_FF), jnp.float32, -scale_in, scale_in)
        w2 = jax.random.uniform(ks[5], (NUM_EXPERTS, D_FF, D_MODEL), jnp.float32, -scale_ff, scale_ff)
        b2 = jax.random.uniform(ks[6], (NUM_EXPERTS, D_MODEL), jnp.float32, -scale_ff, scale_ff)
        return {'x': x, 'gate_w': gate_w, 'gate_b': gate_b, 'expert_bias': expert_bias, 'w1': w1, 'b1': b1, 'w2': w2, 'b2': b2}
    _L0_ffn_in = _L0_ffn_setup()

    def _L1_attn_setup():
        import jax, jax.numpy as jnp
        import numpy as np
        N_HEAD = 16
        PAGE_SIZE = 32
        ROPE_THETA = 10000.0

        def _rope_tables(T, D, dtype):
            inv = 1.0 / ROPE_THETA ** (np.arange(0, D, 2, dtype=np.float32) / D)
            ang = np.outer(np.arange(T, dtype=np.float32), inv)
            return (jnp.asarray(np.cos(ang), dtype), jnp.asarray(np.sin(ang), dtype))

        def _apply_rope(x, cos, sin):
            x1 = x[..., 0::2]
            x2 = x[..., 1::2]
            c = cos[None, :, None, :]
            s = sin[None, :, None, :]
            out = jnp.stack([x1 * c - x2 * s, x1 * s + x2 * c], axis=-1)
            return out.reshape(x.shape)
        key = jax.random.key(seed)
        ks = jax.random.split(key, 6)
        B, T, E = (2, 256, 128)
        L = E // 2
        sc = lambda fan: 1.0 / np.sqrt(fan)
        return {'x': jax.random.normal(ks[0], (B, T, E), jnp.float32), 'wq': jax.random.normal(ks[1], (E, E), jnp.float32) * sc(E), 'w_down': jax.random.normal(ks[2], (E, L), jnp.float32) * sc(E), 'wk_up': jax.random.normal(ks[3], (L, E), jnp.float32) * sc(L), 'wv_up': jax.random.normal(ks[4], (L, E), jnp.float32) * sc(L), 'wo': jax.random.normal(ks[5], (E, E), jnp.float32) * sc(E)}
    _L1_attn_in = _L1_attn_setup()

    def _L1_ffn_setup():
        import jax, jax.numpy as jnp
        import numpy as np
        DIM = 128
        HIDDEN = 512
        E = 8
        K = 2

        def _ffn_hidden(h, multiple_of=32):
            h = int(2 * h / 3)
            return multiple_of * ((h + multiple_of - 1) // multiple_of)
        EXP_HID = _ffn_hidden(HIDDEN)
        SH_HID = _ffn_hidden(HIDDEN // 2)

        def _swiglu(t, a, b, c):
            return jax.nn.silu(t @ a) * (t @ c) @ b
        key = jax.random.key(seed)
        ks = jax.random.split(key, 8)

        def xavier(k, shape, fan_in, fan_out):
            lim = np.sqrt(6.0 / (fan_in + fan_out)).astype(np.float32)
            return jax.random.uniform(k, shape, jnp.float32, -lim, lim)
        return {'x': jax.random.normal(ks[0], (2, 256, DIM), jnp.float32), 'gate_w': xavier(ks[1], (E, DIM), DIM, E), 'w1': xavier(ks[2], (E, DIM, EXP_HID), DIM, EXP_HID), 'w2': xavier(ks[3], (E, EXP_HID, DIM), EXP_HID, DIM), 'w3': xavier(ks[4], (E, DIM, EXP_HID), DIM, EXP_HID), 'sw1': xavier(ks[5], (DIM, SH_HID), DIM, SH_HID), 'sw2': xavier(ks[6], (SH_HID, DIM), SH_HID, DIM), 'sw3': xavier(ks[7], (DIM, SH_HID), DIM, SH_HID)}
    _L1_ffn_in = _L1_ffn_setup()
    _d = {'L0_attn_x': _L0_attn_in['x'], 'L0_attn_Wq': _L0_attn_in['Wq'], 'L0_attn_Wk': _L0_attn_in['Wk'], 'L0_attn_Wv': _L0_attn_in['Wv'], 'L0_attn_Wo': _L0_attn_in['Wo'], 'L0_ffn_gate_w': _L0_ffn_in['gate_w'], 'L0_ffn_gate_b': _L0_ffn_in['gate_b'], 'L0_ffn_expert_bias': _L0_ffn_in['expert_bias'], 'L0_ffn_w1': _L0_ffn_in['w1'], 'L0_ffn_b1': _L0_ffn_in['b1'], 'L0_ffn_w2': _L0_ffn_in['w2'], 'L0_ffn_b2': _L0_ffn_in['b2'], 'L1_attn_wq': _L1_attn_in['wq'], 'L1_attn_w_down': _L1_attn_in['w_down'], 'L1_attn_wk_up': _L1_attn_in['wk_up'], 'L1_attn_wv_up': _L1_attn_in['wv_up'], 'L1_attn_wo': _L1_attn_in['wo'], 'L1_ffn_gate_w': _L1_ffn_in['gate_w'], 'L1_ffn_w1': _L1_ffn_in['w1'], 'L1_ffn_w2': _L1_ffn_in['w2'], 'L1_ffn_w3': _L1_ffn_in['w3'], 'L1_ffn_sw1': _L1_ffn_in['sw1'], 'L1_ffn_sw2': _L1_ffn_in['sw2'], 'L1_ffn_sw3': _L1_ffn_in['sw3']}
    _x0 = _d['L0_attn_x']
    _d['L0_attn_x'] = jax.random.normal(jax.random.fold_in(jax.random.key(seed), 1), (4, 1024, 128), dtype=_x0.dtype)
    del _x0
    return _d

def reference(L0_attn_x, L0_attn_Wq, L0_attn_Wk, L0_attn_Wv, L0_attn_Wo, L0_ffn_gate_w, L0_ffn_gate_b, L0_ffn_expert_bias, L0_ffn_w1, L0_ffn_b1, L0_ffn_w2, L0_ffn_b2, L1_attn_wq, L1_attn_w_down, L1_attn_wk_up, L1_attn_wv_up, L1_attn_wo, L1_ffn_gate_w, L1_ffn_w1, L1_ffn_w2, L1_ffn_w3, L1_ffn_sw1, L1_ffn_sw2, L1_ffn_sw3):

    def _L0_attn_ref(x, Wq, Wk, Wv, Wo):
        import jax, jax.numpy as jnp
        import numpy as np
        B, N, D = (2, 256, 128)
        H, DH = (16, 64)
        SOFTCLAMP = 50.0
        SCALE = DH ** (-0.5)
        b, n, _ = x.shape
        q = jnp.einsum('bnd,fd->bnf', x, Wq).reshape(b, n, H, DH).transpose(0, 2, 1, 3)
        k = jnp.einsum('bnd,fd->bnf', x, Wk).reshape(b, n, H, DH).transpose(0, 2, 1, 3)
        v = jnp.einsum('bnd,fd->bnf', x, Wv).reshape(b, n, H, DH).transpose(0, 2, 1, 3)
        sim = jnp.einsum('bhid,bhjd->bhij', q, k) * SCALE
        sim = SOFTCLAMP * jnp.tanh(sim / SOFTCLAMP)
        causal = jnp.tril(jnp.ones((n, n), dtype=bool))
        sim = jnp.where(causal, sim, jnp.finfo(sim.dtype).min)
        attn = jax.nn.softmax(sim, axis=-1)
        out = jnp.einsum('bhij,bhjd->bhid', attn, v)
        out = out.transpose(0, 2, 1, 3).reshape(b, n, H * DH)
        return jnp.einsum('bnf,df->bnd', out, Wo)

    def _L0_ffn_ref(x, gate_w, gate_b, expert_bias, w1, b1, w2, b2):
        import jax, jax.numpy as jnp
        import numpy as np
        D_MODEL = 128
        D_FF = 512
        NUM_EXPERTS = 8
        gate_logits = jnp.einsum('bsd,ed->bse', x, gate_w) + gate_b + expert_bias
        top_idx = jnp.argmax(gate_logits, axis=-1)
        out = jnp.zeros_like(x)
        for e in range(NUM_EXPERTS):
            mask = (top_idx == e)[..., None].astype(x.dtype)
            h = jax.nn.relu(jnp.einsum('bsd,df->bsf', x, w1[e]) + b1[e])
            y = jnp.einsum('bsf,fd->bsd', h, w2[e]) + b2[e]
            out = out + mask * y
        return out

    def _L1_attn_ref(x, wq, w_down, wk_up, wv_up, wo):
        import jax, jax.numpy as jnp
        import numpy as np
        N_HEAD = 16
        PAGE_SIZE = 32
        ROPE_THETA = 10000.0

        def _rope_tables(T, D, dtype):
            inv = 1.0 / ROPE_THETA ** (np.arange(0, D, 2, dtype=np.float32) / D)
            ang = np.outer(np.arange(T, dtype=np.float32), inv)
            return (jnp.asarray(np.cos(ang), dtype), jnp.asarray(np.sin(ang), dtype))

        def _apply_rope(x, cos, sin):
            x1 = x[..., 0::2]
            x2 = x[..., 1::2]
            c = cos[None, :, None, :]
            s = sin[None, :, None, :]
            out = jnp.stack([x1 * c - x2 * s, x1 * s + x2 * c], axis=-1)
            return out.reshape(x.shape)
        B, T, E = x.shape
        H = N_HEAD
        D = E // H
        q = (x @ wq).reshape(B, T, H, D)
        lat = x @ w_down
        k = (lat @ wk_up).reshape(B, T, H, D)
        v = (lat @ wv_up).reshape(B, T, H, D)
        cos, sin = _rope_tables(T, D, x.dtype)
        q = _apply_rope(q, cos, sin)
        k = _apply_rope(k, cos, sin)
        scale = 1.0 / jnp.sqrt(jnp.asarray(D, x.dtype))
        scores = jnp.einsum('bqhd,bkhd->bhqk', q, k) * scale
        pages = jnp.arange(T) // PAGE_SIZE
        allowed = pages[None, :] <= pages[:, None]
        scores = jnp.where(allowed[None, None], scores, jnp.finfo(scores.dtype).min)
        attn = jax.nn.softmax(scores, axis=-1)
        out = jnp.einsum('bhqk,bkhd->bqhd', attn, v).reshape(B, T, E)
        return out @ wo

    def _L1_ffn_ref(x, gate_w, w1, w2, w3, sw1, sw2, sw3):
        import jax, jax.numpy as jnp
        import numpy as np
        DIM = 128
        HIDDEN = 512
        E = 8
        K = 2

        def _ffn_hidden(h, multiple_of=32):
            h = int(2 * h / 3)
            return multiple_of * ((h + multiple_of - 1) // multiple_of)
        EXP_HID = _ffn_hidden(HIDDEN)
        SH_HID = _ffn_hidden(HIDDEN // 2)

        def _swiglu(t, a, b, c):
            return jax.nn.silu(t @ a) * (t @ c) @ b
        B, S, D = x.shape
        xt = x.reshape(-1, D)
        T = xt.shape[0]
        logits = xt @ gate_w.T
        scores = jax.nn.softmax(logits, axis=-1)
        topk_w, topk_i = jax.lax.top_k(scores, K)
        comb = jnp.zeros((T, E), x.dtype).at[jnp.arange(T)[:, None], topk_i].add(topk_w)
        y = jnp.zeros_like(xt)
        for e in range(E):
            y = y + comb[:, e:e + 1] * _swiglu(xt, w1[e], w2[e], w3[e])
        y = y.reshape(B, S, D)
        return y + _swiglu(x, sw1, sw2, sw3)
    x = L0_attn_x
    x = x + _L0_attn_ref(_layernorm(x, axis=-1), L0_attn_Wq, L0_attn_Wk, L0_attn_Wv, L0_attn_Wo)
    x = x + _L0_ffn_ref(_layernorm(x, axis=-1), L0_ffn_gate_w, L0_ffn_gate_b, L0_ffn_expert_bias, L0_ffn_w1, L0_ffn_b1, L0_ffn_w2, L0_ffn_b2)
    x = x + _L1_attn_ref(_layernorm(x, axis=-1), L1_attn_wq, L1_attn_w_down, L1_attn_wk_up, L1_attn_wv_up, L1_attn_wo)
    x = x + _L1_ffn_ref(_layernorm(x, axis=-1), L1_ffn_gate_w, L1_ffn_w1, L1_ffn_w2, L1_ffn_w3, L1_ffn_sw1, L1_ffn_sw2, L1_ffn_sw3)
    return x

_drawn_inputs = setup_inputs


def setup_inputs(seed=0):
    import zlib

    import numpy as np

    out = dict(_drawn_inputs(seed))
    spreads = {'L0_ffn_expert_bias': (0.0, 0.1)}
    factors = {}
    for name, (base, spread) in spreads.items():
        noise = np.random.default_rng([zlib.crc32(name.encode()), seed]).standard_normal(out[name].shape)
        drawn = base * np.exp(spread * noise) if base else spread * noise
        out[name] = jnp.asarray(drawn.astype(out[name].dtype))
    for name, factor in factors.items():
        out[name] = (out[name] * factor).astype(out[name].dtype)
    return out
```

```python
from contextlib import ExitStack

import concourse.bass as bass
from concourse import mybir

ACT = mybir.ActivationFunctionType
ALU = mybir.AluOpType
AX_X = mybir.AxisListType.X
F32 = mybir.dt.float32
F32R = mybir.dt.float32r
BF16 = mybir.dt.bfloat16
I32 = mybir.dt.int32
U32 = mybir.dt.uint32

P = 128
D = 128
BATCH, SEQ = 4, 1024
TILES = SEQ // P
TOKENS = BATCH * SEQ
ALL_TILES = TOKENS // P
HALF = 512
LN_EPS = 1e-5


def ge(eng, sem, value):
    if isinstance(value, int) and value <= 0:
        return
    eng.wait_ge(sem, value)


class Kit:

    def __init__(self, nc, ctx, passed):
        self.nc, self.ctx, self.passed = nc, ctx, passed

    def scope(self, ctx):
        return Kit(self.nc, ctx, self.passed)

    def sb(self, name, shape, dt=F32):
        return self.ctx.enter_context(self.nc.sbuf_tensor(name, shape, dt))

    def ps(self, name, shape, dt=F32):
        return self.ctx.enter_context(self.nc.psum_tensor(name, shape, dt))

    def ge_apart(self, eng, sem, value):
        ge(eng, sem, value)
        if not isinstance(value, int):
            eng.sem_inc(self.passed, 1)


def load_residual(nc, kit, sem, x_dram, x, ident, ones, eps):
    loaded, made = sem("x_loaded"), sem("consts_made")
    with nc.Block() as block:

        @block.sync
        def _(sp):
            for b in range(BATCH):
                sp.dma_start(x[:, b * TILES:(b + 1) * TILES, :],
                             x_dram[b].rearrange("(t p) d -> p t d", p=P)).then_inc(loaded, 16)
            sp.wait_ge(loaded, 16 * BATCH)

        @block.gpsimd
        def _(pool):
            nc.gpsimd.memset(ident[:], 0.0).then_inc(made, 1)
            nc.gpsimd.memset(ones[:], 1.0).then_inc(made, 1)
            nc.gpsimd.memset(eps[:], LN_EPS).then_inc(made, 1)
            kit.ge_apart(pool, made, 3)
            nc.gpsimd.affine_select(out=ident[:], in_=ident[:], compare_op=ALU.not_equal, fill=1.0, base=0,
                                    pattern=[[1, P]], channel_multiplier=-1).then_inc(made, 1)
            kit.ge_apart(pool, made, 4)


def layernorm(nc, kit, sem, tag, x, ident, eps, xt_dram):
    with ExitStack() as ctx:
        k = kit.scope(ctx)
        stats = k.sb(f"{tag}_stats", [P, TILES, 6])
        mv = k.sb(f"{tag}_mv", [P, TILES, 2])
        std = k.sb(f"{tag}_std", [P, TILES])
        rstd = k.sb(f"{tag}_rstd", [P, TILES])
        xn = k.sb(f"{tag}_xn", [P, TILES, D])
        xt = k.sb(f"{tag}_xt", [P, SEQ])
        high = k.sb(f"{tag}_high", [P, SEQ], F32R)
        low = k.sb(f"{tag}_low", [P, SEQ], F32R)
        turned = k.ps(f"{tag}_turned", [P, SEQ])
        stats_done, mv_done = sem(f"{tag}_stats"), sem(f"{tag}_mv")
        std_done, rstd_done = sem(f"{tag}_std"), sem(f"{tag}_rstd")
        xn_done, turn_done = sem(f"{tag}_xn"), sem(f"{tag}_turn")
        xt_done, high_done, low_done = sem(f"{tag}_xt"), sem(f"{tag}_high"), sem(f"{tag}_low")
        stored, out_free = sem(f"{tag}_stored"), sem(f"{tag}_out_free")
        xflat = x[:].rearrange("p t d -> p (t d)")

        with nc.Block() as block:

            @block.vector
            def _(dve):
                with dve.Fori(0, BATCH) as b:
                    for t in range(TILES):
                        last = nc.vector.bn_stats(stats[:, t, :], xflat[:, bass.ds(b * (TILES * D) + t * D, D)])
                    last.then_inc(stats_done, 1)
                    kit.ge_apart(dve, stats_done, b + 1)
                    for t in range(TILES):
                        last = nc.vector.bn_aggr(mv[:, t, :], stats[:, t, :])
                    last.then_inc(mv_done, 1)
                    dve.wait_ge(std_done, b + 1)
                    nc.vector.reciprocal(rstd[:], std[:]).then_inc(rstd_done, 1)
                    dve.wait_ge(rstd_done, b + 1)
                    for t in range(TILES):
                        last = nc.vector.tensor_scalar(xn[:, t, :], xflat[:, bass.ds(b * (TILES * D) + t * D, D)],
                                                       mv[:, t, 0:1], rstd[:, t:t + 1], ALU.subtract, ALU.mult)
                    last.then_inc(xn_done, 1)
                    dve.wait_ge(high_done, b + 1)
                    nc.vector.tensor_tensor(low[:], xt[:], high[:].bitcast(F32), ALU.subtract).then_inc(low_done, 1)

            @block.scalar
            def _(act):
                with act.Fori(0, BATCH) as b:
                    act.wait_ge(mv_done, b + 1)
                    nc.scalar.activation(std[:], mv[:, :, 1], ACT.Sqrt, bias=eps[:, 0:1]).then_inc(std_done, 1)
                    act.wait_ge(turn_done, b + 1)
                    act.wait_ge(out_free, b + 1)
                    nc.scalar.copy(xt[:], turned[:]).then_inc(xt_done, 1)
                    nc.scalar.copy(high[:], turned[:]).then_inc(high_done, 1)

            @block.tensor
            def _(pe):
                with pe.Fori(0, BATCH) as b:
                    pe.wait_ge(xn_done, b + 1)
                    for t in range(TILES):
                        last = nc.tensor.transpose(turned[:, t * P:(t + 1) * P], xn[:, t, :], ident[:])
                    last.then_inc(turn_done, 1)

            @block.sync
            def _(sp):
                sp.sem_inc(out_free, 1)
                with sp.Fori(0, BATCH) as b:
                    out = xt_dram[bass.ds(b, 1)].rearrange("b k p s -> (b k) p s")
                    sp.wait_ge(xt_done, b + 1)
                    sp.dma_start(out[0], xt[:]).then_inc(stored, 16)
                    sp.wait_ge(high_done, b + 1)
                    sp.dma_start(out[1], high[:].bitcast(F32)).then_inc(stored, 16)
                    sp.wait_ge(low_done, b + 1)
                    sp.dma_start(out[2], low[:].bitcast(F32)).then_inc(stored, 16)
                    sp.wait_ge(stored, b * 48 + 48)
                    sp.sem_inc(out_free, 1)


def chunk_plan():
    chunks, at = [], 0
    for half in range(2):
        for j in range(TILES):
            lead = max(0, j * P - half * HALF)
            if lead >= HALF:
                continue
            chunks.append((half, j, HALF - lead, at))
            at += 2 * (HALF - lead)
    return chunks, at


CHUNKS, P_COLS = chunk_plan()
NCH = len(CHUNKS)
GROUPS = [(0, 4), (4, 6), (6, 8), (8, 12)]
DIAGONAL_GROUPS = (0, 3)


def attention0(nc, kit, sem, x, xt_dram, w_dram, ones, scale, clamp):
    PAIRS = w_dram.shape[0]
    UNITS = BATCH * PAIRS
    DH = P // 2
    SEQ_BITS = PAIRS.bit_length() - 1
    with ExitStack() as ctx:
        k = kit.scope(ctx)
        xt = k.sb("a0_xt", [P, SEQ])
        xh = [k.sb(f"a0_xh{i}", [P, SEQ], F32R) for i in range(2)]
        xl = [k.sb(f"a0_xl{i}", [P, SEQ], F32R) for i in range(2)]
        w = [k.sb(f"a0_w{i}", [P, 2, P]) for i in range(2)]
        wv = [k.sb(f"a0_wv{i}", [P, P]) for i in range(2)]
        wo = [k.sb(f"a0_wo{i}", [P, P]) for i in range(2)]
        wh = [k.sb(f"a0_wh{i}", [P, 2, P], F32R) for i in range(2)]
        wl = [k.sb(f"a0_wl{i}", [P, 2, P], F32R) for i in range(2)]
        stage = k.sb("a0_stage", [P, 2, 2, SEQ], F32R)
        q_st = [k.sb(f"a0_q{i}", [P, 2, SEQ], F32R) for i in range(2)]
        kh_st = [k.sb(f"a0_kh{i}", [P, 2, SEQ], F32R) for i in range(2)]
        kl_st = [k.sb(f"a0_kl{i}", [P, 2, SEQ], F32R) for i in range(2)]
        v = [k.sb(f"a0_v{i}", [P, TILES, P]) for i in range(2)]
        prob = [k.sb(f"a0_p{i}", [P, P_COLS]) for i in range(2)]
        part = k.sb("a0_part", [P, 2, SEQ])
        rsum = k.sb("a0_rsum", [P, HALF])
        rhl = k.sb("a0_rhl", [P, 2, HALF], F32R)
        spread = k.sb("a0_spread", [P, 2, P], F32R)
        ot = k.sb("a0_ot", [P, SEQ])
        score_ps = k.ps("a0_score", [P, 2, 2, HALF])
        out_ps = k.ps("a0_out", [P, 2, HALF])
        misc = k.ps("a0_misc", [P, 2, HALF])

        x_loaded = [sem(f"a0_x_loaded{i}") for i in range(2)]
        xt_loaded = sem("a0_xt_loaded")
        w_loaded = [sem(f"a0_w_loaded{i}") for i in range(2)]
        wv_loaded = [sem(f"a0_wv_loaded{i}") for i in range(2)]
        wo_loaded = [sem(f"a0_wo_loaded{i}") for i in range(2)]
        w_high, w_split = sem("a0_w_high"), sem("a0_w_split")
        NAMES = ["q0", "q1", "k0", "k1", "v0", "v1"]
        proj = {n: sem(f"a0_proj_{n}") for n in NAMES}
        evac = {n: sem(f"a0_evac_{n}") for n in NAMES}
        high = {n: sem(f"a0_high_{n}") for n in NAMES[:4]}
        stacked = sem("a0_stacked")
        scored, tanh_done, exp_done, masked = (sem(f"a0_{n}") for n in ("scored", "tanh", "exp", "masked"))
        pv_done = [sem(f"a0_pv{i}") for i in range(2)]
        added = sem("a0_added")
        summed, recip, r_high, r_split = (sem(f"a0_{n}") for n in ("summed", "recip", "r_high", "r_split"))
        spread_made = sem("a0_spread_made")
        out_evac = [sem(f"a0_out_evac{i}") for i in range(2)]
        bcast = [sem(f"a0_bcast{i}") for i in range(2)]
        normed = [sem(f"a0_normed{i}") for i in range(2)]
        wo_done = [sem(f"a0_wo{i}") for i in range(2)]
        x_added = [sem(f"a0_x_added{i}") for i in range(2)]
        QK_JOBS, V_JOBS = {0: "q0", 2: "k0", 3: "q1", 5: "k1"}, {4: 0, 7: 1}
        ADDS = NCH - 1
        STACK_DMAS = 12
        xflat = x[:].rearrange("p t d -> p (t d)")

        def of(dram, index):
            if isinstance(index, int):
                return dram[index]
            names = " ".join("abcde"[:len(dram.shape) - 1])
            return dram[bass.ds(index, 1)].rearrange(f"z {names} -> (z {names.split()[0]}) {' '.join(names.split()[1:])}")

        def exists(u):
            return not isinstance(u, int) or 0 <= u < UNITS

        def chunk_of(buffer, i, cols=None):
            _, _, width, at = CHUNKS[i]
            a, b = cols or (0, width)
            return buffer[:, at:at + 2 * width].rearrange("p (h q) -> p h q", h=2)[:, :, a:b]

        def load_unit(sp, n, p):
            if not exists(n):
                return
            kit.ge_apart(sp, proj["k1"], n - 1)
            kit.ge_apart(sp, w_split, n - 1)
            sp.dma_start(w[p][:], of(w_dram, n & (PAIRS - 1))[:, 0:2, :]).then_inc(w_loaded[p], 16)
            src = of(xt_dram, (n >> SEQ_BITS) & (BATCH - 1))
            sp.dma_start(xh[p][:].bitcast(F32), src[1]).then_inc(x_loaded[p], 16)
            sp.dma_start(xl[p][:].bitcast(F32), src[2]).then_inc(x_loaded[p], 16)

        def load_xt(sp, n):
            if not exists(n):
                return
            kit.ge_apart(sp, proj["v1"], n)
            sp.dma_start(xt[:], of(xt_dram, (n >> SEQ_BITS) & (BATCH - 1))[0]).then_inc(xt_loaded, 16)

        def sp_step(sp, u, p):
            load_unit(sp, u + 2, p)
            if exists(u):
                kit.ge_apart(sp, wo_done[1], u - 1)
                sp.dma_start(wo[p][:], of(w_dram, u & (PAIRS - 1))[:, 3, :]).then_inc(wo_loaded[p], 16)
            n, pn = u + 1, 1 - p
            if exists(n):
                kit.ge_apart(sp, proj["v1"], n - 1)
                sp.dma_start(wv[pn][:], of(w_dram, n & (PAIRS - 1))[:, 2, :]).then_inc(wv_loaded[pn], 16)
                sg = stage[:].bitcast(F32)
                A, B = slice(0, DH), slice(DH, P)
                for what, first, second in (("q", "q0", "q1"), ("k", "k0", "k1")):
                    kit.ge_apart(sp, evac[first], n + 1)
                    kit.ge_apart(sp, evac[second], n + 1)
                    if what == "q":
                        moves = [(q_st[pn], A, 0, A, 0), (q_st[pn], B, 0, A, 1),
                                 (q_st[pn], A, 1, B, 1), (q_st[pn], B, 1, B, 0)]
                        row = 0
                    else:
                        moves = [(st[pn], half, h, (A, B)[h], part_)
                                 for st, part_ in ((kh_st, 0), (kl_st, 1)) for h in range(2) for half in (A, B)]
                        row = 1
                    for st, to, h, frm, hl in moves:
                        sp.dma_start(st[to, h, :].bitcast(F32), sg[frm, row, hl, :]).then_inc(stacked, 16)
            load_xt(sp, u + 1)

        def split_w(pool, n, p):
            if not exists(n):
                return
            kit.ge_apart(pool, w_loaded[p], 16 * (n >> 1) + 16)
            kit.ge_apart(pool, proj["k1"], n - 1)
            nc.gpsimd.tensor_copy(wh[p][:], w[p][:, 0:2, :]).then_inc(w_high, 1)
            kit.ge_apart(pool, w_high, n + 1)
            nc.gpsimd.tensor_tensor(wl[p][:], w[p][:, 0:2, :], wh[p][:].bitcast(F32),
                                    ALU.subtract).then_inc(w_split, 1)

        def pool_step(pool, u, p):
            for g in DIAGONAL_GROUPS:
                if exists(u):
                    kit.ge_apart(pool, exp_done, u * len(GROUPS) + g + 1)
                    for i in range(*GROUPS[g]):
                        blk = chunk_of(prob[p], i, (0, P))
                        last = nc.gpsimd.affine_select(out=blk, in_=blk, compare_op=ALU.is_ge, fill=0.0, base=0,
                                                       pattern=[[0, 2], [1, P]], channel_multiplier=-1)
                    last.then_inc(masked, 1)
                if g == 0:
                    split_w(pool, u + 2, p)

        def act_high(act, n, name):
            if not exists(n):
                return
            which, half = "qk".index(name[0]), int(name[1])
            act.wait_ge(proj[name], n + 1)
            if name == "q0":
                ge(act, stacked, n * (16 * STACK_DMAS))
            nc.scalar.copy(stage[:, which, 0, half * HALF:(half + 1) * HALF], misc[:, half, :])\
                .then_inc(high[name], 1)

        def act_v(act, u, p, half):
            act.wait_ge(proj[f"v{half}"], u + 1)
            if half == 0:
                ge(act, pv_done[1], u - 1)
            nc.scalar.copy(v[p][:, half * (TILES // 2):(half + 1) * (TILES // 2), :].rearrange("p t d -> p (t d)"),
                           misc[:, half, :]).then_inc(evac[f"v{half}"], 1)

        def act_out(act, m, half):
            if not exists(m):
                return
            act.wait_ge(pv_done[half], m + 1)
            ge(act, wo_done[half], m)
            nc.scalar.copy(ot[:, half * HALF:(half + 1) * HALF], out_ps[:, half, :]).then_inc(out_evac[half], 1)

        def act_step(act, u, p):
            act_out(act, u - 2, 1)
            if exists(u):
                ge(act, pv_done[1], u - 1)
                ge(act, added, (u - 1) * ADDS)
            g = 0
            for i, (_, _, width, at) in enumerate(CHUNKS):
                if exists(u):
                    act.wait_ge(scored, u * NCH + i + 1)
                    nc.scalar.activation(chunk_of(prob[p], i), score_ps[:, i % 2, :, 0:width], ACT.Tanh,
                                         scale=scale / clamp).then_inc(tanh_done, 1)
                if i in QK_JOBS:
                    act_high(act, u + 1, QK_JOBS[i])
                if i == 6:
                    act_out(act, u - 1, 0)
                if i in V_JOBS and exists(u):
                    act_v(act, u, p, V_JOBS[i])
                if i + 1 == GROUPS[g][1] and exists(u):
                    a = CHUNKS[GROUPS[g][0]][3]
                    act.wait_ge(tanh_done, u * NCH + i + 1)
                    nc.scalar.activation(prob[p][:, a:at + 2 * width], prob[p][:, a:at + 2 * width], ACT.Exp,
                                         scale=clamp).then_inc(exp_done, 1)
                    g += 1

        def pe_scores(pe, u, p, i):
            half, j, width, _ = CHUNKS[i]
            q0 = half * HALF + HALF - width
            if i == 0:
                pe.wait_ge(stacked, (u + 1) * (16 * STACK_DMAS))
            ge(pe, tanh_done, u * NCH + i - 1)
            for h in range(2):
                for st in (kh_st, kl_st):
                    last = nc.tensor.matmul(score_ps[:, i % 2, h, 0:width], st[p][:, h, j * P:(j + 1) * P],
                                            q_st[p][:, h, q0:q0 + width], start=st is kh_st, stop=st is kl_st)
            last.then_inc(scored, 1)

        def pe_pv(pe, m, p, i):
            half, j, width, _ = CHUNKS[i]
            g = [g for g, (a, b) in enumerate(GROUPS) if a == i]
            if g and g[0] in DIAGONAL_GROUPS:
                pe.wait_ge(masked, m * 2 + DIAGONAL_GROUPS.index(g[0]) + 1)
            elif g:
                pe.wait_ge(exp_done, m * len(GROUPS) + g[0] + 1)
            if j == 0:
                ge(pe, out_evac[half], m)
                ge(pe, evac["v1"], m + 1)
            last_j = max(c[1] for c in CHUNKS if c[0] == half)
            for h in range(2):
                mm = nc.tensor.matmul(out_ps[h * DH:(h + 1) * DH, half, HALF - width:HALF],
                                      v[p][:, j, h * DH:(h + 1) * DH], chunk_of(prob[p], i)[:, h, :],
                                      start=j == 0, stop=j == last_j)
            if j == last_j:
                mm.then_inc(pv_done[half], 1)

        def pe_qk(pe, n, p, name):
            which, half = "qk".index(name[0]), int(name[1])
            if name == "q0":
                pe.wait_ge(x_loaded[p], 32 * (n >> 1) + 32)
                pe.wait_ge(w_split, n + 1)
                ge(pe, x_added[0], n - 2)
            ge(pe, {"k0": evac["q0"], "k1": evac["q1"], "q1": x_added[1]}.get(name, evac["q0"]),
               {"k0": n + 1, "k1": n + 1, "q1": n - 2}.get(name, 0))
            cols = slice(half * HALF, (half + 1) * HALF)
            terms = [(wh, xh), (wh, xl), (wl, xh)]
            for t, (ws, xs) in enumerate(terms):
                mm = nc.tensor.matmul(misc[:, half, :], ws[p][:, which, :], xs[p][:, cols],
                                      start=t == 0, stop=t == len(terms) - 1)
            mm.then_inc(proj[name], 1)

        def pe_v(pe, n, p, half):
            if exists(n + 1):
                pe.wait_ge(evac[f"k{half}"], n + 2)
            else:
                ge(pe, x_added[half], n - 1)
            if half == 0:
                pe.wait_ge(xt_loaded, n * 16 + 16)
                pe.wait_ge(wv_loaded[p], 16 * (n >> 1) + 16)
            for t in range(TILES // 2):
                tile = half * (TILES // 2) + t
                mm = nc.tensor.matmul(misc[:, half, t * P:(t + 1) * P], xt[:, tile * P:(tile + 1) * P],
                                      wv[p][:], start=True, stop=True)
            mm.then_inc(proj[f"v{half}"], 1)

        def pe_sum(pe, m):
            if exists(m + 1):
                pe.wait_ge(evac["v0"], m + 2)
            else:
                ge(pe, x_added[0], m)
            pe.wait_ge(added, m * ADDS + ADDS)
            for half in range(2):
                for h in range(2):
                    row = 32 * (2 * half + h)
                    mm = nc.tensor.matmul(misc[row:row + 32, 0, :], ones[:, 0:32],
                                          part[:, h, half * HALF:(half + 1) * HALF], start=True, stop=True)
            mm.then_inc(summed, 1)

        def pe_bcast(pe, m, half):
            pe.wait_ge(r_split, m + 1)
            if half == 1:
                if exists(m + 1):
                    pe.wait_ge(evac["v1"], m + 2)
                else:
                    ge(pe, x_added[1], m)
            if isinstance(m, int) and m == 0 and half == 0:
                pe.wait_ge(spread_made, 5)
            for t in range(2):
                mm = nc.tensor.matmul(misc[:, half, :], spread[:, half, :], rhl[:, t, :], start=t == 0, stop=t == 1)
            mm.then_inc(bcast[half], 1)

        def pe_wo(pe, m, p, half):
            if half == 0:
                pe.wait_ge(wo_loaded[p], 16 * (m >> 1) + 16)
            pe.wait_ge(normed[half], m + 1)
            for t in range(TILES // 2):
                tile = half * (TILES // 2) + t
                mm = nc.tensor.matmul(misc[:, half, t * P:(t + 1) * P], ot[:, tile * P:(tile + 1) * P],
                                      wo[p][:], start=True, stop=True)
            mm.then_inc(wo_done[half], 1)

        def pe_step(pe, u, p):
            nxt, prev, before = u + 1, u - 1, u - 2
            for i in range(NCH):
                if exists(u):
                    pe_scores(pe, u, p, i)
                if exists(prev):
                    pe_pv(pe, prev, 1 - p, i)
                if i in QK_JOBS and exists(nxt):
                    pe_qk(pe, nxt, 1 - p, QK_JOBS[i])
                if i in V_JOBS and exists(u):
                    pe_v(pe, u, p, V_JOBS[i])
                if i == 1 and exists(before):
                    pe_wo(pe, before, p, 1)
                if exists(prev):
                    if i == 6:
                        pe_sum(pe, prev)
                    if i in (9, 10):
                        pe_bcast(pe, prev, i - 9)
                    if i == 11:
                        pe_wo(pe, prev, 1 - p, 0)

        def dve_split(dve, n, name):
            which, half = "qk".index(name[0]), int(name[1])
            cols = slice(half * HALF, (half + 1) * HALF)
            dve.wait_ge(high[name], n + 1)
            nc.vector.tensor_tensor(stage[:, which, 1, cols], misc[:, half, :],
                                    stage[:, which, 0, cols].bitcast(F32), ALU.subtract).then_inc(evac[name], 1)

        def dve_adds(dve, m, p, g):
            if g in DIAGONAL_GROUPS:
                dve.wait_ge(masked, m * 2 + DIAGONAL_GROUPS.index(g) + 1)
            else:
                dve.wait_ge(exp_done, m * len(GROUPS) + g + 1)
            steps = []
            if g == 0:
                ge(dve, summed, m)
                steps.append(("copy", slice(0, P), chunk_of(prob[p], 0, (0, P)), None))
                steps.append(("add", slice(P, HALF), chunk_of(prob[p], 0, (P, HALF)), chunk_of(prob[p], 1)))
            elif g == 1:
                steps.append(("add", slice(HALF, SEQ), chunk_of(prob[p], 4), chunk_of(prob[p], 5)))
            for i in range(*GROUPS[g]):
                half, j, width, _ = CHUNKS[i]
                if j >= 2:
                    cols = slice(half * HALF + HALF - width, half * HALF + HALF)
                    steps.append(("acc", cols, part[:, :, cols], chunk_of(prob[p], i)))
            done = {0: 0, 1: 4, 2: 5, 3: 7}[g]
            for s, (kind, cols, a, b) in enumerate(steps):
                if kind == "acc":
                    dve.wait_ge(added, m * ADDS + done + s)
                if kind == "copy":
                    ins = nc.vector.tensor_copy(part[:, :, cols], a)
                else:
                    ins = nc.vector.tensor_tensor(part[:, :, cols], a, b, ALU.add)
                ins.then_inc(added, 1)

        def dve_recip(dve, m):
            dve.wait_ge(summed, m + 1)
            ge(dve, bcast[1], m)
            nc.vector.reciprocal(rsum[:], misc[:, 0, :]).then_inc(recip, 1)

        def dve_r_high(dve, m):
            dve.wait_ge(recip, m + 1)
            nc.vector.tensor_copy(rhl[:, 0, :], rsum[:]).then_inc(r_high, 1)

        def dve_r_low(dve, m):
            dve.wait_ge(r_high, m + 1)
            nc.vector.tensor_tensor(rhl[:, 1, :], rsum[:], rhl[:, 0, :].bitcast(F32), ALU.subtract)\
                .then_inc(r_split, 1)

        def dve_norm(dve, m, half):
            cols = slice(half * HALF, (half + 1) * HALF)
            dve.wait_ge(out_evac[half], m + 1)
            dve.wait_ge(bcast[half], m + 1)
            nc.vector.tensor_tensor(ot[:, cols], misc[:, half, :], ot[:, cols], ALU.mult)\
                .then_inc(normed[half], 1)

        def dve_x_add(dve, m, half):
            dve.wait_ge(wo_done[half], m + 1)
            ge(dve, x_added[half], m)
            at = ((m >> SEQ_BITS) & (BATCH - 1)) * SEQ + half * HALF
            rows = xflat[:, bass.ds(at, HALF)]
            nc.vector.tensor_tensor(rows, rows, misc[:, half, :], ALU.add).then_inc(x_added[half], 1)

        def dve_step(dve, u, p):
            nxt, prev, before = u + 1, u - 1, u - 2
            order = [("x", before, 0), ("norm", before, 1), ("split", nxt, "q0"), ("x", before, 1),
                     ("split", nxt, "k0"), ("split", nxt, "q1"), ("adds", prev, 3), ("split", nxt, "k1"),
                     ("recip", prev, None), ("adds", u, 0), ("r_high", prev, None), ("r_low", prev, None),
                     ("adds", u, 1), ("norm", prev, 0), ("adds", u, 2)]
            for what, m, arg in order:
                if not exists(m):
                    continue
                if what == "norm":
                    dve_norm(dve, m, arg)
                elif what == "split":
                    dve_split(dve, m, arg)
                elif what == "x":
                    dve_x_add(dve, m, arg)
                elif what == "adds":
                    dve_adds(dve, m, p if m is u else 1 - p, arg)
                elif what == "recip":
                    dve_recip(dve, m)
                elif what == "r_high":
                    dve_r_high(dve, m)
                else:
                    dve_r_low(dve, m)

        def steps(eng, step):
            for u in range(-1, 2):
                step(eng, u, u % 2)
            looped = (UNITS - 3) // 2
            with eng.Fori(0, looped) as it:
                for par in range(2):
                    step(eng, it * 2 + (2 + par), par)
            for u in range(2 + 2 * looped, UNITS + 2):
                step(eng, u, u % 2)

        with nc.Block() as block:

            @block.sync
            def _(sp):
                load_unit(sp, 0, 0)
                steps(sp, sp_step)

            @block.gpsimd
            def _(pool):
                split_w(pool, 0, 0)
                steps(pool, pool_step)

            @block.scalar
            def _(act):
                steps(act, act_step)

            @block.tensor
            def _(pe):
                steps(pe, pe_step)

            @block.vector
            def _(dve):
                nc.vector.memset(spread[:].bitcast(F32), 0.0).then_inc(spread_made, 1)
                dve.wait_ge(spread_made, 1)
                for half in range(2):
                    for h in range(2):
                        row = 32 * (2 * half + h)
                        nc.vector.memset(spread[row:row + 1, half, h * DH:(h + 1) * DH].bitcast(F32), 1.0)\
                            .then_inc(spread_made, 1)
                steps(dve, dve_step)


def of(dram, index):
    if isinstance(index, int):
        return dram[index]
    names = "abcde"[:len(dram.shape) - 1]
    rest = " ".join(names[1:])
    return dram[bass.ds(index, 1)].rearrange(f"z {' '.join(names)} -> (z {names[0]}) {rest}")


PAGE = 32
HEADS1, DH1 = 16, 8
QUAD = 4
QUADS = HEADS1 // QUAD
PARTS = 3
V_COLS = 32


def project1(nc, kit, sem, ident, xt_dram, wq_dram, wdown_dram, wk_dram, wv_dram, rope_dram, parts_dram, v_dram):
    with ExitStack() as ctx:
        k = kit.scope(ctx)
        L = wdown_dram.shape[1]
        wq = k.sb("p1_wq", [P, 2, P])
        wd = k.sb("p1_wd", [P, L])
        wk = k.sb("p1_wk", [L, 2, P])
        wv = k.sb("p1_wv", [L, P])
        rope = k.sb("p1_rope", [P, 2, SEQ])
        xt = k.sb("p1_xt", [P, SEQ])
        lat = k.sb("p1_lat", [L, SEQ])
        t_cos, t_sin = k.sb("p1_tcos", [P, SEQ]), k.sb("p1_tsin", [P, SEQ])
        rest = k.sb("p1_rest", [P, SEQ])
        part = [k.sb(f"p1_part{i}", [P, PARTS, SEQ], BF16) for i in range(2)]
        vp = k.sb("p1_v", [P, TILES, HEADS1, V_COLS])
        plain = k.ps("p1_plain", [P, SEQ])
        partner = k.ps("p1_partner", [P, SEQ])
        lat_ps = k.ps("p1_lat_ps", [L, SEQ])
        v_ps = k.ps("p1_v_ps", [P, SEQ])
        w_loaded, x_loaded, v_set = sem("p1_w_loaded"), sem("p1_x_loaded"), sem("p1_v_set")
        lat_done, lat_out, v_done, v_out = (sem(f"p1_{n}") for n in ("lat_done", "lat_out", "v_done", "v_out"))
        plain_done, cos_done, sin_done, rot_done = (sem(f"p1_{n}") for n in ("plain", "cos", "sin", "rot"))
        hi_done, rest_done, mid_done, lo_done = (sem(f"p1_{n}") for n in ("hi", "rest", "mid", "lo"))
        stored, x_free, part_free, v_free = (sem(f"p1_{n}") for n in ("stored", "x_free", "part_free", "v_free"))

        with nc.Block() as block:

            @block.sync
            def _(sp):
                for dst, src in ((wq, wq_dram), (wd, wdown_dram), (wk, wk_dram), (wv, wv_dram), (rope, rope_dram)):
                    sp.dma_start(dst[:], src).then_inc(w_loaded, 16)
                sp.sem_inc(part_free, 1)
                sp.dma_start(xt[:], xt_dram[0, 0]).then_inc(x_loaded, 16)
                with sp.Fori(0, BATCH) as b:
                    for i in range(2):
                        sp.wait_ge(hi_done, b * 2 + i + 1)
                        sp.wait_ge(mid_done, b * 2 + i + 1)
                        kit.ge_apart(sp, lo_done, b * 2 + i + 1)
                        if i == 1:
                            nxt = (b + 1) & (BATCH - 1)
                            sp.dma_start(xt[:], of(xt_dram, nxt)[0]).then_inc(x_loaded, 16)
                        for a in range(PARTS):
                            dst = of(parts_dram, b)[i * PARTS + a]
                            sp.dma_start(dst, part[i][:, a, :]).then_inc(stored, 16)
                    sp.wait_ge(v_out, b + 1)
                    dst = of(v_dram, b)
                    for q in range(QUADS):
                        sp.dma_start(dst[q], vp[:, :, q * QUAD:(q + 1) * QUAD, :]).then_inc(stored, 16)
                    sp.wait_ge(stored, b * (16 * (2 * PARTS + QUADS)) + 16 * (2 * PARTS + QUADS))
                    sp.sem_inc(part_free, 1)
                sp.wait_ge(x_loaded, 16 * (BATCH + 1))

            @block.tensor
            def _(pe):
                pe.wait_ge(w_loaded, 16 * 5)
                with pe.Fori(0, BATCH) as b:
                    pe.wait_ge(x_loaded, b * 16 + 16)
                    for half in range(2):
                        cols = slice(half * HALF, (half + 1) * HALF)
                        mm = nc.tensor.matmul(lat_ps[:, cols], wd[:], xt[:, cols], start=True, stop=True)
                    mm.then_inc(lat_done, 1)
                    for i in range(2):
                        if i == 1:
                            pe.wait_ge(lat_out, b + 1)
                            pe.wait_ge(sin_done, b * 2 + 1)
                        for to, which in ((plain, 0), (partner, 1)):
                            for half in range(2):
                                cols = slice(half * HALF, (half + 1) * HALF)
                                w_, x_ = (wq, xt) if i == 0 else (wk, lat)
                                mm = nc.tensor.matmul(to[:, cols], w_[:, which, :], x_[:, cols],
                                                      start=True, stop=True)
                        mm.then_inc(plain_done, 1)
                    for t in range(TILES):
                        mm = nc.tensor.matmul(v_ps[:, t * P:(t + 1) * P], lat[:, t * P:(t + 1) * P], wv[:],
                                              start=True, stop=True)
                    mm.then_inc(v_done, 1)
                    pe.wait_ge(sin_done, b * 2 + 2)
                    pe.wait_ge(v_out, b + 1)

            @block.scalar
            def _(act):
                act.wait_ge(v_set, 2)
                with act.Fori(0, BATCH) as b:
                    act.wait_ge(lat_done, b + 1)
                    nc.scalar.copy(lat[:], lat_ps[:]).then_inc(lat_out, 1)
                    act.wait_ge(part_free, b + 1)
                    for i in range(2):
                        act.wait_ge(rot_done, b * 2 + i + 1)
                        nc.scalar.copy(part[i][:, 0, :], t_cos[:]).then_inc(hi_done, 1)
                        act.wait_ge(rest_done, b * 2 + i + 1)
                        nc.scalar.copy(part[i][:, 1, :], rest[:]).then_inc(mid_done, 1)
                    act.wait_ge(v_done, b + 1)
                    nc.scalar.copy(vp[:, :, :, 0:DH1], v_ps[:].rearrange("p (t h d) -> p t h d", t=TILES, d=DH1))\
                        .then_inc(v_out, 1)

            @block.vector
            def _(dve):
                nc.vector.memset(vp[:], 0.0).then_inc(v_set, 1)
                dve.wait_ge(v_set, 1)
                nc.vector.memset(vp[:, :, :, DH1:DH1 + 1], 1.0).then_inc(v_set, 1)
                dve.wait_ge(w_loaded, 16 * 5)
                with dve.Fori(0, BATCH) as b:
                    for i in range(2):
                        n = b * 2 + i
                        dve.wait_ge(plain_done, n + 1)
                        if i == 1:
                            dve.wait_ge(lo_done, n)
                            dve.wait_ge(hi_done, n)
                        nc.vector.tensor_tensor(t_cos[:], plain[:], rope[:, 0, :], ALU.mult).then_inc(cos_done, 1)
                        nc.vector.tensor_tensor(t_sin[:], partner[:], rope[:, 1, :], ALU.mult).then_inc(sin_done, 1)
                        dve.wait_ge(cos_done, n + 1)
                        dve.wait_ge(sin_done, n + 1)
                        nc.vector.tensor_tensor(t_cos[:], t_cos[:], t_sin[:], ALU.add).then_inc(rot_done, 1)
                        dve.wait_ge(hi_done, n + 1)
                        nc.vector.tensor_tensor(rest[:], t_cos[:], part[i][:, 0, :], ALU.subtract)\
                            .then_inc(rest_done, 1)
                        dve.wait_ge(mid_done, n + 1)
                        nc.vector.tensor_tensor(part[i][:, 2, :], rest[:], part[i][:, 1, :], ALU.subtract)\
                            .then_inc(lo_done, 1)


def attention1(nc, kit, sem, ident, parts_dram, v_dram, out, scale):
    UNITS = BATCH * QUADS
    ROWS = PARTS * PARTS * DH1
    ROWS_M = ROWS + PARTS
    SLOTS = 2 * NCH
    RING = 6
    PV_LAG = 2
    MAX_SLOTS = 18
    PIECES = [(h, t, c, c * HALF, min(HALF, (t + 1) * P - c * HALF))
              for h in range(QUAD) for t in range(TILES) for c in range(2) if (t + 1) * P > c * HALF]
    BUFS = 3
    BANKS = 3
    with ExitStack() as ctx:
        k = kit.scope(ctx)
        q_st = [k.sb(f"a1_q{i}", [P, QUAD, SEQ], BF16) for i in range(BUFS)]
        k_st = [k.sb(f"a1_k{i}", [P, QUAD, SEQ], BF16) for i in range(BUFS)]
        v_st = [k.sb(f"a1_v{i}", [P, TILES, QUAD, V_COLS]) for i in range(BUFS)]
        prob = [k.sb(f"a1_p{i}", [P, 2, HALF]) for i in range(RING)]
        identb = k.sb("a1_identb", [P, P], BF16)
        page_mask = k.sb("a1_page_mask", [P, P], BF16)
        mx = [k.sb(f"a1_mx{c}", [P, QUAD, TILES]) for c in range(2)]
        neg = k.sb("a1_neg", [QUAD * TILES, P])
        neg_rest = k.sb("a1_neg_rest", [QUAD * TILES, P])
        neg_part = k.sb("a1_neg_part", [QUAD * TILES, PARTS, P], BF16)
        ot = k.sb("a1_ot", [P, 2, HALF])
        rs = k.sb("a1_rs", [P, TILES // 2, QUAD])
        score_ps = k.ps("a1_score", [P, 2, 2, HALF])
        out_ps = k.ps("a1_out", [P, HALF])
        misc = k.ps("a1_misc", [P, BANKS, HALF])

        st_loaded = [sem(f"a1_st_loaded{i}") for i in range(BUFS)]
        masks_made, ones_made, zeros_made = (sem(f"a1_{n}_made") for n in ("masks", "ones", "zeros"))
        ready, free = sem("a1_misc_ready"), sem("a1_misc_free")
        combined, neg_done, hi_done, rest_done, mid_done, lo_done = \
            (sem(f"a1_{n}") for n in ("combined", "neg", "neg_hi", "neg_rest", "neg_mid", "neg_lo"))
        m_stacked = sem("a1_m_stacked")
        scored, exp_done, masked = (sem(f"a1_{n}") for n in ("scored", "exp", "masked"))
        pv_chunks = sem("a1_pv_chunks")
        HALF_END = [1 + max(i for i, c in enumerate(CHUNKS) if c[0] == half) for half in range(2)]
        out_evac = [sem(f"a1_out_evac{i}") for i in range(2)]
        rs_done = sem("a1_rs")
        ST_DMAS = 2 * PARTS * PARTS + 1
        DIAG = [i for i, (half, j, _, _) in enumerate(CHUNKS) if j // (TILES // 2) == half]

        def exists(u):
            return not isinstance(u, int) or 0 <= u < UNITS

        def uses(u):
            by_slot = {s: [] for s in range(SLOTS)}
            if exists(u + 1):
                for n, piece in enumerate(PIECES):
                    by_slot[n * MAX_SLOTS // len(PIECES)].append(("max", piece, n == len(PIECES) - 1))
                by_slot[MAX_SLOTS + 2].append(("turn_max", None, None))
            if exists(u - 1):
                by_slot[6].append(("turn_out", 1, None))
            if exists(u):
                by_slot[14].append(("turn_out", 0, None))
            n = sum(map(len, by_slot.values()))
            return by_slot, n

        FULL = len(PIECES) + 3

        def bank_of(u, at):
            short = FULL - uses(u)[1] if isinstance(u, int) and u < 1 else 0
            return (at + short) % BANKS

        def before(u):
            if isinstance(u, int):
                return sum(uses(s)[1] for s in range(-1, u))
            return before(1) + (u - 1) * FULL

        def wait_prob(eng, m, i, hp):
            if i in DIAG:
                eng.wait_ge(masked, m * (2 * len(DIAG)) + 2 * DIAG.index(i) + hp + 1)
            else:
                eng.wait_ge(exp_done, m * SLOTS + 2 * i + hp + 1)

        def load_unit(sp, n, b3, d3):
            if not exists(n):
                return
            kit.ge_apart(sp, pv_chunks, (n - BUFS + 1) * NCH)
            batch, quad = (n >> 2) & (BATCH - 1), n & (QUADS - 1)
            src = of(parts_dram, batch)
            for which, st in ((0, q_st), (1, k_st)):
                for a in range(PARTS):
                    row0 = a * (PARTS * DH1)
                    for b in range(PARTS):
                        part = a if which == 0 else b
                        rows = src[which * PARTS + part].rearrange("(g h d) t -> g d h t", g=QUADS, h=QUAD)
                        sp.dma_start(st[b3][row0 + b * DH1:row0 + (b + 1) * DH1, :, :], of(rows, quad))\
                            .then_inc(st_loaded[b3], 16)
            sp.dma_start(v_st[b3][:], of(of(v_dram, batch), quad)).then_inc(st_loaded[b3], 16)

        def sp_step(sp, u, b3, d3):
            load_unit(sp, u + 2, (b3 + 2) % BUFS, d3(2))
            n, bn = u + 1, (b3 + 1) % BUFS
            if exists(n):
                for a, done in enumerate((hi_done, mid_done, lo_done)):
                    sp.wait_ge(done, n + 1)
                    row = q_st[bn][ROWS + a:ROWS + a + 1, :, :].rearrange("o h (t c) -> o (h t) c", c=P)
                    sp.dma_start(row, neg_part[:, a, :]).then_inc(m_stacked, 16)

        def pool_step(pool, u, b3, d3):
            if not exists(u):
                return
            for i in DIAG:
                for hp in range(2):
                    slot = 2 * i + hp
                    kit.ge_apart(pool, exp_done, u * SLOTS + slot + 1)
                    blk = prob[slot % RING][:, :, 0:P].rearrange("p h (g q) -> p h g q", q=PAGE)
                    nc.gpsimd.affine_select(out=blk, in_=blk, compare_op=ALU.is_ge, fill=0.0, base=PAGE - 1,
                                            pattern=[[0, 2], [PAGE, P // PAGE], [0, PAGE]], channel_multiplier=-1)\
                        .then_inc(masked, 1)

        def act_out(act, m, half):
            if not exists(m):
                return
            act.wait_ge(pv_chunks, m * NCH + HALF_END[half])
            ge(act, rs_done, m * 2 - 1 + half)
            nc.scalar.copy(ot[:, half, :], out_ps[:]).then_inc(out_evac[half], 1)

        def act_step(act, u, b3, d3):
            for s in range(SLOTS):
                i = s // 2
                if exists(u):
                    width = CHUNKS[i][2]
                    ge(act, pv_chunks, u * NCH + (s // 2 - RING // 2 + 1))
                    act.wait_ge(scored, u * SLOTS + s + 1)
                    nc.scalar.activation(prob[s % RING][:, :, 0:width], score_ps[:, s % 2, :, 0:width], ACT.Exp,
                                         scale=scale).then_inc(exp_done, 1)
                if s == 2:
                    act_out(act, u - 1, 1)
                if s == 10:
                    act_out(act, u, 0)

        def pe_scores(pe, u, b3, s, h2):
            i, hp = s // 2, s % 2
            half, j, width, _ = CHUNKS[i]
            q0 = half * HALF + HALF - width
            if s == 0 and h2 == 0:
                pe.wait_ge(m_stacked, u * (16 * PARTS) + 16 * PARTS)
            if h2 == 0:
                ge(pe, exp_done, u * SLOTS + s - 1)
            h = 2 * hp + h2
            mm = nc.tensor.matmul(score_ps[:, s % 2, h2, 0:width], k_st[b3][:, h, j * P:(j + 1) * P],
                                  q_st[b3][:, h, q0:q0 + width], start=True, stop=True)
            if h2 == 1:
                mm.then_inc(scored, 1)

        def pe_pv(pe, m, b3, i):
            half, j, width, _ = CHUNKS[i]
            wait_prob(pe, m, i, 0)
            wait_prob(pe, m, i, 1)
            if j == 0:
                ge(pe, out_evac[1 - half], m + half)
            last_j = max(c[1] for c in CHUNKS if c[0] == half)
            for h in range(QUAD):
                slot = (2 * i + h // 2) % RING
                mm = nc.tensor.matmul(out_ps[h * V_COLS:(h + 1) * V_COLS, HALF - width:HALF],
                                      v_st[b3][:, j, h, :], prob[slot][:, h % 2, 0:width],
                                      start=j == 0, stop=j == last_j)
            mm.then_inc(pv_chunks, 1)

        def pe_use(pe, u, b3, kind, arg, number, at):
            bank = bank_of(u, at)
            ge(pe, free, number if isinstance(u, int) and at < BANKS else number - (BANKS - 1))
            if kind == "max":
                h, t, c, key0, keys = arg
                bn = (b3 + 1) % BUFS
                diagonal = key0 + keys == (t + 1) * P
                mm = nc.tensor.matmul(misc[:, bank, 0:keys], q_st[bn][0:ROWS, h, t * P:(t + 1) * P],
                                      k_st[bn][0:ROWS, h, key0:key0 + keys], start=True, stop=not diagonal)
                if diagonal:
                    mm = nc.tensor.matmul(misc[:, bank, keys - P:keys], identb[:], page_mask[:],
                                          start=False, stop=True)
            elif kind == "turn_max":
                pe.wait_ge(combined, u + 2)
                mm = nc.tensor.transpose(misc[0:QUAD * TILES, bank, 0:P], mx[0][:].rearrange("p h t -> p (h t)"),
                                         ident[:])
            else:
                m = u if arg == 0 else u - 1
                pe.wait_ge(out_evac[arg], m + 1)
                for t in range(TILES // 2):
                    mm = nc.tensor.transpose(misc[:, bank, t * P:(t + 1) * P], ot[:, arg, t * P:(t + 1) * P], ident[:])
            mm.then_inc(ready, 1)

        def numbered(u):
            by_slot, _ = uses(u)
            first = before(u)
            at = 0
            result = {}
            for s in range(SLOTS):
                result[s] = []
                for kind, arg, last in by_slot[s]:
                    result[s].append((kind, arg, last, first + at, at))
                    at += 1
            return result

        def pe_step(pe, u, b3, d3):
            numb = numbered(u)
            if isinstance(u, int) and u == -1:
                pe.wait_ge(masks_made, 2 + P // PAGE - 1)
            if exists(u + 1):
                pe.wait_ge(st_loaded[(b3 + 1) % BUFS], d3(1) * (16 * ST_DMAS) + 16 * ST_DMAS)
            for s in range(SLOTS):
                todo = numb[s][:]
                for h2 in range(2):
                    if todo:
                        kind, arg, last, number, at = todo.pop(0)
                        pe_use(pe, u, b3, kind, arg, number, at)
                    if exists(u):
                        pe_scores(pe, u, b3, s, h2)
                if s % 2 == 0:
                    i = s // 2 - PV_LAG
                    m, c, bm = (u, i, b3) if i >= 0 else (u - 1, NCH + i, (b3 - 1) % BUFS)
                    if exists(m):
                        pe_pv(pe, m, bm, c)
                for kind, arg, last, number, at in todo:
                    pe_use(pe, u, b3, kind, arg, number, at)

        def dve_use(dve, u, b3, kind, arg, last, number, at):
            bank = bank_of(u, at)
            dve.wait_ge(ready, number + 1)
            n = u + 1
            if kind == "max":
                h, t, c, key0, keys = arg
                nc.vector.tensor_reduce(mx[c][:, h, t:t + 1], misc[:, bank, 0:keys], AX_X, ALU.max).then_inc(free, 1)
                if last:
                    dve.wait_ge(free, number + 1)
                    upper = slice(TILES // 2, TILES)
                    nc.vector.tensor_tensor(mx[0][:, :, upper], mx[0][:, :, upper], mx[1][:, :, upper], ALU.max)\
                        .then_inc(combined, 1)
            elif kind == "turn_max":
                ge(dve, m_stacked, n * (16 * PARTS))
                nc.vector.tensor_scalar(neg[:], misc[0:QUAD * TILES, bank, 0:P], -1.0, None, ALU.mult)\
                    .then_inc(free, 1)
                dve.wait_ge(free, number + 1)
                nc.vector.tensor_copy(neg_part[:, 0, :], neg[:]).then_inc(hi_done, 1)
                dve.wait_ge(hi_done, n + 1)
                nc.vector.tensor_tensor(neg_rest[:], neg[:], neg_part[:, 0, :], ALU.subtract).then_inc(rest_done, 1)
                dve.wait_ge(rest_done, n + 1)
                nc.vector.tensor_copy(neg_part[:, 1, :], neg_rest[:]).then_inc(mid_done, 1)
                dve.wait_ge(mid_done, n + 1)
                nc.vector.tensor_tensor(neg_part[:, 2, :], neg_rest[:], neg_part[:, 1, :], ALU.subtract)\
                    .then_inc(lo_done, 1)
            else:
                m = u if arg == 0 else u - 1
                order = m * 2 + arg
                turned = misc[:, bank, :].rearrange("p (t h c) -> p t h c", t=TILES // 2, h=QUAD)
                ge(dve, free, number)
                nc.vector.reciprocal(rs[:], turned[:, :, :, DH1]).then_inc(rs_done, 1)
                dve.wait_ge(rs_done, order + 1)
                col0 = (m & (QUADS - 1)) * (QUAD * DH1)
                to = out[:].rearrange("p t c -> p (t c)")
                for t in range(TILES // 2):
                    rows = to[:, bass.ds(((m >> 2) & (BATCH - 1)) * SEQ + (arg * (TILES // 2) + t) * P + col0, QUAD * DH1)]
                    ins = nc.vector.tensor_tensor(rows.rearrange("p (h d) -> p h d", d=DH1), turned[:, t, :, 0:DH1],
                                                  rs[:, t, :].unsqueeze(2).to_broadcast([P, QUAD, DH1]), ALU.mult)
                ins.then_inc(free, 1)

        def dve_step(dve, u, b3, d3):
            numb = numbered(u)
            for s in range(SLOTS):
                for kind, arg, last, number, at in numb[s]:
                    dve_use(dve, u, b3, kind, arg, last, number, at)

        def steps(eng, step):
            def plain(u):
                step(eng, u, u % BUFS, lambda k: (u + k) // BUFS)
            for u in (-1, 0):
                plain(u)
            looped = (UNITS - BUFS) // BUFS
            with eng.Fori(0, looped) as it:
                for i in range(BUFS):
                    step(eng, it * BUFS + (1 + i), (1 + i) % BUFS, lambda k, i=i: it + (1 + i + k) // BUFS)
            for u in range(1 + looped * BUFS, UNITS + 1):
                plain(u)

        with nc.Block() as block:

            @block.sync
            def _(sp):
                sp.wait_ge(ones_made, 2 * BUFS)
                load_unit(sp, 0, 0, None)
                steps(sp, sp_step)

            @block.gpsimd
            def _(pool):
                steps(pool, pool_step)

            @block.scalar
            def _(act):
                steps(act, act_step)

            @block.tensor
            def _(pe):
                steps(pe, pe_step)

            @block.vector
            def _(dve):
                for st in k_st:
                    nc.vector.memset(st[64:P, :, :].bitcast(F32), 0.0).then_inc(zeros_made, 1)
                for st in q_st:
                    nc.vector.memset(st[64:P, :, :].bitcast(F32), 0.0).then_inc(ones_made, 1)
                dve.wait_ge(zeros_made, BUFS)
                for st in k_st:
                    nc.vector.memset(st[64:96, :, :], 1.0).then_inc(ones_made, 1)
                nc.vector.tensor_copy(identb[:], ident[:]).then_inc(masks_made, 1)
                nc.vector.memset(page_mask[:], 0.0).then_inc(masks_made, 1)
                dve.wait_ge(masks_made, 2)
                for g in range(P // PAGE - 1):
                    nc.vector.memset(page_mask[g * PAGE:(g + 1) * PAGE, (g + 1) * PAGE:], NEGATIVE)\
                        .then_inc(masks_made, 1)
                steps(dve, dve_step)


NEGATIVE = -3e38


def project_out1(nc, kit, sem, ident, x, heads, wo_dram):
    with ExitStack() as ctx:
        k = kit.scope(ctx)
        wo = k.sb("po_wo", [P, D])
        turned = k.sb("po_turned", [P, SEQ])
        turned_ps = k.ps("po_turned_ps", [P, SEQ])
        y_ps = k.ps("po_y", [P, SEQ])
        w_loaded, turn_done, turn_out, y_done, added = (sem(f"po_{n}") for n in ("w", "turn", "turn_out", "y", "added"))
        staged = sem("po_staged")
        hflat = heads[:].rearrange("p t c -> p (t c)")
        xflat = x[:].rearrange("p t d -> p (t d)")
        here = k.sb("po_here", [P, SEQ])

        with nc.Block() as block:

            @block.sync
            def _(sp):
                sp.dma_start(wo[:], wo_dram).then_inc(w_loaded, 16)

            @block.tensor
            def _(pe):
                pe.wait_ge(w_loaded, 16)
                with pe.Fori(0, BATCH) as b:
                    pe.wait_ge(staged, b + 1)
                    for t in range(TILES):
                        mm = nc.tensor.transpose(turned_ps[:, t * P:(t + 1) * P], here[:, t * P:(t + 1) * P], ident[:])
                    mm.then_inc(turn_done, 1)
                    pe.wait_ge(turn_out, b + 1)
                    for t in range(TILES):
                        mm = nc.tensor.matmul(y_ps[:, t * P:(t + 1) * P], turned[:, t * P:(t + 1) * P], wo[:],
                                              start=True, stop=True)
                    mm.then_inc(y_done, 1)

            @block.scalar
            def _(act):
                with act.Fori(0, BATCH) as b:
                    act.wait_ge(turn_done, b + 1)
                    nc.scalar.copy(turned[:], turned_ps[:]).then_inc(turn_out, 1)

            @block.vector
            def _(dve):
                nc.vector.tensor_copy(here[:], hflat[:, 0:SEQ]).then_inc(staged, 1)
                with dve.Fori(0, BATCH) as b:
                    dve.wait_ge(y_done, b + 1)
                    rows = xflat[:, bass.ds(b * SEQ, SEQ)]
                    nc.vector.tensor_tensor(rows, rows, y_ps[:], ALU.add).then_inc(added, 1)
                    nxt = (b + 1) & (BATCH - 1)
                    nc.vector.tensor_copy(here[:], hflat[:, bass.ds(nxt * SEQ, SEQ)]).then_inc(staged, 1)


def norm_and_gate(nc, kit, sem, tag, x, ident, eps, gate_dram, bias_dram, xt_all, logits):
    E = gate_dram.shape[1]
    with ExitStack() as ctx:
        k = kit.scope(ctx)
        gate = k.sb(f"{tag}_gate", [P, E])
        biases = 0 if bias_dram is None else bias_dram.shape[1]
        bias = k.sb(f"{tag}_bias", [P, max(biases, 1), E])
        stats = k.sb(f"{tag}_stats", [P, TILES, 6])
        mv = k.sb(f"{tag}_mv", [P, TILES, 2])
        std = k.sb(f"{tag}_std", [P, TILES])
        rstd = k.sb(f"{tag}_rstd", [P, TILES])
        xn = k.sb(f"{tag}_xn", [P, TILES, D])
        xt = k.sb(f"{tag}_xt", [P, SEQ])
        turned = k.ps(f"{tag}_turned", [P, SEQ])
        gate_ps = k.ps(f"{tag}_gate_ps", [P, TILES, E])
        loaded, stats_done, mv_done = sem(f"{tag}_loaded"), sem(f"{tag}_stats"), sem(f"{tag}_mv")
        std_done, rstd_done = sem(f"{tag}_std"), sem(f"{tag}_rstd")
        xn_done, turn_done = sem(f"{tag}_xn"), sem(f"{tag}_turn")
        xt_done, kept, gated, biased = sem(f"{tag}_xt"), sem(f"{tag}_kept"), sem(f"{tag}_gated"), sem(f"{tag}_biased")
        xflat = x[:].rearrange("p t d -> p (t d)")
        lflat = logits[:].rearrange("p t e -> p (t e)")

        def dve_logits(dve, b):
            dve.wait_ge(gated, b + 1)
            rows = lflat[:, bass.ds(b * (TILES * E), TILES * E)].rearrange("p (t e) -> p t e", e=E)
            if biases == 0:
                nc.vector.tensor_copy(rows, gate_ps[:]).then_inc(biased, 1)
            for i in range(biases):
                if i > 0:
                    dve.wait_ge(biased, b * biases + i)
                nc.vector.tensor_tensor(rows, gate_ps[:] if i == 0 else rows,
                                        bias[:, i:i + 1, :].to_broadcast([P, TILES, E]), ALU.add).then_inc(biased, 1)

        with nc.Block() as block:

            @block.sync
            def _(sp):
                sp.dma_start(gate[:], gate_dram).then_inc(loaded, 16)
                if biases:
                    sp.dma_start(bias[:], bias_dram).then_inc(loaded, 16)

            @block.vector
            def _(dve):
                dve.wait_ge(loaded, 16 * (1 + (biases > 0)))
                with dve.Fori(0, BATCH) as b:
                    for t in range(TILES):
                        last = nc.vector.bn_stats(stats[:, t, :], xflat[:, bass.ds(b * (TILES * D) + t * D, D)])
                    last.then_inc(stats_done, 1)
                    kit.ge_apart(dve, stats_done, b + 1)
                    for t in range(TILES):
                        last = nc.vector.bn_aggr(mv[:, t, :], stats[:, t, :])
                    last.then_inc(mv_done, 1)
                    dve.wait_ge(std_done, b + 1)
                    nc.vector.reciprocal(rstd[:], std[:]).then_inc(rstd_done, 1)
                    dve.wait_ge(rstd_done, b + 1)
                    for t in range(TILES):
                        last = nc.vector.tensor_scalar(xn[:, t, :], xflat[:, bass.ds(b * (TILES * D) + t * D, D)],
                                                       mv[:, t, 0:1], rstd[:, t:t + 1], ALU.subtract, ALU.mult)
                    last.then_inc(xn_done, 1)
                    dve.wait_ge(turn_done, b + 1)
                    dve_logits(dve, b)

            @block.scalar
            def _(act):
                with act.Fori(0, BATCH) as b:
                    act.wait_ge(mv_done, b + 1)
                    nc.scalar.activation(std[:], mv[:, :, 1], ACT.Sqrt, bias=eps[:, 0:1]).then_inc(std_done, 1)
                    act.wait_ge(turn_done, b + 1)
                    nc.scalar.copy(xt[:], turned[:]).then_inc(xt_done, 1)
                    nc.scalar.copy(xt_all[:, bass.ds(b * SEQ, SEQ)], turned[:]).then_inc(kept, 1)

            @block.tensor
            def _(pe):
                pe.wait_ge(loaded, 16 * (1 + (biases > 0)))
                with pe.Fori(0, BATCH) as b:
                    pe.wait_ge(xn_done, b + 1)
                    for t in range(TILES):
                        last = nc.tensor.transpose(turned[:, t * P:(t + 1) * P], xn[:, t, :], ident[:])
                    last.then_inc(turn_done, 1)
                    pe.wait_ge(xt_done, b + 1)
                    for t in range(TILES):
                        last = nc.tensor.matmul(gate_ps[:, t, :], xt[:, t * P:(t + 1) * P], gate[:],
                                                start=True, stop=True)
                    last.then_inc(gated, 1)
                    pe.wait_ge(kept, b + 1)


def choose(nc, kit, sem, tag, logits, comb, choices):
    E = logits.shape[2]
    FAR = -3e38
    with ExitStack() as ctx:
        k = kit.scope(ctx)
        shape = [P, ALL_TILES, E]
        m = [k.sb(f"{tag}_m{i}", [P, ALL_TILES]) for i in range(2)]
        at_max = k.sb(f"{tag}_at_max", shape)
        first = k.sb(f"{tag}_first", [P, ALL_TILES])
        number = k.sb(f"{tag}_number", [P, 1, E])
        one = [k.sb(f"{tag}_one{i}", shape) for i in range(2)]
        left = k.sb(f"{tag}_left", shape)
        ex = k.sb(f"{tag}_ex", shape)
        total = k.sb(f"{tag}_total", [P, ALL_TILES])
        gap = k.sb(f"{tag}_gap", [P, ALL_TILES])
        step, exp_done, exp_in = sem(f"{tag}_step"), sem(f"{tag}_exp"), sem(f"{tag}_exp_in")
        wide = lambda a: a[:].unsqueeze(2).to_broadcast(shape)
        with nc.Block() as block:

            @block.vector
            def _(dve):
                done = 0

                def next_(ins):
                    nonlocal done
                    ins.then_inc(step, 1)
                    done += 1
                    dve.wait_ge(step, done)

                for e in range(E):
                    nc.vector.memset(number[:, :, e:e + 1], float(e - E)).then_inc(step, 1)
                done = E
                dve.wait_ge(step, done)
                for c in range(choices):
                    src = logits if c == 0 else left
                    next_(nc.vector.tensor_reduce(m[c][:], src[:], AX_X, ALU.max))
                    next_(nc.vector.tensor_tensor(at_max[:], src[:], wide(m[c]), ALU.is_ge))
                    next_(nc.vector.tensor_tensor(at_max[:], at_max[:], number[:].to_broadcast(shape), ALU.mult))
                    next_(nc.vector.tensor_reduce(first[:], at_max[:], AX_X, ALU.min))
                    next_(nc.vector.tensor_tensor(one[c][:], number[:].to_broadcast(shape), wide(first), ALU.is_equal))
                    if c + 1 < choices:
                        next_(nc.vector.scalar_tensor_tensor(left[:], one[c][:], FAR, logits[:], ALU.mult, ALU.add))
                if choices == 1:
                    nc.vector.tensor_copy(comb[:].rearrange("p e t -> p t e"), one[0][:]).then_inc(step, 1)
                else:
                    next_(nc.vector.tensor_tensor(left[:], logits[:], wide(m[0]), ALU.subtract))
                    next_(nc.vector.tensor_tensor(gap[:], m[1][:], m[0][:], ALU.subtract))
                    nc.vector.memset(first[:], 0.0).then_inc(exp_in, 1)
                    dve.wait_ge(exp_done, 2)
                    next_(nc.vector.tensor_reduce(total[:], ex[:], AX_X, ALU.add))
                    next_(nc.vector.reciprocal(total[:], total[:]))
                    next_(nc.vector.tensor_tensor(gap[:], gap[:], total[:], ALU.mult))
                    next_(nc.vector.tensor_tensor(one[0][:], one[0][:], wide(total), ALU.mult))
                    next_(nc.vector.tensor_tensor(one[1][:], one[1][:], wide(gap), ALU.mult))
                    nc.vector.tensor_tensor(comb[:].rearrange("p e t -> p t e"), one[0][:], one[1][:], ALU.add).then_inc(step, 1)

            @block.scalar
            def _(act):
                if choices == 2:
                    act.wait_ge(exp_in, 1)
                    nc.scalar.activation(ex[:], left[:], ACT.Exp).then_inc(exp_done, 1)
                    nc.scalar.activation(gap[:], gap[:], ACT.Exp).then_inc(exp_done, 1)


def experts(nc, kit, sem, tag, x, xt_all, comb, w1_dram, w3_dram, w2_dram, b1_dram, b2_dram):
    E, FF = w1_dram.shape[1:]
    NC = w2_dram.shape[2]
    ROWS = w2_dram.shape[0]
    widths = [min(ROWS, FF - c * ROWS) for c in range(NC)]
    BLOCKS = TOKENS // HALF
    BT = HALF // P
    gated = w3_dram is not None
    HB = NC if not gated else 2 * NC
    with ExitStack() as ctx:
        k = kit.scope(ctx)
        w1_all = k.sb(f"{tag}_w1_all", [P, E, FF])
        w3_all = k.sb(f"{tag}_w3_all", [P, E, FF]) if gated else None
        w2_all = k.sb(f"{tag}_w2_all", [P, E, NC, D])
        b1_all = k.sb(f"{tag}_b1_all", [P, E, NC]) if b1_dram is not None else None
        b2_all = k.sb(f"{tag}_b2_all", [P, E, D]) if b2_dram is not None else None
        w1 = k.sb(f"{tag}_w1", [P, FF])
        w3 = k.sb(f"{tag}_w3", [P, FF]) if gated else None
        w2 = k.sb(f"{tag}_w2", [P, NC, D])
        b1 = k.sb(f"{tag}_b1", [P, NC]) if b1_dram is not None else None
        silu = [k.sb(f"{tag}_silu{i}", [P, NC, HALF]) for i in range(2)] if gated else None
        ht = [k.sb(f"{tag}_ht{i}", [P, NC, HALF]) for i in range(2)]
        tmp = k.sb(f"{tag}_tmp", [P, BT, D])
        h_ps = k.ps(f"{tag}_h", [P, HB, HALF])
        y_ps = k.ps(f"{tag}_y", [P, 2, HALF])
        loaded = sem(f"{tag}_loaded")
        w_ready = sem(f"{tag}_w_ready")
        h_done, h_out, silu_done, y_done, y_out, landed = \
            (sem(f"{tag}_{n}") for n in ("h_done", "h_out", "silu", "y_done", "y_out", "landed"))
        ht_free, ht_free_v, w_free = sem(f"{tag}_ht_free"), sem(f"{tag}_ht_free_v"), sem(f"{tag}_w_free")
        b2_flat = b2_all[:].rearrange("p e d -> p (e d)") if b2_dram is not None else None
        xflat = x[:].rearrange("p t d -> p (t d)")
        cflat = comb[:].rearrange("p e t -> p (e t)") if comb is not None else None
        loads = [(w1_all, w1_dram, P), (w2_all, w2_dram, ROWS)]
        if gated:
            loads.append((w3_all, w3_dram, P))
        if b1 is not None:
            loads += [(b1_all, b1_dram, ROWS), (b2_all, b2_dram, P)]
        stages = [(w1, w1_all, FF, P), (w2, w2_all, NC * D, ROWS)]
        if gated:
            stages.append((w3, w3_all, FF, P))
        if b1 is not None:
            stages.append((b1, b1_all, NC, ROWS))
        NST = len(stages)
        adds = (b2_dram is not None) + (comb is not None) + 1

        def flat(a):
            names = "abc"[:len(a.shape) - 1]
            return a[:].rearrange(f"p {' '.join(names)} -> p ({' '.join(names)})")

        with nc.Block() as block:

            @block.sync
            def _(sp):
                for dst, src, rows in loads:
                    sp.dma_start(dst[0:rows], src).then_inc(loaded, 16)

            @block.tensor
            def _(pe):
                def y(n, par):
                    pe.wait_ge(h_out, n * NC + 2 * NC)
                    pe.wait_ge(y_out, n + 1)
                    for t in range(BT):
                        for c, rows in enumerate(widths):
                            mm = nc.tensor.matmul(y_ps[:, par, t * P:(t + 1) * P], ht[par][0:rows, c, t * P:(t + 1) * P],
                                                  w2[0:rows, c, :], start=c == 0, stop=c == NC - 1)
                    mm.then_inc(y_done, 1)
                    pe.wait_ge(y_done, n + 1)
                    pe.sem_inc(ht_free_v if gated else ht_free, 1)

                def h(n, at):
                    for c, rows in enumerate(widths):
                        pe.wait_ge(h_out, n * NC + c + 1)
                        cols = slice(c * ROWS, c * ROWS + rows)
                        rhs = xt_all[:, bass.ds(at * HALF, HALF)]
                        mm = nc.tensor.matmul(h_ps[0:rows, c, :], w1[:, cols], rhs, start=True, stop=True)
                        if gated:
                            mm = nc.tensor.matmul(h_ps[0:rows, NC + c, :], w3[:, cols], rhs, start=True, stop=True)
                        mm.then_inc(h_done, 1)

                with pe.Fori(0, E) as e:
                    kit.ge_apart(pe, w_ready, e * NST + NST)
                    with pe.Fori(0, BLOCKS // 2) as it:
                        n = e * BLOCKS + it * 2
                        h(n, it * 2)
                        h(n + 1, it * 2 + 1)
                        y(n, 0)
                        y(n + 1, 1)
                    pe.wait_ge(y_done, e * BLOCKS + BLOCKS)
                    pe.sem_inc(w_free, 1)

            @block.scalar
            def _(act):
                act.wait_ge(loaded, 16 * len(loads))
                act.sem_inc(h_out, NC)
                act.sem_inc(ht_free, 2)
                act.sem_inc(ht_free_v, 2)
                act.sem_inc(w_free, 1)
                with act.Fori(0, E) as e:
                    act.wait_ge(w_free, e + 1)
                    for dst, src, cols, rows in stages:
                        nc.scalar.copy(flat(dst)[0:rows], flat(src)[0:rows, bass.ds(e * cols, cols)]).then_inc(w_ready, 1)
                    act.wait_ge(w_ready, e * NST + NST)
                    with act.Fori(0, BLOCKS // 2) as it:
                        for par in range(2):
                            n = e * BLOCKS + it * 2 + par
                            act.wait_ge(ht_free, n + 1)
                            for c, rows in enumerate(widths):
                                act.wait_ge(h_done, n * NC + c + 1)
                                if gated:
                                    nc.scalar.activation(silu[par][0:rows, c, :], h_ps[0:rows, c, :], ACT.Silu)\
                                        .then_inc(silu_done, 1)
                                elif b1 is not None:
                                    nc.scalar.activation(ht[par][0:rows, c, :], h_ps[0:rows, c, :], ACT.Relu,
                                                         bias=b1[0:rows, c:c + 1]).then_inc(h_out, 1)

            @block.vector
            def _(dve):
                dve.sem_inc(y_out, 2)

                def add(e, par, at):
                    n = e * BLOCKS + at
                    dve.wait_ge(y_done, n + 1)
                    done = 0
                    src = y_ps[:, par, :].rearrange("p (t d) -> p t d", d=D)
                    if b2_all is not None:
                        bias = b2_flat[:, bass.ds(e * D, D)].unsqueeze(1).to_broadcast([P, BT, D])
                        nc.vector.tensor_tensor(tmp[:], src, bias, ALU.add).then_inc(landed, 1)
                        done += 1
                        dve.wait_ge(landed, n * adds + done)
                        src = tmp[:]
                    if comb is not None:
                        weight = cflat[:, bass.ds(e * ALL_TILES + at * BT, BT)].unsqueeze(2).to_broadcast([P, BT, D])
                        nc.vector.tensor_tensor(tmp[:], src, weight, ALU.mult).then_inc(landed, 1)
                        done += 1
                        dve.wait_ge(landed, n * adds + done)
                        src = tmp[:]
                    rows = xflat[:, bass.ds(at * (BT * D), BT * D)].rearrange("p (t d) -> p t d", d=D)
                    nc.vector.tensor_tensor(rows, rows, src, ALU.add).then_inc(landed, 1)
                    dve.wait_ge(landed, n * adds + adds)
                    dve.sem_inc(y_out, 1)

                def gate_mult(n, par):
                    for c, rows in enumerate(widths):
                        dve.wait_ge(silu_done, n * NC + c + 1)
                        if c == 0:
                            dve.wait_ge(ht_free_v, n + 1)
                        nc.vector.tensor_tensor(ht[par][0:rows, c, :], silu[par][0:rows, c, :],
                                                h_ps[0:rows, NC + c, :], ALU.mult).then_inc(h_out, 1)
                    dve.wait_ge(h_out, n * NC + 2 * NC)
                    dve.sem_inc(ht_free, 1)

                with dve.Fori(0, E) as e:
                    with dve.Fori(0, BLOCKS // 2) as it:
                        for par in range(2):
                            if gated:
                                gate_mult(e * BLOCKS + it * 2 + par, par)
                        for par in range(2):
                            add(e, par, it * 2 + par)


def ffn0(nc, kit, sem, x, ident, eps, gate_dram, bias_dram, w1_dram, b1_dram, w2_dram, b2_dram):
    E = gate_dram.shape[1]
    with ExitStack() as ctx:
        k = kit.scope(ctx)
        xt_all = k.sb("f0_xt_all", [P, TOKENS])
        logits = k.sb("f0_logits", [P, ALL_TILES, E])
        comb = k.sb("f0_comb", [P, E, ALL_TILES])
        norm_and_gate(nc, k, sem, "g0", x, ident, eps, gate_dram, bias_dram, xt_all, logits)
        choose(nc, k, sem, "c0", logits, comb, 1)
        experts(nc, k, sem, "e0", x, xt_all, comb, w1_dram, None, w2_dram, b1_dram, b2_dram)


def ffn1(nc, kit, sem, x, ident, eps, gate_dram, w1_dram, w3_dram, w2_dram, sw1_dram, sw3_dram, sw2_dram):
    E = gate_dram.shape[1]
    with ExitStack() as ctx:
        k = kit.scope(ctx)
        xt_all = k.sb("f1_xt_all", [P, TOKENS])
        logits = k.sb("f1_logits", [P, ALL_TILES, E])
        comb = k.sb("f1_comb", [P, E, ALL_TILES])
        norm_and_gate(nc, k, sem, "g1", x, ident, eps, gate_dram, None, xt_all, logits)
        choose(nc, k, sem, "c1", logits, comb, 2)
        experts(nc, k, sem, "e1", x, xt_all, comb, w1_dram, w3_dram, w2_dram, None, None)
        experts(nc, k, sem, "es", x, xt_all, None, sw1_dram, sw3_dram, sw2_dram, None, None)


def transformer_kernel(nc, x_in, l0_attn_w, gate0, gate0_bias, w1_0, b1_0, w2_0, b2_0,
                       wq, w_down, wk_up, wv_up, wo, rope, gate1, w1_1, w3_1, w2_1, sw1, sw3, sw2, out):
    DH0, CLAMP = 64, 50.0
    with ExitStack() as ctx:
        kit = Kit(nc, ctx, ctx.enter_context(nc.semaphore("passed")))

        def in_stage(stage, *args):
            taken = []

            def sem(name):
                taken.append(nc.alloc_semaphore(name=name))
                return taken[-1]

            stage(nc, kit, sem, *args)
            nc.clear_and_free_semaphores(taken)
            nc.all_engine_barrier()

        x = kit.sb("x", [P, ALL_TILES, D])
        ident = kit.sb("ident", [P, P])
        ones = kit.sb("ones", [P, 32])
        eps = kit.sb("eps", [P, 1])
        xt0 = nc.dram_tensor("xt0", [BATCH, 3, P, SEQ], F32).ap()
        xt1 = nc.dram_tensor("xt1", [BATCH, 3, P, SEQ], F32).ap()
        parts = nc.dram_tensor("qk_parts", [BATCH, 2 * PARTS, P, SEQ], BF16).ap()
        values = nc.dram_tensor("values", [BATCH, QUADS, P, TILES, QUAD, V_COLS], F32).ap()

        in_stage(load_residual, x_in, x, ident, ones, eps)
        in_stage(layernorm, "ln0", x, ident, eps, xt0)
        in_stage(attention0, x, xt0, l0_attn_w, ones, DH0 ** -0.5, CLAMP)
        in_stage(ffn0, x, ident, eps, gate0, gate0_bias, w1_0, b1_0, w2_0, b2_0)
        in_stage(layernorm, "ln1", x, ident, eps, xt1)
        in_stage(project1, ident, xt1, wq, w_down, wk_up, wv_up, rope, parts, values)
        with ExitStack() as heads_ctx:
            heads = kit.scope(heads_ctx).sb("heads", [P, ALL_TILES, D])
            in_stage(attention1, ident, parts, values, heads, DH1 ** -0.5)
            in_stage(project_out1, ident, x, heads, wo)
        in_stage(ffn1, x, ident, eps, gate1, w1_1, w3_1, w2_1, sw1, sw3, sw2)

        stored = ctx.enter_context(nc.semaphore("stored"))
        with nc.Block() as block:

            @block.sync
            def _(sp):
                for b in range(BATCH):
                    sp.dma_start(out[b].rearrange("(t p) d -> p t d", p=P), x[:, b * TILES:(b + 1) * TILES, :])\
                        .then_inc(stored, 16)
                sp.wait_ge(stored, 16 * BATCH)


def _rope_constants():
    import numpy as np
    theta = 10000.0
    inverse = 1.0 / theta ** (np.arange(0, DH1, 2, dtype=np.float32) / DH1)
    angle = np.outer(np.arange(SEQ, dtype=np.float32), inverse)
    table = np.empty((D, 2, SEQ), np.float32)
    for d in range(D):
        pair = d % DH1 // 2
        table[d, 0] = np.cos(angle[:, pair])
        table[d, 1] = np.sin(angle[:, pair]) * (-1 if d % 2 == 0 else 1)
    return table


def kernel(L0_attn_x, L0_attn_Wq, L0_attn_Wk, L0_attn_Wv, L0_attn_Wo, L0_ffn_gate_w, L0_ffn_gate_b,
           L0_ffn_expert_bias, L0_ffn_w1, L0_ffn_b1, L0_ffn_w2, L0_ffn_b2, L1_attn_wq, L1_attn_w_down,
           L1_attn_wk_up, L1_attn_wv_up, L1_attn_wo, L1_ffn_gate_w, L1_ffn_w1, L1_ffn_w2, L1_ffn_w3,
           L1_ffn_sw1, L1_ffn_sw2, L1_ffn_sw3):
    import numpy as np
    import concourse.bacc as bacc
    from concourse.bass_utils import run_bass_kernel_spmd

    a = np.asarray
    pairs = L0_attn_Wq.shape[0] // P

    def chunked(w, rows):
        w = a(w)
        n = -(-w.shape[1] // rows)
        w = np.pad(w, ((0, 0), (0, n * rows - w.shape[1]), (0, 0)))
        return w.reshape(w.shape[0], n, rows, D).transpose(2, 0, 1, 3)

    exchanged = np.arange(D) ^ 1
    by_pair = [a(w).reshape(pairs, P, D).transpose(0, 2, 1) for w in (L0_attn_Wq, L0_attn_Wk, L0_attn_Wv)]
    by_pair.append(a(L0_attn_Wo).T.reshape(pairs, P, D))
    shared_rows = L1_ffn_sw2.shape[0] // 2
    laid_out = {
        "x": a(L0_attn_x),
        "l0_attn_w": np.stack(by_pair, 2),
        "gate0": a(L0_ffn_gate_w).T,
        "gate0_bias": np.broadcast_to(np.stack([a(L0_ffn_gate_b), a(L0_ffn_expert_bias)]), (P, 2, L0_ffn_gate_b.shape[0])),
        "w1_0": a(L0_ffn_w1).transpose(1, 0, 2),
        "b1_0": a(L0_ffn_b1).reshape(L0_ffn_b1.shape[0], -1, P).transpose(2, 0, 1),
        "w2_0": chunked(L0_ffn_w2, P),
        "b2_0": np.broadcast_to(a(L0_ffn_b2), (P,) + L0_ffn_b2.shape),
        "wq": np.stack([a(L1_attn_wq), a(L1_attn_wq)[:, exchanged]], 1),
        "w_down": a(L1_attn_w_down),
        "wk_up": np.stack([a(L1_attn_wk_up), a(L1_attn_wk_up)[:, exchanged]], 1),
        "wv_up": a(L1_attn_wv_up),
        "wo": a(L1_attn_wo),
        "rope": _rope_constants(),
        "gate1": a(L1_ffn_gate_w).T,
        "w1_1": a(L1_ffn_w1).transpose(1, 0, 2),
        "w3_1": a(L1_ffn_w3).transpose(1, 0, 2),
        "w2_1": chunked(L1_ffn_w2, P),
        "sw1": a(L1_ffn_sw1)[:, None],
        "sw3": a(L1_ffn_sw3)[:, None],
        "sw2": chunked(a(L1_ffn_sw2)[None], shared_rows),
    }
    nc = bacc.Bacc("TRN2", target_bir_lowering=False, num_devices=1)
    arrays, args = {}, []
    for name, array in laid_out.items():
        array = np.ascontiguousarray(array)
        arrays[f"in_{name}"] = array
        args.append(nc.dram_tensor(f"in_{name}", array.shape, mybir.dt.from_np(array.dtype), kind="ExternalInput").ap())
    out = nc.dram_tensor("out_x", (BATCH, SEQ, D), F32, kind="ExternalOutput").ap()
    transformer_kernel(nc, *args, out)
    result = run_bass_kernel_spmd(nc, [arrays], core_ids=[0])
    return result.results[0]["out_x"]
```

```python
from contextlib import ExitStack

import concourse.bass as bass
from concourse import mybir

ACT = mybir.ActivationFunctionType
ALU = mybir.AluOpType
AX_X = mybir.AxisListType.X
F32 = mybir.dt.float32
F32R = mybir.dt.float32r
BF16 = mybir.dt.bfloat16
I32 = mybir.dt.int32
U32 = mybir.dt.uint32

P = 128
D = 128
BATCH, SEQ = 4, 1024
TILES = SEQ // P
TOKENS = BATCH * SEQ
ALL_TILES = TOKENS // P
HALF = 512
LN_EPS = 1e-5


def ge(eng, sem, value):
    if isinstance(value, int) and value <= 0:
        return
    eng.wait_ge(sem, value)


class Kit:

    def __init__(self, nc, ctx, passed):
        self.nc, self.ctx, self.passed = nc, ctx, passed

    def scope(self, ctx):
        return Kit(self.nc, ctx, self.passed)

    def sb(self, name, shape, dt=F32):
        return self.ctx.enter_context(self.nc.sbuf_tensor(name, shape, dt))

    def ps(self, name, shape, dt=F32):
        return self.ctx.enter_context(self.nc.psum_tensor(name, shape, dt))

    def ge_apart(self, eng, sem, value):
        ge(eng, sem, value)
        if not isinstance(value, int):
            eng.sem_inc(self.passed, 1)


def load_residual(nc, kit, sem, x_dram, x, ident, ones, eps):
    loaded, made = sem("x_loaded"), sem("consts_made")
    with nc.Block() as block:

        @block.sync
        def _(sp):
            for b in range(BATCH):
                sp.dma_start(x[:, b * TILES:(b + 1) * TILES, :],
                             x_dram[b].rearrange("(t p) d -> p t d", p=P)).then_inc(loaded, 16)
            sp.wait_ge(loaded, 16 * BATCH)

        @block.gpsimd
        def _(pool):
            nc.gpsimd.memset(ident[:], 0.0).then_inc(made, 1)
            nc.gpsimd.memset(ones[:], 1.0).then_inc(made, 1)
            nc.gpsimd.memset(eps[:], LN_EPS).then_inc(made, 1)
            kit.ge_apart(pool, made, 3)
            nc.gpsimd.affine_select(out=ident[:], in_=ident[:], compare_op=ALU.not_equal, fill=1.0, base=0,
                                    pattern=[[1, P]], channel_multiplier=-1).then_inc(made, 1)
            kit.ge_apart(pool, made, 4)


def layernorm(nc, kit, sem, tag, x, ident, eps, xt_dram):
    with ExitStack() as ctx:
        k = kit.scope(ctx)
        stats = k.sb(f"{tag}_stats", [P, TILES, 6])
        mv = k.sb(f"{tag}_mv", [P, TILES, 2])
        std = k.sb(f"{tag}_std", [P, TILES])
        rstd = k.sb(f"{tag}_rstd", [P, TILES])
        xn = k.sb(f"{tag}_xn", [P, TILES, D])
        xt = k.sb(f"{tag}_xt", [P, SEQ])
        high = k.sb(f"{tag}_high", [P, SEQ], F32R)
        low = k.sb(f"{tag}_low", [P, SEQ], F32R)
        turned = k.ps(f"{tag}_turned", [P, SEQ])
        stats_done, mv_done = sem(f"{tag}_stats"), sem(f"{tag}_mv")
        std_done, rstd_done = sem(f"{tag}_std"), sem(f"{tag}_rstd")
        xn_done, turn_done = sem(f"{tag}_xn"), sem(f"{tag}_turn")
        xt_done, high_done, low_done = sem(f"{tag}_xt"), sem(f"{tag}_high"), sem(f"{tag}_low")
        stored, out_free = sem(f"{tag}_stored"), sem(f"{tag}_out_free")
        xflat = x[:].rearrange("p t d -> p (t d)")

        with nc.Block() as block:

            @block.vector
            def _(dve):
                with dve.Fori(0, BATCH) as b:
                    for t in range(TILES):
                        last = nc.vector.bn_stats(stats[:, t, :], xflat[:, bass.ds(b * (TILES * D) + t * D, D)])
                    last.then_inc(stats_done, 1)
                    kit.ge_apart(dve, stats_done, b + 1)
                    for t in range(TILES):
                        last = nc.vector.bn_aggr(mv[:, t, :], stats[:, t, :])
                    last.then_inc(mv_done, 1)
                    dve.wait_ge(std_done, b + 1)
                    nc.vector.reciprocal(rstd[:], std[:]).then_inc(rstd_done, 1)
                    dve.wait_ge(rstd_done, b + 1)
                    for t in range(TILES):
                        last = nc.vector.tensor_scalar(xn[:, t, :], xflat[:, bass.ds(b * (TILES * D) + t * D, D)],
                                                       mv[:, t, 0:1], rstd[:, t:t + 1], ALU.subtract, ALU.mult)
                    last.then_inc(xn_done, 1)
                    dve.wait_ge(high_done, b + 1)
                    nc.vector.tensor_tensor(low[:], xt[:], high[:].bitcast(F32), ALU.subtract).then_inc(low_done, 1)

            @block.scalar
            def _(act):
                with act.Fori(0, BATCH) as b:
                    act.wait_ge(mv_done, b + 1)
                    nc.scalar.activation(std[:], mv[:, :, 1], ACT.Sqrt, bias=eps[:, 0:1]).then_inc(std_done, 1)
                    act.wait_ge(turn_done, b + 1)
                    act.wait_ge(out_free, b + 1)
                    nc.scalar.copy(xt[:], turned[:]).then_inc(xt_done, 1)
                    nc.scalar.copy(high[:], turned[:]).then_inc(high_done, 1)

            @block.tensor
            def _(pe):
                with pe.Fori(0, BATCH) as b:
                    pe.wait_ge(xn_done, b + 1)
                    for t in range(TILES):
                        last = nc.tensor.transpose(turned[:, t * P:(t + 1) * P], xn[:, t, :], ident[:])
                    last.then_inc(turn_done, 1)

            @block.sync
            def _(sp):
                sp.sem_inc(out_free, 1)
                with sp.Fori(0, BATCH) as b:
                    out = xt_dram[bass.ds(b, 1)].rearrange("b k p s -> (b k) p s")
                    sp.wait_ge(xt_done, b + 1)
                    sp.dma_start(out[0], xt[:]).then_inc(stored, 16)
                    sp.wait_ge(high_done, b + 1)
                    sp.dma_start(out[1], high[:].bitcast(F32)).then_inc(stored, 16)
                    sp.wait_ge(low_done, b + 1)
                    sp.dma_start(out[2], low[:].bitcast(F32)).then_inc(stored, 16)
                    sp.wait_ge(stored, b * 48 + 48)
                    sp.sem_inc(out_free, 1)


def chunk_plan():
    chunks, at = [], 0
    for half in range(2):
        for j in range(TILES):
            lead = max(0, j * P - half * HALF)
            if lead >= HALF:
                continue
            chunks.append((half, j, HALF - lead, at))
            at += 2 * (HALF - lead)
    return chunks, at


CHUNKS, P_COLS = chunk_plan()
NCH = len(CHUNKS)
GROUPS = [(0, 4), (4, 6), (6, 8), (8, 12)]
DIAGONAL_GROUPS = (0, 3)


def attention0(nc, kit, sem, x, xt_dram, w_dram, ones, scale, clamp):
    PAIRS = w_dram.shape[0]
    UNITS = BATCH * PAIRS
    DH = P // 2
    SEQ_BITS = PAIRS.bit_length() - 1
    with ExitStack() as ctx:
        k = kit.scope(ctx)
        xt = k.sb("a0_xt", [P, SEQ])
        xh = [k.sb(f"a0_xh{i}", [P, SEQ], F32R) for i in range(2)]
        xl = [k.sb(f"a0_xl{i}", [P, SEQ], F32R) for i in range(2)]
        w = [k.sb(f"a0_w{i}", [P, 2, P]) for i in range(2)]
        wv = [k.sb(f"a0_wv{i}", [P, P]) for i in range(2)]
        wo = [k.sb(f"a0_wo{i}", [P, P]) for i in range(2)]
        wh = [k.sb(f"a0_wh{i}", [P, 2, P], F32R) for i in range(2)]
        wl = [k.sb(f"a0_wl{i}", [P, 2, P], F32R) for i in range(2)]
        stage = k.sb("a0_stage", [P, 2, 2, SEQ], F32R)
        q_st = [k.sb(f"a0_q{i}", [P, 2, SEQ], F32R) for i in range(2)]
        kh_st = [k.sb(f"a0_kh{i}", [P, 2, SEQ], F32R) for i in range(2)]
        kl_st = [k.sb(f"a0_kl{i}", [P, 2, SEQ], F32R) for i in range(2)]
        v = [k.sb(f"a0_v{i}", [P, TILES, P]) for i in range(2)]
        prob = [k.sb(f"a0_p{i}", [P, P_COLS]) for i in range(2)]
        part = k.sb("a0_part", [P, 2, SEQ])
        rsum = k.sb("a0_rsum", [P, HALF])
        rhl = k.sb("a0_rhl", [P, 2, HALF], F32R)
        spread = k.sb("a0_spread", [P, 2, P], F32R)
        ot = k.sb("a0_ot", [P, SEQ])
        score_ps = k.ps("a0_score", [P, 2, 2, HALF])
        out_ps = k.ps("a0_out", [P, 2, HALF])
        misc = k.ps("a0_misc", [P, 2, HALF])

        x_loaded = [sem(f"a0_x_loaded{i}") for i in range(2)]
        xt_loaded = sem("a0_xt_loaded")
        w_loaded = [sem(f"a0_w_loaded{i}") for i in range(2)]
        wv_loaded = [sem(f"a0_wv_loaded{i}") for i in range(2)]
        wo_loaded = [sem(f"a0_wo_loaded{i}") for i in range(2)]
        w_high, w_split = sem("a0_w_high"), sem("a0_w_split")
        NAMES = ["q0", "q1", "k0", "k1", "v0", "v1"]
        proj = {n: sem(f"a0_proj_{n}") for n in NAMES}
        evac = {n: sem(f"a0_evac_{n}") for n in NAMES}
        high = {n: sem(f"a0_high_{n}") for n in NAMES[:4]}
        stacked = sem("a0_stacked")
        scored, tanh_done, exp_done, masked = (sem(f"a0_{n}") for n in ("scored", "tanh", "exp", "masked"))
        pv_done = [sem(f"a0_pv{i}") for i in range(2)]
        added = sem("a0_added")
        summed, recip, r_high, r_split = (sem(f"a0_{n}") for n in ("summed", "recip", "r_high", "r_split"))
        spread_made = sem("a0_spread_made")
        out_evac = [sem(f"a0_out_evac{i}") for i in range(2)]
        bcast = [sem(f"a0_bcast{i}") for i in range(2)]
        normed = [sem(f"a0_normed{i}") for i in range(2)]
        wo_done = [sem(f"a0_wo{i}") for i in range(2)]
        x_added = [sem(f"a0_x_added{i}") for i in range(2)]
        QK_JOBS, V_JOBS = {0: "q0", 2: "k0", 3: "q1", 5: "k1"}, {4: 0, 7: 1}
        ADDS = NCH - 1
        STACK_DMAS = 12
        xflat = x[:].rearrange("p t d -> p (t d)")

        def of(dram, index):
            if isinstance(index, int):
                return dram[index]
            names = " ".join("abcde"[:len(dram.shape) - 1])
            return dram[bass.ds(index, 1)].rearrange(f"z {names} -> (z {names.split()[0]}) {' '.join(names.split()[1:])}")

        def exists(u):
            return not isinstance(u, int) or 0 <= u < UNITS

        def chunk_of(buffer, i, cols=None):
            _, _, width, at = CHUNKS[i]
            a, b = cols or (0, width)
            return buffer[:, at:at + 2 * width].rearrange("p (h q) -> p h q", h=2)[:, :, a:b]

        def load_unit(sp, n, p):
            if not exists(n):
                return
            kit.ge_apart(sp, proj["k1"], n - 1)
            kit.ge_apart(sp, w_split, n - 1)
            sp.dma_start(w[p][:], of(w_dram, n & (PAIRS - 1))[:, 0:2, :]).then_inc(w_loaded[p], 16)
            src = of(xt_dram, (n >> SEQ_BITS) & (BATCH - 1))
            sp.dma_start(xh[p][:].bitcast(F32), src[1]).then_inc(x_loaded[p], 16)
            sp.dma_start(xl[p][:].bitcast(F32), src[2]).then_inc(x_loaded[p], 16)

        def load_xt(sp, n):
            if not exists(n):
                return
            kit.ge_apart(sp, proj["v1"], n)
            sp.dma_start(xt[:], of(xt_dram, (n >> SEQ_BITS) & (BATCH - 1))[0]).then_inc(xt_loaded, 16)

        def sp_step(sp, u, p):
            load_unit(sp, u + 2, p)
            if exists(u):
                kit.ge_apart(sp, wo_done[1], u - 1)
                sp.dma_start(wo[p][:], of(w_dram, u & (PAIRS - 1))[:, 3, :]).then_inc(wo_loaded[p], 16)
            n, pn = u + 1, 1 - p
            if exists(n):
                kit.ge_apart(sp, proj["v1"], n - 1)
                sp.dma_start(wv[pn][:], of(w_dram, n & (PAIRS - 1))[:, 2, :]).then_inc(wv_loaded[pn], 16)
                sg = stage[:].bitcast(F32)
                A, B = slice(0, DH), slice(DH, P)
                for what, first, second in (("q", "q0", "q1"), ("k", "k0", "k1")):
                    kit.ge_apart(sp, evac[first], n + 1)
                    kit.ge_apart(sp, evac[second], n + 1)
                    if what == "q":
                        moves = [(q_st[pn], A, 0, A, 0), (q_st[pn], B, 0, A, 1),
                                 (q_st[pn], A, 1, B, 1), (q_st[pn], B, 1, B, 0)]
                        row = 0
                    else:
                        moves = [(st[pn], half, h, (A, B)[h], part_)
                                 for st, part_ in ((kh_st, 0), (kl_st, 1)) for h in range(2) for half in (A, B)]
                        row = 1
                    for st, to, h, frm, hl in moves:
                        sp.dma_start(st[to, h, :].bitcast(F32), sg[frm, row, hl, :]).then_inc(stacked, 16)
            load_xt(sp, u + 1)

        def split_w(pool, n, p):
            if not exists(n):
                return
            kit.ge_apart(pool, w_loaded[p], 16 * (n >> 1) + 16)
            kit.ge_apart(pool, proj["k1"], n - 1)
            nc.gpsimd.tensor_copy(wh[p][:], w[p][:, 0:2, :]).then_inc(w_high, 1)
            kit.ge_apart(pool, w_high, n + 1)
            nc.gpsimd.tensor_tensor(wl[p][:], w[p][:, 0:2, :], wh[p][:].bitcast(F32),
                                    ALU.subtract).then_inc(w_split, 1)

        def pool_step(pool, u, p):
            for g in DIAGONAL_GROUPS:
                if exists(u):
                    kit.ge_apart(pool, exp_done, u * len(GROUPS) + g + 1)
                    for i in range(*GROUPS[g]):
                        blk = chunk_of(prob[p], i, (0, P))
                        last = nc.gpsimd.affine_select(out=blk, in_=blk, compare_op=ALU.is_ge, fill=0.0, base=0,
                                                       pattern=[[0, 2], [1, P]], channel_multiplier=-1)
                    last.then_inc(masked, 1)
                if g == 0:
                    split_w(pool, u + 2, p)

        def act_high(act, n, name):
            if not exists(n):
                return
            which, half = "qk".index(name[0]), int(name[1])
            act.wait_ge(proj[name], n + 1)
            if name == "q0":
                ge(act, stacked, n * (16 * STACK_DMAS))
            nc.scalar.copy(stage[:, which, 0, half * HALF:(half + 1) * HALF], misc[:, half, :])\
                .then_inc(high[name], 1)

        def act_v(act, u, p, half):
            act.wait_ge(proj[f"v{half}"], u + 1)
            if half == 0:
                ge(act, pv_done[1], u - 1)
            nc.scalar.copy(v[p][:, half * (TILES // 2):(half + 1) * (TILES // 2), :].rearrange("p t d -> p (t d)"),
                           misc[:, half, :]).then_inc(evac[f"v{half}"], 1)

        def act_out(act, m, half):
            if not exists(m):
                return
            act.wait_ge(pv_done[half], m + 1)
            ge(act, wo_done[half], m)
            nc.scalar.copy(ot[:, half * HALF:(half + 1) * HALF], out_ps[:, half, :]).then_inc(out_evac[half], 1)

        def act_step(act, u, p):
            act_out(act, u - 2, 1)
            if exists(u):
                ge(act, pv_done[1], u - 1)
                ge(act, added, (u - 1) * ADDS)
            g = 0
            for i, (_, _, width, at) in enumerate(CHUNKS):
                if exists(u):
                    act.wait_ge(scored, u * NCH + i + 1)
                    nc.scalar.activation(chunk_of(prob[p], i), score_ps[:, i % 2, :, 0:width], ACT.Tanh,
                                         scale=scale / clamp).then_inc(tanh_done, 1)
                if i in QK_JOBS:
                    act_high(act, u + 1, QK_JOBS[i])
                if i == 6:
                    act_out(act, u - 1, 0)
                if i in V_JOBS and exists(u):
                    act_v(act, u, p, V_JOBS[i])
                if i + 1 == GROUPS[g][1] and exists(u):
                    a = CHUNKS[GROUPS[g][0]][3]
                    act.wait_ge(tanh_done, u * NCH + i + 1)
                    nc.scalar.activation(prob[p][:, a:at + 2 * width], prob[p][:, a:at + 2 * width], ACT.Exp,
                                         scale=clamp).then_inc(exp_done, 1)
                    g += 1

        def pe_scores(pe, u, p, i):
            half, j, width, _ = CHUNKS[i]
            q0 = half * HALF + HALF - width
            if i == 0:
                pe.wait_ge(stacked, (u + 1) * (16 * STACK_DMAS))
            ge(pe, tanh_done, u * NCH + i - 1)
            for h in range(2):
                for st in (kh_st, kl_st):
                    last = nc.tensor.matmul(score_ps[:, i % 2, h, 0:width], st[p][:, h, j * P:(j + 1) * P],
                                            q_st[p][:, h, q0:q0 + width], start=st is kh_st, stop=st is kl_st)
            last.then_inc(scored, 1)

        def pe_pv(pe, m, p, i):
            half, j, width, _ = CHUNKS[i]
            g = [g for g, (a, b) in enumerate(GROUPS) if a == i]
            if g and g[0] in DIAGONAL_GROUPS:
                pe.wait_ge(masked, m * 2 + DIAGONAL_GROUPS.index(g[0]) + 1)
            elif g:
                pe.wait_ge(exp_done, m * len(GROUPS) + g[0] + 1)
            if j == 0:
                ge(pe, out_evac[half], m)
                ge(pe, evac["v1"], m + 1)
            last_j = max(c[1] for c in CHUNKS if c[0] == half)
            for h in range(2):
                mm = nc.tensor.matmul(out_ps[h * DH:(h + 1) * DH, half, HALF - width:HALF],
                                      v[p][:, j, h * DH:(h + 1) * DH], chunk_of(prob[p], i)[:, h, :],
                                      start=j == 0, stop=j == last_j)
            if j == last_j:
                mm.then_inc(pv_done[half], 1)

        def pe_qk(pe, n, p, name):
            which, half = "qk".index(name[0]), int(name[1])
            if name == "q0":
                pe.wait_ge(x_loaded[p], 32 * (n >> 1) + 32)
                pe.wait_ge(w_split, n + 1)
                ge(pe, x_added[0], n - 2)
            ge(pe, {"k0": evac["q0"], "k1": evac["q1"], "q1": x_added[1]}.get(name, evac["q0"]),
               {"k0": n + 1, "k1": n + 1, "q1": n - 2}.get(name, 0))
            cols = slice(half * HALF, (half + 1) * HALF)
            terms = [(wh, xh), (wh, xl), (wl, xh)]
            for t, (ws, xs) in enumerate(terms):
                mm = nc.tensor.matmul(misc[:, half, :], ws[p][:, which, :], xs[p][:, cols],
                                      start=t == 0, stop=t == len(terms) - 1)
            mm.then_inc(proj[name], 1)

        def pe_v(pe, n, p, half):
            if exists(n + 1):
                pe.wait_ge(evac[f"k{half}"], n + 2)
            else:
                ge(pe, x_added[half], n - 1)
            if half == 0:
                pe.wait_ge(xt_loaded, n * 16 + 16)
                pe.wait_ge(wv_loaded[p], 16 * (n >> 1) + 16)
            for t in range(TILES // 2):
                tile = half * (TILES // 2) + t
                mm = nc.tensor.matmul(misc[:, half, t * P:(t + 1) * P], xt[:, tile * P:(tile + 1) * P],
                                      wv[p][:], start=True, stop=True)
            mm.then_inc(proj[f"v{half}"], 1)

        def pe_sum(pe, m):
            if exists(m + 1):
                pe.wait_ge(evac["v0"], m + 2)
            else:
                ge(pe, x_added[0], m)
            pe.wait_ge(added, m * ADDS + ADDS)
            for half in range(2):
                for h in range(2):
                    row = 32 * (2 * half + h)
                    mm = nc.tensor.matmul(misc[row:row + 32, 0, :], ones[:, 0:32],
                                          part[:, h, half * HALF:(half + 1) * HALF], start=True, stop=True)
            mm.then_inc(summed, 1)

        def pe_bcast(pe, m, half):
            pe.wait_ge(r_split, m + 1)
            if half == 1:
                if exists(m + 1):
                    pe.wait_ge(evac["v1"], m + 2)
                else:
                    ge(pe, x_added[1], m)
            if isinstance(m, int) and m == 0 and half == 0:
                pe.wait_ge(spread_made, 5)
            for t in range(2):
                mm = nc.tensor.matmul(misc[:, half, :], spread[:, half, :], rhl[:, t, :], start=t == 0, stop=t == 1)
            mm.then_inc(bcast[half], 1)

        def pe_wo(pe, m, p, half):
            if half == 0:
                pe.wait_ge(wo_loaded[p], 16 * (m >> 1) + 16)
            pe.wait_ge(normed[half], m + 1)
            for t in range(TILES // 2):
                tile = half * (TILES // 2) + t
                mm = nc.tensor.matmul(misc[:, half, t * P:(t + 1) * P], ot[:, tile * P:(tile + 1) * P],
                                      wo[p][:], start=True, stop=True)
            mm.then_inc(wo_done[half], 1)

        def pe_step(pe, u, p):
            nxt, prev, before = u + 1, u - 1, u - 2
            for i in range(NCH):
                if exists(u):
                    pe_scores(pe, u, p, i)
                if exists(prev):
                    pe_pv(pe, prev, 1 - p, i)
                if i in QK_JOBS and exists(nxt):
                    pe_qk(pe, nxt, 1 - p, QK_JOBS[i])
                if i in V_JOBS and exists(u):
                    pe_v(pe, u, p, V_JOBS[i])
                if i == 1 and exists(before):
                    pe_wo(pe, before, p, 1)
                if exists(prev):
                    if i == 6:
                        pe_sum(pe, prev)
                    if i in (9, 10):
                        pe_bcast(pe, prev, i - 9)
                    if i == 11:
                        pe_wo(pe, prev, 1 - p, 0)

        def dve_split(dve, n, name):
            which, half = "qk".index(name[0]), int(name[1])
            cols = slice(half * HALF, (half + 1) * HALF)
            dve.wait_ge(high[name], n + 1)
            nc.vector.tensor_tensor(stage[:, which, 1, cols], misc[:, half, :],
                                    stage[:, which, 0, cols].bitcast(F32), ALU.subtract).then_inc(evac[name], 1)

        def dve_adds(dve, m, p, g):
            if g in DIAGONAL_GROUPS:
                dve.wait_ge(masked, m * 2 + DIAGONAL_GROUPS.index(g) + 1)
            else:
                dve.wait_ge(exp_done, m * len(GROUPS) + g + 1)
            steps = []
            if g == 0:
                ge(dve, summed, m)
                steps.append(("copy", slice(0, P), chunk_of(prob[p], 0, (0, P)), None))
                steps.append(("add", slice(P, HALF), chunk_of(prob[p], 0, (P, HALF)), chunk_of(prob[p], 1)))
            elif g == 1:
                steps.append(("add", slice(HALF, SEQ), chunk_of(prob[p], 4), chunk_of(prob[p], 5)))
            for i in range(*GROUPS[g]):
                half, j, width, _ = CHUNKS[i]
                if j >= 2:
                    cols = slice(half * HALF + HALF - width, half * HALF + HALF)
                    steps.append(("acc", cols, part[:, :, cols], chunk_of(prob[p], i)))
            done = {0: 0, 1: 4, 2: 5, 3: 7}[g]
            for s, (kind, cols, a, b) in enumerate(steps):
                if kind == "acc":
                    dve.wait_ge(added, m * ADDS + done + s)
                if kind == "copy":
                    ins = nc.vector.tensor_copy(part[:, :, cols], a)
                else:
                    ins = nc.vector.tensor_tensor(part[:, :, cols], a, b, ALU.add)
                ins.then_inc(added, 1)

        def dve_recip(dve, m):
            dve.wait_ge(summed, m + 1)
            ge(dve, bcast[1], m)
            nc.vector.reciprocal(rsum[:], misc[:, 0, :]).then_inc(recip, 1)

        def dve_r_high(dve, m):
            dve.wait_ge(recip, m + 1)
            nc.vector.tensor_copy(rhl[:, 0, :], rsum[:]).then_inc(r_high, 1)

        def dve_r_low(dve, m):
            dve.wait_ge(r_high, m + 1)
            nc.vector.tensor_tensor(rhl[:, 1, :], rsum[:], rhl[:, 0, :].bitcast(F32), ALU.subtract)\
                .then_inc(r_split, 1)

        def dve_norm(dve, m, half):
            cols = slice(half * HALF, (half + 1) * HALF)
            dve.wait_ge(out_evac[half], m + 1)
            dve.wait_ge(bcast[half], m + 1)
            nc.vector.tensor_tensor(ot[:, cols], misc[:, half, :], ot[:, cols], ALU.mult)\
                .then_inc(normed[half], 1)

        def dve_x_add(dve, m, half):
            dve.wait_ge(wo_done[half], m + 1)
            ge(dve, x_added[half], m)
            at = ((m >> SEQ_BITS) & (BATCH - 1)) * SEQ + half * HALF
            rows = xflat[:, bass.ds(at, HALF)]
            nc.vector.tensor_tensor(rows, rows, misc[:, half, :], ALU.add).then_inc(x_added[half], 1)

        def dve_step(dve, u, p):
            nxt, prev, before = u + 1, u - 1, u - 2
            order = [("x", before, 0), ("norm", before, 1), ("split", nxt, "q0"), ("x", before, 1),
                     ("split", nxt, "k0"), ("split", nxt, "q1"), ("adds", prev, 3), ("split", nxt, "k1"),
                     ("recip", prev, None), ("adds", u, 0), ("r_high", prev, None), ("r_low", prev, None),
                     ("adds", u, 1), ("norm", prev, 0), ("adds", u, 2)]
            for what, m, arg in order:
                if not exists(m):
                    continue
                if what == "norm":
                    dve_norm(dve, m, arg)
                elif what == "split":
                    dve_split(dve, m, arg)
                elif what == "x":
                    dve_x_add(dve, m, arg)
                elif what == "adds":
                    dve_adds(dve, m, p if m is u else 1 - p, arg)
                elif what == "recip":
                    dve_recip(dve, m)
                elif what == "r_high":
                    dve_r_high(dve, m)
                else:
                    dve_r_low(dve, m)

        def steps(eng, step):
            for u in range(-1, 4):
                step(eng, u, u % 2)
            looped = (UNITS - 5) // 2
            with eng.Fori(0, looped) as it:
                for par in range(2):
                    step(eng, it * 2 + (4 + par), par)
            for u in range(4 + 2 * looped, UNITS + 2):
                step(eng, u, u % 2)

        with nc.Block() as block:

            @block.sync
            def _(sp):
                load_unit(sp, 0, 0)
                steps(sp, sp_step)

            @block.gpsimd
            def _(pool):
                split_w(pool, 0, 0)
                steps(pool, pool_step)

            @block.scalar
            def _(act):
                steps(act, act_step)

            @block.tensor
            def _(pe):
                steps(pe, pe_step)

            @block.vector
            def _(dve):
                nc.vector.memset(spread[:].bitcast(F32), 0.0).then_inc(spread_made, 1)
                dve.wait_ge(spread_made, 1)
                for half in range(2):
                    for h in range(2):
                        row = 32 * (2 * half + h)
                        nc.vector.memset(spread[row:row + 1, half, h * DH:(h + 1) * DH].bitcast(F32), 1.0)\
                            .then_inc(spread_made, 1)
                steps(dve, dve_step)


def of(dram, index):
    if isinstance(index, int):
        return dram[index]
    names = "abcde"[:len(dram.shape) - 1]
    rest = " ".join(names[1:])
    return dram[bass.ds(index, 1)].rearrange(f"z {' '.join(names)} -> (z {names[0]}) {rest}")


PAGE = 32
HEADS1, DH1 = 16, 8
QUAD = 4
QUADS = HEADS1 // QUAD
PARTS = 3
V_COLS = 32


def project1(nc, kit, sem, ident, xt_dram, wq_dram, wdown_dram, wk_dram, wv_dram, rope_dram, parts_dram, v_dram):
    with ExitStack() as ctx:
        k = kit.scope(ctx)
        L = wdown_dram.shape[1]
        wq = k.sb("p1_wq", [P, 2, P])
        wd = k.sb("p1_wd", [P, L])
        wk = k.sb("p1_wk", [L, 2, P])
        wv = k.sb("p1_wv", [L, P])
        rope = k.sb("p1_rope", [P, 2, SEQ])
        xt = k.sb("p1_xt", [P, SEQ])
        lat = k.sb("p1_lat", [L, SEQ])
        t_cos, t_sin = k.sb("p1_tcos", [P, SEQ]), k.sb("p1_tsin", [P, SEQ])
        rest = k.sb("p1_rest", [P, SEQ])
        part = [k.sb(f"p1_part{i}", [P, PARTS, SEQ], BF16) for i in range(2)]
        vp = k.sb("p1_v", [P, TILES, HEADS1, V_COLS])
        plain = k.ps("p1_plain", [P, SEQ])
        partner = k.ps("p1_partner", [P, SEQ])
        lat_ps = k.ps("p1_lat_ps", [L, SEQ])
        v_ps = k.ps("p1_v_ps", [P, SEQ])
        w_loaded, x_loaded, v_set = sem("p1_w_loaded"), sem("p1_x_loaded"), sem("p1_v_set")
        lat_done, lat_out, v_done, v_out = (sem(f"p1_{n}") for n in ("lat_done", "lat_out", "v_done", "v_out"))
        plain_done, cos_done, sin_done, rot_done = (sem(f"p1_{n}") for n in ("plain", "cos", "sin", "rot"))
        hi_done, rest_done, mid_done, lo_done = (sem(f"p1_{n}") for n in ("hi", "rest", "mid", "lo"))
        stored, x_free, part_free, v_free = (sem(f"p1_{n}") for n in ("stored", "x_free", "part_free", "v_free"))

        with nc.Block() as block:

            @block.sync
            def _(sp):
                for dst, src in ((wq, wq_dram), (wd, wdown_dram), (wk, wk_dram), (wv, wv_dram), (rope, rope_dram)):
                    sp.dma_start(dst[:], src).then_inc(w_loaded, 16)
                sp.sem_inc(part_free, 1)
                sp.dma_start(xt[:], xt_dram[0, 0]).then_inc(x_loaded, 16)
                with sp.Fori(0, BATCH) as b:
                    for i in range(2):
                        sp.wait_ge(hi_done, b * 2 + i + 1)
                        sp.wait_ge(mid_done, b * 2 + i + 1)
                        kit.ge_apart(sp, lo_done, b * 2 + i + 1)
                        if i == 1:
                            nxt = (b + 1) & (BATCH - 1)
                            sp.dma_start(xt[:], of(xt_dram, nxt)[0]).then_inc(x_loaded, 16)
                        for a in range(PARTS):
                            dst = of(parts_dram, b)[i * PARTS + a]
                            sp.dma_start(dst, part[i][:, a, :]).then_inc(stored, 16)
                    sp.wait_ge(v_out, b + 1)
                    dst = of(v_dram, b)
                    for q in range(QUADS):
                        sp.dma_start(dst[q], vp[:, :, q * QUAD:(q + 1) * QUAD, :]).then_inc(stored, 16)
                    sp.wait_ge(stored, b * (16 * (2 * PARTS + QUADS)) + 16 * (2 * PARTS + QUADS))
                    sp.sem_inc(part_free, 1)
                sp.wait_ge(x_loaded, 16 * (BATCH + 1))

            @block.tensor
            def _(pe):
                pe.wait_ge(w_loaded, 16 * 5)
                with pe.Fori(0, BATCH) as b:
                    pe.wait_ge(x_loaded, b * 16 + 16)
                    for half in range(2):
                        cols = slice(half * HALF, (half + 1) * HALF)
                        mm = nc.tensor.matmul(lat_ps[:, cols], wd[:], xt[:, cols], start=True, stop=True)
                    mm.then_inc(lat_done, 1)
                    for i in range(2):
                        if i == 1:
                            pe.wait_ge(lat_out, b + 1)
                            pe.wait_ge(sin_done, b * 2 + 1)
                        for to, which in ((plain, 0), (partner, 1)):
                            for half in range(2):
                                cols = slice(half * HALF, (half + 1) * HALF)
                                w_, x_ = (wq, xt) if i == 0 else (wk, lat)
                                mm = nc.tensor.matmul(to[:, cols], w_[:, which, :], x_[:, cols],
                                                      start=True, stop=True)
                        mm.then_inc(plain_done, 1)
                    for t in range(TILES):
                        mm = nc.tensor.matmul(v_ps[:, t * P:(t + 1) * P], lat[:, t * P:(t + 1) * P], wv[:],
                                              start=True, stop=True)
                    mm.then_inc(v_done, 1)
                    pe.wait_ge(sin_done, b * 2 + 2)
                    pe.wait_ge(v_out, b + 1)

            @block.scalar
            def _(act):
                act.wait_ge(v_set, 2)
                with act.Fori(0, BATCH) as b:
                    act.wait_ge(lat_done, b + 1)
                    nc.scalar.copy(lat[:], lat_ps[:]).then_inc(lat_out, 1)
                    act.wait_ge(part_free, b + 1)
                    for i in range(2):
                        act.wait_ge(rot_done, b * 2 + i + 1)
                        nc.scalar.copy(part[i][:, 0, :], t_cos[:]).then_inc(hi_done, 1)
                        act.wait_ge(rest_done, b * 2 + i + 1)
                        nc.scalar.copy(part[i][:, 1, :], rest[:]).then_inc(mid_done, 1)
                    act.wait_ge(v_done, b + 1)
                    nc.scalar.copy(vp[:, :, :, 0:DH1], v_ps[:].rearrange("p (t h d) -> p t h d", t=TILES, d=DH1))\
                        .then_inc(v_out, 1)

            @block.vector
            def _(dve):
                nc.vector.memset(vp[:], 0.0).then_inc(v_set, 1)
                dve.wait_ge(v_set, 1)
                nc.vector.memset(vp[:, :, :, DH1:DH1 + 1], 1.0).then_inc(v_set, 1)
                dve.wait_ge(w_loaded, 16 * 5)
                with dve.Fori(0, BATCH) as b:
                    for i in range(2):
                        n = b * 2 + i
                        dve.wait_ge(plain_done, n + 1)
                        if i == 1:
                            dve.wait_ge(lo_done, n)
                            dve.wait_ge(hi_done, n)
                        nc.vector.tensor_tensor(t_cos[:], plain[:], rope[:, 0, :], ALU.mult).then_inc(cos_done, 1)
                        nc.vector.tensor_tensor(t_sin[:], partner[:], rope[:, 1, :], ALU.mult).then_inc(sin_done, 1)
                        dve.wait_ge(cos_done, n + 1)
                        dve.wait_ge(sin_done, n + 1)
                        nc.vector.tensor_tensor(t_cos[:], t_cos[:], t_sin[:], ALU.add).then_inc(rot_done, 1)
                        dve.wait_ge(hi_done, n + 1)
                        nc.vector.tensor_tensor(rest[:], t_cos[:], part[i][:, 0, :], ALU.subtract)\
                            .then_inc(rest_done, 1)
                        dve.wait_ge(mid_done, n + 1)
                        nc.vector.tensor_tensor(part[i][:, 2, :], rest[:], part[i][:, 1, :], ALU.subtract)\
                            .then_inc(lo_done, 1)


def attention1(nc, kit, sem, ident, parts_dram, v_dram, out, scale):
    UNITS = BATCH * QUADS
    ROWS = PARTS * PARTS * DH1
    ROWS_M = ROWS + PARTS
    SLOTS = 2 * NCH
    RING = 6
    PV_LAG = 2
    MAX_SLOTS = 18
    PIECES = [(h, t, c, c * HALF, min(HALF, (t + 1) * P - c * HALF))
              for h in range(QUAD) for t in range(TILES) for c in range(2) if (t + 1) * P > c * HALF]
    BUFS = 3
    BANKS = 3
    with ExitStack() as ctx:
        k = kit.scope(ctx)
        q_st = [k.sb(f"a1_q{i}", [P, QUAD, SEQ], BF16) for i in range(BUFS)]
        k_st = [k.sb(f"a1_k{i}", [P, QUAD, SEQ], BF16) for i in range(BUFS)]
        v_st = [k.sb(f"a1_v{i}", [P, TILES, QUAD, V_COLS]) for i in range(BUFS)]
        prob = [k.sb(f"a1_p{i}", [P, 2, HALF]) for i in range(RING)]
        identb = k.sb("a1_identb", [P, P], BF16)
        page_mask = k.sb("a1_page_mask", [P, P], BF16)
        mx = [k.sb(f"a1_mx{c}", [P, QUAD, TILES]) for c in range(2)]
        neg = k.sb("a1_neg", [QUAD * TILES, P])
        neg_rest = k.sb("a1_neg_rest", [QUAD * TILES, P])
        neg_part = k.sb("a1_neg_part", [QUAD * TILES, PARTS, P], BF16)
        ot = k.sb("a1_ot", [P, 2, HALF])
        rs = k.sb("a1_rs", [P, TILES // 2, QUAD])
        score_ps = k.ps("a1_score", [P, 2, 2, HALF])
        out_ps = k.ps("a1_out", [P, HALF])
        misc = k.ps("a1_misc", [P, BANKS, HALF])

        st_loaded = [sem(f"a1_st_loaded{i}") for i in range(BUFS)]
        masks_made, ones_made, zeros_made = (sem(f"a1_{n}_made") for n in ("masks", "ones", "zeros"))
        ready, free = sem("a1_misc_ready"), sem("a1_misc_free")
        combined, neg_done, hi_done, rest_done, mid_done, lo_done = \
            (sem(f"a1_{n}") for n in ("combined", "neg", "neg_hi", "neg_rest", "neg_mid", "neg_lo"))
        m_stacked = sem("a1_m_stacked")
        scored, exp_done, masked = (sem(f"a1_{n}") for n in ("scored", "exp", "masked"))
        pv_chunks = sem("a1_pv_chunks")
        HALF_END = [1 + max(i for i, c in enumerate(CHUNKS) if c[0] == half) for half in range(2)]
        out_evac = [sem(f"a1_out_evac{i}") for i in range(2)]
        rs_done = sem("a1_rs")
        ST_DMAS = 2 * PARTS * PARTS + 1
        DIAG = [i for i, (half, j, _, _) in enumerate(CHUNKS) if j // (TILES // 2) == half]

        def exists(u):
            return not isinstance(u, int) or 0 <= u < UNITS

        def uses(u):
            by_slot = {s: [] for s in range(SLOTS)}
            if exists(u + 1):
                for n, piece in enumerate(PIECES):
                    by_slot[n * MAX_SLOTS // len(PIECES)].append(("max", piece, n == len(PIECES) - 1))
                by_slot[MAX_SLOTS + 2].append(("turn_max", None, None))
            if exists(u - 1):
                by_slot[6].append(("turn_out", 1, None))
            if exists(u):
                by_slot[14].append(("turn_out", 0, None))
            n = sum(map(len, by_slot.values()))
            return by_slot, n

        FULL = len(PIECES) + 3

        def bank_of(u, at):
            short = FULL - uses(u)[1] if isinstance(u, int) and u < 1 else 0
            return (at + short) % BANKS

        def before(u):
            if isinstance(u, int):
                return sum(uses(s)[1] for s in range(-1, u))
            return before(1) + (u - 1) * FULL

        def wait_prob(eng, m, i, hp):
            if i in DIAG:
                eng.wait_ge(masked, m * (2 * len(DIAG)) + 2 * DIAG.index(i) + hp + 1)
            else:
                eng.wait_ge(exp_done, m * SLOTS + 2 * i + hp + 1)

        def load_unit(sp, n, b3, d3):
            if not exists(n):
                return
            kit.ge_apart(sp, pv_chunks, (n - BUFS + 1) * NCH)
            batch, quad = (n >> 2) & (BATCH - 1), n & (QUADS - 1)
            src = of(parts_dram, batch)
            for which, st in ((0, q_st), (1, k_st)):
                for a in range(PARTS):
                    row0 = a * (PARTS * DH1)
                    for b in range(PARTS):
                        part = a if which == 0 else b
                        rows = src[which * PARTS + part].rearrange("(g h d) t -> g d h t", g=QUADS, h=QUAD)
                        sp.dma_start(st[b3][row0 + b * DH1:row0 + (b + 1) * DH1, :, :], of(rows, quad))\
                            .then_inc(st_loaded[b3], 16)
            sp.dma_start(v_st[b3][:], of(of(v_dram, batch), quad)).then_inc(st_loaded[b3], 16)

        def sp_step(sp, u, b3, d3):
            load_unit(sp, u + 2, (b3 + 2) % BUFS, d3(2))
            n, bn = u + 1, (b3 + 1) % BUFS
            if exists(n):
                for a, done in enumerate((hi_done, mid_done, lo_done)):
                    sp.wait_ge(done, n + 1)
                    row = q_st[bn][ROWS + a:ROWS + a + 1, :, :].rearrange("o h (t c) -> o (h t) c", c=P)
                    sp.dma_start(row, neg_part[:, a, :]).then_inc(m_stacked, 16)

        def pool_step(pool, u, b3, d3):
            if not exists(u):
                return
            for i in DIAG:
                for hp in range(2):
                    slot = 2 * i + hp
                    kit.ge_apart(pool, exp_done, u * SLOTS + slot + 1)
                    blk = prob[slot % RING][:, :, 0:P].rearrange("p h (g q) -> p h g q", q=PAGE)
                    nc.gpsimd.affine_select(out=blk, in_=blk, compare_op=ALU.is_ge, fill=0.0, base=PAGE - 1,
                                            pattern=[[0, 2], [PAGE, P // PAGE], [0, PAGE]], channel_multiplier=-1)\
                        .then_inc(masked, 1)

        def act_out(act, m, half):
            if not exists(m):
                return
            act.wait_ge(pv_chunks, m * NCH + HALF_END[half])
            ge(act, rs_done, m * 2 + half)
            nc.scalar.copy(ot[:, half, :], out_ps[:]).then_inc(out_evac[half], 1)

        def act_step(act, u, b3, d3):
            for s in range(SLOTS):
                i = s // 2
                if exists(u):
                    width = CHUNKS[i][2]
                    ge(act, pv_chunks, u * NCH + (s // 2 - RING // 2 + 1))
                    act.wait_ge(scored, u * SLOTS + s + 1)
                    nc.scalar.activation(prob[s % RING][:, :, 0:width], score_ps[:, s % 2, :, 0:width], ACT.Exp,
                                         scale=scale).then_inc(exp_done, 1)
                if s == 2:
                    act_out(act, u - 1, 1)
                if s == 10:
                    act_out(act, u, 0)

        def pe_scores(pe, u, b3, s, h2):
            i, hp = s // 2, s % 2
            half, j, width, _ = CHUNKS[i]
            q0 = half * HALF + HALF - width
            if s == 0 and h2 == 0:
                pe.wait_ge(m_stacked, u * (16 * PARTS) + 16 * PARTS)
            if h2 == 0:
                ge(pe, exp_done, u * SLOTS + s - 1)
            h = 2 * hp + h2
            mm = nc.tensor.matmul(score_ps[:, s % 2, h2, 0:width], k_st[b3][:, h, j * P:(j + 1) * P],
                                  q_st[b3][:, h, q0:q0 + width], start=True, stop=True)
            if h2 == 1:
                mm.then_inc(scored, 1)

        def pe_pv(pe, m, b3, i):
            half, j, width, _ = CHUNKS[i]
            wait_prob(pe, m, i, 0)
            wait_prob(pe, m, i, 1)
            if j == 0:
                ge(pe, out_evac[1 - half], m + half)
            last_j = max(c[1] for c in CHUNKS if c[0] == half)
            for h in range(QUAD):
                slot = (2 * i + h // 2) % RING
                mm = nc.tensor.matmul(out_ps[h * V_COLS:(h + 1) * V_COLS, HALF - width:HALF],
                                      v_st[b3][:, j, h, :], prob[slot][:, h % 2, 0:width],
                                      start=j == 0, stop=j == last_j)
            mm.then_inc(pv_chunks, 1)

        def pe_use(pe, u, b3, kind, arg, number, at):
            bank = bank_of(u, at)
            ge(pe, free, number if isinstance(u, int) and at < BANKS else number - (BANKS - 1))
            if kind == "max":
                h, t, c, key0, keys = arg
                bn = (b3 + 1) % BUFS
                diagonal = key0 + keys == (t + 1) * P
                mm = nc.tensor.matmul(misc[:, bank, 0:keys], q_st[bn][0:ROWS, h, t * P:(t + 1) * P],
                                      k_st[bn][0:ROWS, h, key0:key0 + keys], start=True, stop=not diagonal)
                if diagonal:
                    mm = nc.tensor.matmul(misc[:, bank, keys - P:keys], identb[:], page_mask[:],
                                          start=False, stop=True)
            elif kind == "turn_max":
                pe.wait_ge(combined, u + 2)
                mm = nc.tensor.transpose(misc[0:QUAD * TILES, bank, 0:P], mx[0][:].rearrange("p h t -> p (h t)"),
                                         ident[:])
            else:
                m = u if arg == 0 else u - 1
                pe.wait_ge(out_evac[arg], m + 1)
                for t in range(TILES // 2):
                    mm = nc.tensor.transpose(misc[:, bank, t * P:(t + 1) * P], ot[:, arg, t * P:(t + 1) * P], ident[:])
            mm.then_inc(ready, 1)

        def numbered(u):
            by_slot, _ = uses(u)
            first = before(u)
            at = 0
            result = {}
            for s in range(SLOTS):
                result[s] = []
                for kind, arg, last in by_slot[s]:
                    result[s].append((kind, arg, last, first + at, at))
                    at += 1
            return result

        def pe_step(pe, u, b3, d3):
            numb = numbered(u)
            if isinstance(u, int) and u == -1:
                pe.wait_ge(masks_made, 2 + P // PAGE - 1)
            if exists(u + 1):
                pe.wait_ge(st_loaded[(b3 + 1) % BUFS], d3(1) * (16 * ST_DMAS) + 16 * ST_DMAS)
            for s in range(SLOTS):
                todo = numb[s][:]
                for h2 in range(2):
                    if todo:
                        kind, arg, last, number, at = todo.pop(0)
                        pe_use(pe, u, b3, kind, arg, number, at)
                    if exists(u):
                        pe_scores(pe, u, b3, s, h2)
                if s % 2 == 0:
                    i = s // 2 - PV_LAG
                    m, c, bm = (u, i, b3) if i >= 0 else (u - 1, NCH + i, (b3 - 1) % BUFS)
                    if exists(m):
                        pe_pv(pe, m, bm, c)
                for kind, arg, last, number, at in todo:
                    pe_use(pe, u, b3, kind, arg, number, at)

        def dve_use(dve, u, b3, kind, arg, last, number, at):
            bank = bank_of(u, at)
            dve.wait_ge(ready, number + 1)
            n = u + 1
            if kind == "max":
                h, t, c, key0, keys = arg
                nc.vector.tensor_reduce(mx[c][:, h, t:t + 1], misc[:, bank, 0:keys], AX_X, ALU.max).then_inc(free, 1)
                if last:
                    dve.wait_ge(free, number + 1)
                    upper = slice(TILES // 2, TILES)
                    nc.vector.tensor_tensor(mx[0][:, :, upper], mx[0][:, :, upper], mx[1][:, :, upper], ALU.max)\
                        .then_inc(combined, 1)
            elif kind == "turn_max":
                ge(dve, m_stacked, n * (16 * PARTS))
                nc.vector.tensor_scalar(neg[:], misc[0:QUAD * TILES, bank, 0:P], -1.0, None, ALU.mult)\
                    .then_inc(free, 1)
                dve.wait_ge(free, number + 1)
                nc.vector.tensor_copy(neg_part[:, 0, :], neg[:]).then_inc(hi_done, 1)
                dve.wait_ge(hi_done, n + 1)
                nc.vector.tensor_tensor(neg_rest[:], neg[:], neg_part[:, 0, :], ALU.subtract).then_inc(rest_done, 1)
                dve.wait_ge(rest_done, n + 1)
                nc.vector.tensor_copy(neg_part[:, 1, :], neg_rest[:]).then_inc(mid_done, 1)
                dve.wait_ge(mid_done, n + 1)
                nc.vector.tensor_tensor(neg_part[:, 2, :], neg_rest[:], neg_part[:, 1, :], ALU.subtract)\
                    .then_inc(lo_done, 1)
            else:
                m = u if arg == 0 else u - 1
                order = m * 2 + arg
                turned = misc[:, bank, :].rearrange("p (t h c) -> p t h c", t=TILES // 2, h=QUAD)
                ge(dve, free, number)
                nc.vector.reciprocal(rs[:], turned[:, :, :, DH1]).then_inc(rs_done, 1)
                dve.wait_ge(rs_done, order + 2)
                col0 = (m & (QUADS - 1)) * (QUAD * DH1)
                to = out[:].rearrange("p t c -> p (t c)")
                for t in range(TILES // 2):
                    rows = to[:, bass.ds(((m >> 2) & (BATCH - 1)) * SEQ + (arg * (TILES // 2) + t) * P + col0, QUAD * DH1)]
                    ins = nc.vector.tensor_tensor(rows.rearrange("p (h d) -> p h d", d=DH1), turned[:, t, :, 0:DH1],
                                                  rs[:, t, :].unsqueeze(2).to_broadcast([P, QUAD, DH1]), ALU.mult)
                ins.then_inc(free, 1)

        def dve_step(dve, u, b3, d3):
            numb = numbered(u)
            for s in range(SLOTS):
                for kind, arg, last, number, at in numb[s]:
                    dve_use(dve, u, b3, kind, arg, last, number, at)

        def steps(eng, step):
            def plain(u):
                step(eng, u, u % BUFS, lambda k: (u + k) // BUFS)
            for u in (-1, 0):
                plain(u)
            looped = (UNITS - BUFS) // BUFS
            with eng.Fori(0, looped) as it:
                for i in range(BUFS):
                    step(eng, it * BUFS + (1 + i), (1 + i) % BUFS, lambda k, i=i: it + (1 + i + k) // BUFS)
            for u in range(1 + looped * BUFS, UNITS + 1):
                plain(u)

        with nc.Block() as block:

            @block.sync
            def _(sp):
                sp.wait_ge(ones_made, 2 * BUFS)
                load_unit(sp, 0, 0, None)
                steps(sp, sp_step)

            @block.gpsimd
            def _(pool):
                steps(pool, pool_step)

            @block.scalar
            def _(act):
                steps(act, act_step)

            @block.tensor
            def _(pe):
                steps(pe, pe_step)

            @block.vector
            def _(dve):
                for st in k_st:
                    nc.vector.memset(st[64:P, :, :].bitcast(F32), 0.0).then_inc(zeros_made, 1)
                for st in q_st:
                    nc.vector.memset(st[64:P, :, :].bitcast(F32), 0.0).then_inc(ones_made, 1)
                dve.wait_ge(zeros_made, BUFS)
                for st in k_st:
                    nc.vector.memset(st[64:96, :, :], 1.0).then_inc(ones_made, 1)
                nc.vector.tensor_copy(identb[:], ident[:]).then_inc(masks_made, 1)
                nc.vector.memset(page_mask[:], 0.0).then_inc(masks_made, 1)
                dve.wait_ge(masks_made, 2)
                for g in range(P // PAGE - 1):
                    nc.vector.memset(page_mask[g * PAGE:(g + 1) * PAGE, (g + 1) * PAGE:], NEGATIVE)\
                        .then_inc(masks_made, 1)
                dve.sem_inc(rs_done, 1)
                steps(dve, dve_step)


NEGATIVE = -3e38


def project_out1(nc, kit, sem, ident, x, heads, wo_dram):
    with ExitStack() as ctx:
        k = kit.scope(ctx)
        wo = k.sb("po_wo", [P, D])
        turned = k.sb("po_turned", [P, SEQ])
        turned_ps = k.ps("po_turned_ps", [P, SEQ])
        y_ps = k.ps("po_y", [P, SEQ])
        w_loaded, turn_done, turn_out, y_done, added = (sem(f"po_{n}") for n in ("w", "turn", "turn_out", "y", "added"))
        staged = sem("po_staged")
        hflat = heads[:].rearrange("p t c -> p (t c)")
        xflat = x[:].rearrange("p t d -> p (t d)")
        here = k.sb("po_here", [P, SEQ])

        with nc.Block() as block:

            @block.sync
            def _(sp):
                sp.dma_start(wo[:], wo_dram).then_inc(w_loaded, 16)

            @block.tensor
            def _(pe):
                pe.wait_ge(w_loaded, 16)
                with pe.Fori(0, BATCH) as b:
                    pe.wait_ge(staged, b + 1)
                    for t in range(TILES):
                        mm = nc.tensor.transpose(turned_ps[:, t * P:(t + 1) * P], here[:, t * P:(t + 1) * P], ident[:])
                    mm.then_inc(turn_done, 1)
                    pe.wait_ge(turn_out, b + 1)
                    for t in range(TILES):
                        mm = nc.tensor.matmul(y_ps[:, t * P:(t + 1) * P], turned[:, t * P:(t + 1) * P], wo[:],
                                              start=True, stop=True)
                    mm.then_inc(y_done, 1)

            @block.scalar
            def _(act):
                with act.Fori(0, BATCH) as b:
                    act.wait_ge(turn_done, b + 1)
                    nc.scalar.copy(turned[:], turned_ps[:]).then_inc(turn_out, 1)

            @block.vector
            def _(dve):
                nc.vector.tensor_copy(here[:], hflat[:, 0:SEQ]).then_inc(staged, 1)
                with dve.Fori(0, BATCH) as b:
                    dve.wait_ge(y_done, b + 1)
                    rows = xflat[:, bass.ds(b * SEQ, SEQ)]
                    nc.vector.tensor_tensor(rows, rows, y_ps[:], ALU.add).then_inc(added, 1)
                    nxt = (b + 1) & (BATCH - 1)
                    nc.vector.tensor_copy(here[:], hflat[:, bass.ds(nxt * SEQ, SEQ)]).then_inc(staged, 1)


def norm_and_gate(nc, kit, sem, tag, x, ident, eps, gate_dram, bias_dram, xn_all, xt_all, logits):
    E = gate_dram.shape[1]
    with ExitStack() as ctx:
        k = kit.scope(ctx)
        gate = k.sb(f"{tag}_gate", [P, E])
        biases = 0 if bias_dram is None else bias_dram.shape[1]
        bias = k.sb(f"{tag}_bias", [P, max(biases, 1), E])
        stats = k.sb(f"{tag}_stats", [P, TILES, 6])
        mv = k.sb(f"{tag}_mv", [P, TILES, 2])
        std = k.sb(f"{tag}_std", [P, TILES])
        rstd = k.sb(f"{tag}_rstd", [P, TILES])
        xn = k.sb(f"{tag}_xn", [P, TILES, D])
        xt = k.sb(f"{tag}_xt", [P, SEQ])
        turned = k.ps(f"{tag}_turned", [P, SEQ])
        gate_ps = k.ps(f"{tag}_gate_ps", [P, TILES, E])
        loaded, stats_done, mv_done = sem(f"{tag}_loaded"), sem(f"{tag}_stats"), sem(f"{tag}_mv")
        std_done, rstd_done = sem(f"{tag}_std"), sem(f"{tag}_rstd")
        xn_done, turn_done = sem(f"{tag}_xn"), sem(f"{tag}_turn")
        xt_done, kept, gated, biased = sem(f"{tag}_xt"), sem(f"{tag}_kept"), sem(f"{tag}_gated"), sem(f"{tag}_biased")
        xflat = x[:].rearrange("p t d -> p (t d)")
        xn_flat = xn_all[:].rearrange("p t d -> p (t d)")
        keeps = 1 + (xt_all is not None)
        lflat = logits[:].rearrange("p t e -> p (t e)")

        def dve_logits(dve, b):
            dve.wait_ge(gated, b + 1)
            rows = lflat[:, bass.ds(b * (TILES * E), TILES * E)].rearrange("p (t e) -> p t e", e=E)
            if biases == 0:
                nc.vector.tensor_copy(rows, gate_ps[:]).then_inc(biased, 1)
            for i in range(biases):
                if i > 0:
                    dve.wait_ge(biased, b * biases + i)
                nc.vector.tensor_tensor(rows, gate_ps[:] if i == 0 else rows,
                                        bias[:, i:i + 1, :].to_broadcast([P, TILES, E]), ALU.add).then_inc(biased, 1)

        with nc.Block() as block:

            @block.sync
            def _(sp):
                sp.dma_start(gate[:], gate_dram).then_inc(loaded, 16)
                if biases:
                    sp.dma_start(bias[:], bias_dram).then_inc(loaded, 16)

            @block.vector
            def _(dve):
                dve.wait_ge(loaded, 16 * (1 + (biases > 0)))
                with dve.Fori(0, BATCH) as b:
                    for t in range(TILES):
                        last = nc.vector.bn_stats(stats[:, t, :], xflat[:, bass.ds(b * (TILES * D) + t * D, D)])
                    last.then_inc(stats_done, 1)
                    kit.ge_apart(dve, stats_done, b + 1)
                    for t in range(TILES):
                        last = nc.vector.bn_aggr(mv[:, t, :], stats[:, t, :])
                    last.then_inc(mv_done, 1)
                    dve.wait_ge(std_done, b + 1)
                    nc.vector.reciprocal(rstd[:], std[:]).then_inc(rstd_done, 1)
                    dve.wait_ge(rstd_done, b + 1)
                    for t in range(TILES):
                        last = nc.vector.tensor_scalar(xn[:, t, :], xflat[:, bass.ds(b * (TILES * D) + t * D, D)],
                                                       mv[:, t, 0:1], rstd[:, t:t + 1], ALU.subtract, ALU.mult)
                    last.then_inc(xn_done, 1)
                    dve.wait_ge(turn_done, b + 1)
                    dve.wait_ge(kept, b * keeps + keeps)
                    dve_logits(dve, b)

            @block.scalar
            def _(act):
                with act.Fori(0, BATCH) as b:
                    act.wait_ge(mv_done, b + 1)
                    nc.scalar.activation(std[:], mv[:, :, 1], ACT.Sqrt, bias=eps[:, 0:1]).then_inc(std_done, 1)
                    act.wait_ge(turn_done, b + 1)
                    nc.scalar.copy(xt[:], turned[:]).then_inc(xt_done, 1)
                    nc.scalar.copy(xn_flat[:, bass.ds(b * SEQ, SEQ)], xn[:].rearrange("p t d -> p (t d)"))\
                        .then_inc(kept, 1)
                    if xt_all is not None:
                        nc.scalar.copy(xt_all[:, bass.ds(b * SEQ, SEQ)], turned[:]).then_inc(kept, 1)

            @block.tensor
            def _(pe):
                pe.wait_ge(loaded, 16 * (1 + (biases > 0)))
                with pe.Fori(0, BATCH) as b:
                    pe.wait_ge(xn_done, b + 1)
                    for t in range(TILES):
                        last = nc.tensor.transpose(turned[:, t * P:(t + 1) * P], xn[:, t, :], ident[:])
                    last.then_inc(turn_done, 1)
                    pe.wait_ge(xt_done, b + 1)
                    for t in range(TILES):
                        last = nc.tensor.matmul(gate_ps[:, t, :], xt[:, t * P:(t + 1) * P], gate[:],
                                                start=True, stop=True)
                    last.then_inc(gated, 1)
                    pe.wait_ge(kept, b * keeps + keeps)


def route(nc, kit, sem, tag, logits, choices, starts_dram, rows_of, weights, tile_expert):
    E = logits.shape[2]
    ENTRIES = choices * ALL_TILES
    SLOT_TILES = tile_expert.shape[1]
    FAR = -3e38
    with ExitStack() as ctx:
        k = kit.scope(ctx)
        shape, wide_shape = [P, ALL_TILES, E], [P, ENTRIES, E]
        m = [k.sb(f"{tag}_m{i}", [P, ALL_TILES]) for i in range(2)]
        at_max = k.sb(f"{tag}_at_max", shape)
        first = k.sb(f"{tag}_first", [P, ALL_TILES])
        number = k.sb(f"{tag}_number", [P, 1, E])
        one = k.sb(f"{tag}_one", wide_shape)
        left = k.sb(f"{tag}_left", shape)
        ex = k.sb(f"{tag}_ex", shape)
        below = k.sb(f"{tag}_below", [P, P])
        full = k.sb(f"{tag}_full", [P, P])
        scan = [k.sb(f"{tag}_scan{i}", wide_shape) for i in range(2)]
        place = k.sb(f"{tag}_place", wide_shape)
        row = k.sb(f"{tag}_row", [P, ENTRIES])
        count_int = k.sb(f"{tag}_count_int", [P, E], I32)
        padded = k.sb(f"{tag}_padded", [P, 1, E])
        ends = [k.sb(f"{tag}_ends{i}", [P, 1, E]) for i in range(2)]
        starts = k.sb(f"{tag}_starts", [1, SLOT_TILES, E])
        passed = k.sb(f"{tag}_passed", [1, SLOT_TILES, E])
        tile_number = k.sb(f"{tag}_tile_number", [1, SLOT_TILES])
        rank_ps = k.ps(f"{tag}_rank", wide_shape)
        total_ps = k.ps(f"{tag}_total_ps", wide_shape)
        step, exp_done, exp_in, made = (sem(f"{tag}_{n}") for n in ("step", "exp", "exp_in", "made"))
        loaded, chosen, counted = sem(f"{tag}_starts_loaded"), sem(f"{tag}_chosen"), sem(f"{tag}_counted")

        with nc.Block() as block:

            @block.sync
            def _(sp):
                sp.dma_start(starts[:], starts_dram).then_inc(loaded, 16)

            @block.gpsimd
            def _(pool):
                nc.gpsimd.memset(full[:], 1.0).then_inc(made, 1)
                pool.wait_ge(made, 1)
                nc.gpsimd.affine_select(out=below[:], in_=full[:], compare_op=ALU.is_gt, fill=0.0, base=0,
                                        pattern=[[1, P]], channel_multiplier=-1).then_inc(made, 1)

            @block.tensor
            def _(pe):
                pe.wait_ge(made, 2)
                pe.wait_ge(chosen, 1)
                nc.tensor.matmul(total_ps[:], full[:], one[:], start=True, stop=True).then_inc(counted, 1)
                nc.tensor.matmul(rank_ps[:], below[:], one[:], start=True, stop=True).then_inc(counted, 1)

            @block.vector
            def _(dve):
                done = 0

                def in_turn(ins):
                    nonlocal done
                    ins.then_inc(step, 1)
                    done += 1
                    dve.wait_ge(step, done)

                V = nc.vector
                for e in range(E):
                    V.memset(number[:, :, e:e + 1], float(e - E)).then_inc(step, 1)
                done = E
                dve.wait_ge(step, done)
                of_choice = [one[:, c * ALL_TILES:(c + 1) * ALL_TILES, :] for c in range(choices)]

                def wide(a, shape=shape):
                    return a.unsqueeze(2).to_broadcast(shape)

                for c in range(choices):
                    src = logits if c == 0 else left
                    in_turn(V.tensor_reduce(m[c][:], src[:], AX_X, ALU.max))
                    in_turn(V.tensor_tensor(at_max[:], src[:], wide(m[c][:]), ALU.is_ge))
                    in_turn(V.tensor_tensor(at_max[:], at_max[:], number[:].to_broadcast(shape), ALU.mult))
                    in_turn(V.tensor_reduce(first[:], at_max[:], AX_X, ALU.min))
                    in_turn(V.tensor_tensor(of_choice[c], number[:].to_broadcast(shape), wide(first[:]), ALU.is_equal))
                    if c + 1 < choices:
                        in_turn(V.scalar_tensor_tensor(left[:], of_choice[c], FAR, logits[:], ALU.mult, ALU.add))
                dve.sem_inc(chosen, 1)
                if choices == 2:
                    in_turn(V.tensor_tensor(left[:], logits[:], wide(m[0][:]), ALU.subtract))
                    in_turn(V.tensor_tensor(first[:], m[1][:], m[0][:], ALU.subtract))
                    dve.sem_inc(exp_in, 1)

                dve.wait_ge(counted, 1)
                in_turn(V.tensor_copy(scan[0][:], total_ps[:]))
                now, gap = 0, 1
                while gap < ENTRIES:
                    a, b = scan[now], scan[1 - now]
                    V.tensor_copy(b[:, 0:gap, :], a[:, 0:gap, :]).then_inc(step, 1)
                    V.tensor_tensor(b[:, gap:, :], a[:, gap:, :], a[:, 0:ENTRIES - gap, :], ALU.add).then_inc(step, 1)
                    done += 2
                    dve.wait_ge(step, done)
                    now, gap = 1 - now, gap * 2
                inclusive, exclusive = scan[now], scan[1 - now]
                in_turn(V.tensor_tensor(exclusive[:], inclusive[:], total_ps[:], ALU.subtract))
                in_turn(V.tensor_scalar(padded[:], inclusive[:, ENTRIES - 1:, :], float(P - 1), None, ALU.add))
                in_turn(V.tensor_copy(count_int[:], padded[:, 0, :]))
                in_turn(V.tensor_scalar(count_int[:], count_int[:], -P, None, ALU.bitwise_and))
                in_turn(V.tensor_copy(padded[:, 0, :], count_int[:]))
                in_turn(V.tensor_copy(ends[0][:], padded[:]))
                now, gap = 0, 1
                while gap < E:
                    a, b = ends[now], ends[1 - now]
                    V.tensor_copy(b[:, :, 0:gap], a[:, :, 0:gap]).then_inc(step, 1)
                    V.tensor_tensor(b[:, :, gap:], a[:, :, gap:], a[:, :, 0:E - gap], ALU.add).then_inc(step, 1)
                    done += 2
                    dve.wait_ge(step, done)
                    now, gap = 1 - now, gap * 2
                end, base = ends[now], ends[1 - now]
                in_turn(V.tensor_tensor(base[:], end[:], padded[:], ALU.subtract))
                dve.wait_ge(counted, 2)
                in_turn(V.tensor_tensor(place[:], exclusive[:], rank_ps[:], ALU.add))
                in_turn(V.tensor_tensor(place[:], place[:], base[:].to_broadcast(wide_shape), ALU.add))
                in_turn(V.tensor_tensor(place[:], place[:], one[:], ALU.mult))
                in_turn(V.tensor_reduce(row[:], place[:], AX_X, ALU.add))
                in_turn(V.tensor_copy(rows_of[:], row[:]))
                dve.wait_ge(loaded, 16)
                in_turn(V.tensor_tensor(passed[:], starts[:], end[0:1].to_broadcast([1, SLOT_TILES, E]), ALU.is_ge))
                in_turn(V.tensor_reduce(tile_number[:], passed[:], AX_X, ALU.add))
                in_turn(V.tensor_scalar(tile_number[:], tile_number[:], float(E - 1), None, ALU.min))
                in_turn(V.tensor_copy(tile_expert[:], tile_number[:]))
                if choices == 2:
                    dve.wait_ge(exp_done, 2)
                    in_turn(V.tensor_reduce(m[0][:], ex[:], AX_X, ALU.add))
                    in_turn(V.reciprocal(weights[:, 0:ALL_TILES], m[0][:]))
                    in_turn(V.tensor_tensor(weights[:, ALL_TILES:], first[:], weights[:, 0:ALL_TILES], ALU.mult))

            @block.scalar
            def _(act):
                if choices == 2:
                    act.wait_ge(exp_in, 1)
                    nc.scalar.activation(ex[:], left[:], ACT.Exp).then_inc(exp_done, 1)
                    nc.scalar.activation(first[:], first[:], ACT.Exp).then_inc(exp_done, 1)


def scatter_rows(nc, pool, xn_all, rows_of, buffer_dram, scattered):
    for n in range(rows_of.shape[1]):
        nc.gpsimd.indirect_dma_start(
            out=buffer_dram, out_offset=bass.IndirectOffsetOnAxis(ap=rows_of[:, n:n + 1], axis=0),
            in_=xn_all[:, n % ALL_TILES, :], in_offset=None).then_inc(scattered, 16)
    pool.wait_ge(scattered, 16 * rows_of.shape[1])


def expert_tiles(nc, kit, sem, tag, ident, tile_expert, wa_dram, wb_dram, NC, gated, biased, x_rows, y_rows):
    E, A = wa_dram.shape[1:]
    B = wb_dram.shape[2]
    N = tile_expert.shape[1]
    HID = NC * P
    with ExitStack() as ctx:
        k = kit.scope(ctx)
        wa_all = k.sb(f"{tag}_wa_all", [P, E, A])
        wb_all = k.sb(f"{tag}_wb_all", [P, E, B])
        wa = [k.sb(f"{tag}_wa{i}", [P, A]) for i in range(2)]
        wb = [k.sb(f"{tag}_wb{i}", [P, B]) for i in range(2)]
        xs = [k.sb(f"{tag}_xs{i}", [P, D]) for i in range(2)]
        xst = [k.sb(f"{tag}_xst{i}", [P, P]) for i in range(2)]
        silu = [k.sb(f"{tag}_silu{i}", [P, HID]) for i in range(2)] if gated else None
        ht = [k.sb(f"{tag}_ht{i}", [P, HID]) for i in range(2)]
        ys = [k.sb(f"{tag}_ys{i}", [P, D]) for i in range(2)]
        turned = [k.ps(f"{tag}_turned{i}", [P, HALF]) for i in range(2)]
        y_ps = [k.ps(f"{tag}_y{i}", [P, HALF]) for i in range(2)]
        h_ps = [k.ps(f"{tag}_h{i}", [P, HALF]) for i in range(2)]
        g_ps = [k.ps(f"{tag}_g{i}", [P, HALF]) for i in range(2)] if gated else None
        w_loaded = sem(f"{tag}_w_loaded")
        x_loaded = [sem(f"{tag}_x_loaded{i}") for i in range(2)]
        stored = [sem(f"{tag}_stored{i}") for i in range(2)]
        turn_done, xst_done, wa_done, wb_done, h_done, silu_done, ht_done, y_done, y_out = \
            (sem(f"{tag}_{n}") for n in ("turn", "xst", "wa", "wb", "h", "silu", "ht", "y", "y_out"))
        wa_flat = wa_all[:].rearrange("p e c -> p (e c)")
        wb_flat = wb_all[:].rearrange("p e c -> p (e c)")
        experts_flat = tile_expert[:]

        def exists(u):
            return not isinstance(u, int) or 0 <= u < N

        def load(sp, n, p):
            if exists(n):
                kit.ge_apart(sp, turn_done, n - 1)
                sp.dma_start(xs[p][:], of(x_rows, n)).then_inc(x_loaded[p], 16)

        def sp_step(sp, u, p):
            load(sp, u + 2, p)
            if exists(u - 1):
                m, pm = u - 1, 1 - p
                kit.ge_apart(sp, y_out, m + 1)
                sp.dma_start(of(y_rows, m), ys[pm][:]).then_inc(stored[pm], 16)

        def pe_step(pe, u, p):
            if exists(u):
                pe.wait_ge(xst_done, u + 1)
                pe.wait_ge(wa_done, u + 1)
                ge(pe, ht_done, u - 1)
                for c in range(NC):
                    mm = nc.tensor.matmul(h_ps[p][:, c * P:(c + 1) * P], wa[p][:, c * P:(c + 1) * P], xst[p][:],
                                          start=True, stop=True)
                if gated:
                    for c in range(NC):
                        mm = nc.tensor.matmul(g_ps[p][:, c * P:(c + 1) * P], wa[p][:, HID + c * P:HID + (c + 1) * P],
                                              xst[p][:], start=True, stop=True)
                mm.then_inc(h_done, 1)
            n, pn = u + 1, 1 - p
            if exists(n):
                pe.wait_ge(x_loaded[pn], ((n >> 1) << 4) + 16)
                ge(pe, xst_done, n - 1)
                nc.tensor.transpose(turned[pn][:, 0:P], xs[pn][:], ident[:]).then_inc(turn_done, 1)
            m, pm = u - 1, 1 - p
            if exists(m):
                pe.wait_ge(ht_done, m + 1)
                pe.wait_ge(wb_done, m + 1)
                ge(pe, y_out, m - 1)
                for c in range(NC):
                    mm = nc.tensor.matmul(y_ps[pm][:, 0:D], ht[pm][:, c * P:(c + 1) * P],
                                          wb[pm][:, c * P:(c + 1) * P], start=c == 0, stop=c == NC - 1)
                mm.then_inc(y_done, 1)

        def y_evac(eng, m, pm):
            eng.wait_ge(y_done, m + 1)
            if exists(m - 2):
                ge(eng, stored[pm], (m >> 1) << 4)
            y = y_ps[pm][:, 0:D]
            if biased:
                nc.vector.tensor_tensor(ys[pm][:], y, wb[pm][:, HID:HID + D], ALU.add).then_inc(y_out, 1)
            else:
                nc.scalar.copy(ys[pm][:], y).then_inc(y_out, 1)

        def act_step(act, u, p):
            if exists(u):
                act.wait_ge(h_done, u + 1)
                ge(act, y_done, u - 1)
                if gated:
                    nc.scalar.activation(silu[p][:], h_ps[p][:, 0:HID], ACT.Silu).then_inc(silu_done, 1)
                else:
                    for c in range(NC):
                        last = nc.scalar.activation(ht[p][:, c * P:(c + 1) * P], h_ps[p][:, c * P:(c + 1) * P],
                                                    ACT.Relu, bias=wa[p][:, HID + c:HID + c + 1])
                    last.then_inc(ht_done, 1)
            n, pn = u + 1, 1 - p
            if exists(n):
                act.wait_ge(turn_done, n + 1)
                ge(act, h_done, n - 1)
                nc.scalar.copy(xst[pn][:], turned[pn][:, 0:P]).then_inc(xst_done, 1)
            if exists(u - 1) and not biased:
                y_evac(act, u - 1, 1 - p)

        def dve_step(dve, u, p):
            n, pn = u + 1, 1 - p
            if exists(n):
                expert = nc.vector.value_load(experts_flat[0:1, bass.ds(n, 1)], min_val=0, max_val=E - 1)
                ge(dve, h_done, n - 1)
                if not gated:
                    ge(dve, ht_done, n - 1)
                nc.vector.tensor_copy(wa[pn][:], wa_flat[:, bass.ds(expert * A, A)]).then_inc(wa_done, 1)
            if exists(u) and gated:
                dve.wait_ge(silu_done, u + 1)
                nc.vector.tensor_tensor(ht[p][:], silu[p][:], g_ps[p][:, 0:HID], ALU.mult).then_inc(ht_done, 1)
            if exists(u - 1) and biased:
                y_evac(dve, u - 1, 1 - p)
            if exists(n):
                ge(dve, y_done, n - 1)
                if biased:
                    ge(dve, y_out, n - 1)
                nc.vector.tensor_copy(wb[pn][:], wb_flat[:, bass.ds(expert * B, B)]).then_inc(wb_done, 1)

        def steps(eng, step):
            for u in range(-1, 3):
                step(eng, u, u % 2)
            looped = (N - 5) // 2
            with eng.Fori(0, looped) as it:
                for i in range(2):
                    step(eng, it * 2 + (3 + i), (3 + i) % 2)
            for u in range(3 + 2 * looped, N + 1):
                step(eng, u, u % 2)

        with nc.Block() as block:

            @block.sync
            def _(sp):
                load(sp, 0, 0)
                sp.dma_start(wa_all[:], wa_dram).then_inc(w_loaded, 16)
                sp.dma_start(wb_all[:], wb_dram).then_inc(w_loaded, 16)
                steps(sp, sp_step)
                for p in range(2):
                    sp.wait_ge(stored[p], 16 * ((N + 1 - p) // 2))

            @block.tensor
            def _(pe):
                steps(pe, pe_step)

            @block.scalar
            def _(act):
                steps(act, act_step)

            @block.vector
            def _(dve):
                dve.wait_ge(w_loaded, 32)
                steps(dve, dve_step)


def add_rows(nc, kit, sem, tag, x, rows_of, weights, buffer_dram):
    ENTRIES = rows_of.shape[1]
    RING = 8
    with ExitStack() as ctx:
        k = kit.scope(ctx)
        got = k.sb(f"{tag}_got", [P, RING, D])
        arrived = [sem(f"{tag}_arrived{i}") for i in range(RING)]
        added = sem(f"{tag}_added")
        with nc.Block() as block:

            @block.gpsimd
            def _(pool):
                for n in range(ENTRIES):
                    ge(pool, added, n - RING + 1)
                    nc.gpsimd.indirect_dma_start(
                        out=got[:, n % RING, :], out_offset=None, in_=buffer_dram,
                        in_offset=bass.IndirectOffsetOnAxis(ap=rows_of[:, n:n + 1], axis=0))\
                        .then_inc(arrived[n % RING], 16)

            @block.vector
            def _(dve):
                for n in range(ENTRIES):
                    dve.wait_ge(arrived[n % RING], 16 * (n // RING + 1))
                    to = x[:, n % ALL_TILES, :]
                    ge(dve, added, n - ALL_TILES + 1)
                    if weights is None:
                        nc.vector.tensor_tensor(to, to, got[:, n % RING, :], ALU.add).then_inc(added, 1)
                    else:
                        nc.vector.scalar_tensor_tensor(to, got[:, n % RING, :], weights[:, n:n + 1], to,
                                                       ALU.mult, ALU.add).then_inc(added, 1)


def clear_rows(nc, kit, sem, tag, zero, rows_dram):
    cleared = sem(f"{tag}_cleared")
    with nc.Block() as block:

        @block.vector
        def _(dve):
            nc.vector.memset(zero[:], 0.0).then_inc(cleared, 1)

        @block.sync
        def _(sp):
            sp.wait_ge(cleared, 1)
            n = rows_dram.shape[0]
            for at in range(0, n, TILES):
                sp.dma_start(rows_dram[at:min(at + TILES, n)].rearrange("t p d -> p t d"),
                             zero[:, 0:min(TILES, n - at), :])\
                    .then_inc(cleared, 16)
            sp.wait_ge(cleared, 1 + 16 * -(-n // TILES))


def shared_expert(nc, kit, sem, tag, x, xt_all, w1_dram, w3_dram, w2_dram, meanwhile):
    ROWS, NC = w2_dram.shape[:2]
    FF = w1_dram.shape[1]
    BLOCKS = TOKENS // HALF
    BT = HALF // P
    with ExitStack() as ctx:
        k = kit.scope(ctx)
        w1 = k.sb(f"{tag}_w1", [P, FF])
        w3 = k.sb(f"{tag}_w3", [P, FF])
        w2 = k.sb(f"{tag}_w2", [ROWS, NC, D])
        silu = [k.sb(f"{tag}_silu{i}", [ROWS, NC, HALF]) for i in range(2)]
        ht = [k.sb(f"{tag}_ht{i}", [ROWS, NC, HALF]) for i in range(2)]
        h_ps = k.ps(f"{tag}_h", [P, NC, HALF])
        g_ps = k.ps(f"{tag}_g", [P, NC, HALF])
        y_ps = k.ps(f"{tag}_y", [P, 2, HALF])
        loaded = sem(f"{tag}_loaded")
        h_done, ht_done, silu_done, y_done, added = (sem(f"{tag}_{n}") for n in ("h", "ht", "silu", "y", "added"))
        xflat = x[:].rearrange("p t d -> p (t d)")

        with nc.Block() as block:

            @block.sync
            def _(sp):
                sp.dma_start(w1[:], w1_dram).then_inc(loaded, 16)
                sp.dma_start(w3[:], w3_dram).then_inc(loaded, 16)
                sp.dma_start(w2[:], w2_dram).then_inc(loaded, 16)

            @block.gpsimd
            def _(pool):
                meanwhile(pool)

            @block.tensor
            def _(pe):
                def up(n):
                    for c in range(NC):
                        pe.wait_ge(ht_done, n * NC + c + 1)
                        rhs = xt_all[:, bass.ds(n * HALF, HALF)]
                        cols = slice(c * ROWS, (c + 1) * ROWS)
                        nc.tensor.matmul(h_ps[0:ROWS, c, :], w1[:, cols], rhs, start=True, stop=True)
                        nc.tensor.matmul(g_ps[0:ROWS, c, :], w3[:, cols], rhs, start=True, stop=True)\
                            .then_inc(h_done, 1)

                def down(n, par):
                    pe.wait_ge(ht_done, n * NC + 2 * NC)
                    pe.wait_ge(added, n + 1)
                    for t in range(BT):
                        for c in range(NC):
                            mm = nc.tensor.matmul(y_ps[:, par, t * P:(t + 1) * P], ht[par][:, c, t * P:(t + 1) * P],
                                                  w2[:, c, :], start=c == 0, stop=c == NC - 1)
                    mm.then_inc(y_done, 1)

                pe.wait_ge(loaded, 48)
                with pe.Fori(0, BLOCKS // 2) as it:
                    up(it * 2)
                    up(it * 2 + 1)
                    down(it * 2, 0)
                    down(it * 2 + 1, 1)

            @block.scalar
            def _(act):
                with act.Fori(0, BLOCKS // 2) as it:
                    for par in range(2):
                        n = it * 2 + par
                        for c in range(NC):
                            act.wait_ge(h_done, n * NC + c + 1)
                            act.wait_ge(ht_done, n * NC + c + 1)
                            nc.scalar.activation(silu[par][:, c, :], h_ps[0:ROWS, c, :], ACT.Silu)\
                                .then_inc(silu_done, 1)

            @block.vector
            def _(dve):
                dve.sem_inc(ht_done, NC)
                dve.sem_inc(added, 2)
                dve.sem_inc(y_done, 2)
                with dve.Fori(0, BLOCKS // 2) as it:
                    for par in range(2):
                        n = it * 2 + par
                        dve.wait_ge(y_done, n + 1)
                        for c in range(NC):
                            dve.wait_ge(silu_done, n * NC + c + 1)
                            nc.vector.tensor_tensor(ht[par][:, c, :], silu[par][:, c, :], g_ps[0:ROWS, c, :],
                                                    ALU.mult).then_inc(ht_done, 1)
                    for par in range(2):
                        n = it * 2 + par
                        dve.wait_ge(y_done, n + 3)
                        rows = xflat[:, bass.ds(n * HALF, HALF)]
                        nc.vector.tensor_tensor(rows, rows, y_ps[:, par, :], ALU.add).then_inc(added, 1)


def tiles_of_rows(choices, experts):
    return choices * ALL_TILES + experts - 1


def ffn0(nc, kit, sem, x, ident, eps, gate_dram, bias_dram, starts_dram, wa_dram, wb_dram):
    E = gate_dram.shape[1]
    N = tiles_of_rows(1, E)
    x_rows = nc.dram_tensor("f0_x_rows", [N, P, D], F32).ap()
    y_rows = nc.dram_tensor("f0_y_rows", [N, P, D], F32).ap()
    with ExitStack() as ctx:
        k = kit.scope(ctx)
        rows_of = k.sb("f0_rows_of", [P, ALL_TILES], U32)
        tile_expert = k.sb("f0_tile_expert", [1, N], I32)
        with ExitStack() as gate_ctx:
            g = k.scope(gate_ctx)
            xn_all = g.sb("f0_xn_all", [P, ALL_TILES, D])
            logits = g.sb("f0_logits", [P, ALL_TILES, E])
            zero = g.sb("f0_zero", [P, TILES, D])
            clear_rows(nc, g, sem, "z0", zero, x_rows)
            norm_and_gate(nc, g, sem, "g0", x, ident, eps, gate_dram, bias_dram, xn_all, None, logits)
            route(nc, g, sem, "r0", logits, 1, starts_dram, rows_of, None, tile_expert)
            scattered = sem("f0_scattered")
            with nc.Block() as block:

                @block.gpsimd
                def _(pool):
                    scatter_rows(nc, pool, xn_all, rows_of, x_rows.rearrange("n p d -> (n p) d"), scattered)

        expert_tiles(nc, k, sem, "e0", ident, tile_expert, wa_dram, wb_dram, 4, False, True, x_rows, y_rows)
        add_rows(nc, k, sem, "add0", x, rows_of, None, y_rows.rearrange("n p d -> (n p) d"))


def ffn1(nc, kit, sem, x, ident, eps, gate_dram, starts_dram, wa_dram, wb_dram, sw1_dram, sw3_dram, sw2_dram):
    E = gate_dram.shape[1]
    N = tiles_of_rows(2, E)
    x_rows = nc.dram_tensor("f1_x_rows", [N, P, D], F32).ap()
    y_rows = nc.dram_tensor("f1_y_rows", [N, P, D], F32).ap()
    with ExitStack() as ctx:
        k = kit.scope(ctx)
        rows_of = k.sb("f1_rows_of", [P, 2 * ALL_TILES], U32)
        weights = k.sb("f1_weights", [P, 2 * ALL_TILES])
        tile_expert = k.sb("f1_tile_expert", [1, N], I32)
        with ExitStack() as gate_ctx:
            g = k.scope(gate_ctx)
            xn_all = g.sb("f1_xn_all", [P, ALL_TILES, D])
            xt_all = g.sb("f1_xt_all", [P, TOKENS])
            logits = g.sb("f1_logits", [P, ALL_TILES, E])
            zero = g.sb("f1_zero", [P, TILES, D])
            clear_rows(nc, g, sem, "z1", zero, x_rows)
            norm_and_gate(nc, g, sem, "g1", x, ident, eps, gate_dram, None, xn_all, xt_all, logits)
            route(nc, g, sem, "r1", logits, 2, starts_dram, rows_of, weights, tile_expert)
            scattered = sem("f1_scattered")

            def meanwhile(pool):
                scatter_rows(nc, pool, xn_all, rows_of, x_rows.rearrange("n p d -> (n p) d"), scattered)

            shared_expert(nc, g, sem, "es", x, xt_all, sw1_dram, sw3_dram, sw2_dram, meanwhile)
        expert_tiles(nc, k, sem, "e1", ident, tile_expert, wa_dram, wb_dram, 3, True, False, x_rows, y_rows)
        add_rows(nc, k, sem, "add1", x, rows_of, weights, y_rows.rearrange("n p d -> (n p) d"))


def transformer_kernel(nc, x_in, l0_attn_w, gate0, gate0_bias, starts0, wa_0, wb_0,
                       wq, w_down, wk_up, wv_up, wo, rope, gate1, starts1, wa_1, wb_1,
                       sw1, sw3, sw2, out):
    DH0, CLAMP = 64, 50.0
    with ExitStack() as ctx:
        kit = Kit(nc, ctx, ctx.enter_context(nc.semaphore("passed")))

        def in_stage(stage, *args):
            taken = []

            def sem(name):
                taken.append(nc.alloc_semaphore(name=name))
                return taken[-1]

            stage(nc, kit, sem, *args)
            nc.clear_and_free_semaphores(taken)
            nc.all_engine_barrier()

        x = kit.sb("x", [P, ALL_TILES, D])
        ident = kit.sb("ident", [P, P])
        ones = kit.sb("ones", [P, 32])
        eps = kit.sb("eps", [P, 1])
        xt0 = nc.dram_tensor("xt0", [BATCH, 3, P, SEQ], F32).ap()
        xt1 = nc.dram_tensor("xt1", [BATCH, 3, P, SEQ], F32).ap()
        parts = nc.dram_tensor("qk_parts", [BATCH, 2 * PARTS, P, SEQ], BF16).ap()
        values = nc.dram_tensor("values", [BATCH, QUADS, P, TILES, QUAD, V_COLS], F32).ap()

        in_stage(load_residual, x_in, x, ident, ones, eps)
        in_stage(layernorm, "ln0", x, ident, eps, xt0)
        in_stage(attention0, x, xt0, l0_attn_w, ones, DH0 ** -0.5, CLAMP)
        in_stage(ffn0, x, ident, eps, gate0, gate0_bias, starts0, wa_0, wb_0)
        in_stage(layernorm, "ln1", x, ident, eps, xt1)
        in_stage(project1, ident, xt1, wq, w_down, wk_up, wv_up, rope, parts, values)
        with ExitStack() as heads_ctx:
            heads = kit.scope(heads_ctx).sb("heads", [P, ALL_TILES, D])
            in_stage(attention1, ident, parts, values, heads, DH1 ** -0.5)
            in_stage(project_out1, ident, x, heads, wo)
        in_stage(ffn1, x, ident, eps, gate1, starts1, wa_1, wb_1, sw1, sw3, sw2)

        stored = ctx.enter_context(nc.semaphore("stored"))
        with nc.Block() as block:

            @block.sync
            def _(sp):
                for b in range(BATCH):
                    sp.dma_start(out[b].rearrange("(t p) d -> p t d", p=P), x[:, b * TILES:(b + 1) * TILES, :])\
                        .then_inc(stored, 16)
                sp.wait_ge(stored, 16 * BATCH)


def _rope_constants():
    import numpy as np
    theta = 10000.0
    inverse = 1.0 / theta ** (np.arange(0, DH1, 2, dtype=np.float32) / DH1)
    angle = np.outer(np.arange(SEQ, dtype=np.float32), inverse)
    table = np.empty((D, 2, SEQ), np.float32)
    for d in range(D):
        pair = d % DH1 // 2
        table[d, 0] = np.cos(angle[:, pair])
        table[d, 1] = np.sin(angle[:, pair]) * (-1 if d % 2 == 0 else 1)
    return table


def kernel(L0_attn_x, L0_attn_Wq, L0_attn_Wk, L0_attn_Wv, L0_attn_Wo, L0_ffn_gate_w, L0_ffn_gate_b,
           L0_ffn_expert_bias, L0_ffn_w1, L0_ffn_b1, L0_ffn_w2, L0_ffn_b2, L1_attn_wq, L1_attn_w_down,
           L1_attn_wk_up, L1_attn_wv_up, L1_attn_wo, L1_ffn_gate_w, L1_ffn_w1, L1_ffn_w2, L1_ffn_w3,
           L1_ffn_sw1, L1_ffn_sw2, L1_ffn_sw3):
    import numpy as np
    import concourse.bacc as bacc
    from concourse.bass_utils import run_bass_kernel_spmd

    a = np.asarray
    pairs = L0_attn_Wq.shape[0] // P

    def chunked(w, rows):
        w = a(w)
        n = -(-w.shape[1] // rows)
        w = np.pad(w, ((0, 0), (0, n * rows - w.shape[1]), (0, 0)))
        return w.reshape(w.shape[0], n, rows, D).transpose(2, 0, 1, 3).reshape(rows, w.shape[0], n * D)

    def whole_chunks(w):
        w = a(w).transpose(1, 0, 2)
        return np.pad(w, ((0, 0), (0, 0), (0, -w.shape[2] % P)))

    def starts(choices, experts):
        n = tiles_of_rows(choices, experts)
        return np.broadcast_to((np.arange(n, dtype=np.float32) * P)[None, :, None], (1, n, experts))

    exchanged = np.arange(D) ^ 1
    by_pair = [a(w).reshape(pairs, P, D).transpose(0, 2, 1) for w in (L0_attn_Wq, L0_attn_Wk, L0_attn_Wv)]
    by_pair.append(a(L0_attn_Wo).T.reshape(pairs, P, D))
    experts = L0_ffn_gate_b.shape[0]
    shared_rows = L1_ffn_sw2.shape[0] // 2
    laid_out = {
        "x": a(L0_attn_x),
        "l0_attn_w": np.stack(by_pair, 2),
        "gate0": a(L0_ffn_gate_w).T,
        "gate0_bias": np.broadcast_to(np.stack([a(L0_ffn_gate_b), a(L0_ffn_expert_bias)]), (P, 2, experts)),
        "starts0": starts(1, experts),
        "wa_0": np.concatenate([a(L0_ffn_w1).transpose(1, 0, 2),
                                a(L0_ffn_b1).reshape(experts, -1, P).transpose(2, 0, 1)], 2),
        "wb_0": np.concatenate([chunked(L0_ffn_w2, P), np.broadcast_to(a(L0_ffn_b2), (P, experts, D))], 2),
        "wq": np.stack([a(L1_attn_wq), a(L1_attn_wq)[:, exchanged]], 1),
        "w_down": a(L1_attn_w_down),
        "wk_up": np.stack([a(L1_attn_wk_up), a(L1_attn_wk_up)[:, exchanged]], 1),
        "wv_up": a(L1_attn_wv_up),
        "wo": a(L1_attn_wo),
        "rope": _rope_constants(),
        "gate1": a(L1_ffn_gate_w).T,
        "starts1": starts(2, experts),
        "wa_1": np.concatenate([whole_chunks(L1_ffn_w1), whole_chunks(L1_ffn_w3)], 2),
        "wb_1": chunked(L1_ffn_w2, P),
        "sw1": a(L1_ffn_sw1),
        "sw3": a(L1_ffn_sw3),
        "sw2": chunked(a(L1_ffn_sw2)[None], shared_rows).reshape(shared_rows, -1, D),
    }
    nc = bacc.Bacc("TRN2", target_bir_lowering=False, num_devices=1)
    arrays, args = {}, []
    for name, array in laid_out.items():
        array = np.ascontiguousarray(array)
        arrays[f"in_{name}"] = array
        args.append(nc.dram_tensor(f"in_{name}", array.shape, mybir.dt.from_np(array.dtype), kind="ExternalInput").ap())
    out = nc.dram_tensor("out_x", (BATCH, SEQ, D), F32, kind="ExternalOutput").ap()
    transformer_kernel(nc, *args, out)
    result = run_bass_kernel_spmd(nc, [arrays], core_ids=[0])
    return result.results[0]["out_x"]
```

```python
from contextlib import ExitStack

import concourse.bass as bass
from concourse import mybir

ACT = mybir.ActivationFunctionType
ALU = mybir.AluOpType
AX_X = mybir.AxisListType.X
F32 = mybir.dt.float32
F32R = mybir.dt.float32r
BF16 = mybir.dt.bfloat16
I32 = mybir.dt.int32
U32 = mybir.dt.uint32

P = 128
D = 128
BATCH, SEQ = 4, 1024
TILES = SEQ // P
TOKENS = BATCH * SEQ
ALL_TILES = TOKENS // P
HALF = 512
LN_EPS = 1e-5


def ge(eng, sem, value):
    if isinstance(value, int) and value <= 0:
        return
    eng.wait_ge(sem, value)


def of(dram, index):
    if isinstance(index, int):
        return dram[index]
    names = "abcde"[:len(dram.shape) - 1]
    rest = " ".join(names[1:])
    return dram[bass.ds(index, 1)].rearrange(f"z {' '.join(names)} -> (z {names[0]}) {rest}")


class Kit:

    def __init__(self, nc, ctx, passed):
        self.nc, self.ctx, self.passed = nc, ctx, passed

    def scope(self, ctx):
        return Kit(self.nc, ctx, self.passed)

    def sb(self, name, shape, dt=F32):
        return self.ctx.enter_context(self.nc.sbuf_tensor(name, shape, dt))

    def ps(self, name, shape, dt=F32):
        return self.ctx.enter_context(self.nc.psum_tensor(name, shape, dt))

    def ge_apart(self, eng, sem, value):
        ge(eng, sem, value)
        if not isinstance(value, int):
            eng.sem_inc(self.passed, 1)


def load_residual(nc, kit, sem, x_dram, x, ident, ones, eps):
    loaded, made = sem("x_loaded"), sem("consts_made")
    with nc.Block() as block:

        @block.sync
        def _(sp):
            for b in range(BATCH):
                sp.dma_start(x[:, b * TILES:(b + 1) * TILES, :],
                             x_dram[b].rearrange("(t p) d -> p t d", p=P)).then_inc(loaded, 16)
            sp.wait_ge(loaded, 16 * BATCH)

        @block.gpsimd
        def _(pool):
            nc.gpsimd.memset(ident[:], 0.0).then_inc(made, 1)
            nc.gpsimd.memset(ones[:], 1.0).then_inc(made, 1)
            nc.gpsimd.memset(eps[:], LN_EPS).then_inc(made, 1)
            kit.ge_apart(pool, made, 3)
            nc.gpsimd.affine_select(out=ident[:], in_=ident[:], compare_op=ALU.not_equal, fill=1.0, base=0,
                                    pattern=[[1, P]], channel_multiplier=-1).then_inc(made, 1)
            kit.ge_apart(pool, made, 4)


class Norm:

    def __init__(self, nc, kit, sem, tag, x):
        self.nc, self.kit = nc, kit
        self.xflat = x[:].rearrange("p t d -> p (t d)")
        self.stats = kit.sb(f"{tag}_stats", [P, TILES, 6])
        self.mv = kit.sb(f"{tag}_mv", [P, TILES, 2])
        self.mv_all = kit.sb(f"{tag}_mv_all", [P, ALL_TILES, 2])
        self.std = kit.sb(f"{tag}_std", [P, ALL_TILES])
        self.rstd = kit.sb(f"{tag}_rstd", [P, ALL_TILES])
        self.centred = kit.sb(f"{tag}_centred", [P, TILES, D])
        self.xn = [kit.sb(f"{tag}_xn{i}", [P, TILES, D]) for i in range(2)]
        self.stats_done, self.mv_done, self.kept = (sem(f"{tag}_{n}") for n in ("stats", "mv", "mv_kept"))
        self.std_done, self.rstd_done = sem(f"{tag}_std"), sem(f"{tag}_rstd")
        self.centred_done, self.xn_done = sem(f"{tag}_centred"), sem(f"{tag}_xn")

    def dve_statistics(self, dve):
        nc = self.nc
        mv_flat = self.mv_all[:].rearrange("p t c -> p (t c)")
        with dve.Fori(0, BATCH) as b:
            for t in range(TILES):
                last = nc.vector.bn_stats(self.stats[:, t, :], self.xflat[:, bass.ds(b * SEQ + t * D, D)])
            last.then_inc(self.stats_done, 1)
            self.kit.ge_apart(dve, self.stats_done, b + 1)
            for t in range(TILES):
                last = nc.vector.bn_aggr(self.mv[:, t, :], self.stats[:, t, :])
            last.then_inc(self.mv_done, 1)
            dve.wait_ge(self.mv_done, b + 1)
            nc.vector.tensor_copy(mv_flat[:, bass.ds(b * (2 * TILES), 2 * TILES)],
                                  self.mv[:].rearrange("p t c -> p (t c)")).then_inc(self.kept, 1)
            dve.wait_ge(self.kept, b + 1)
        dve.wait_ge(self.std_done, 1)
        nc.vector.reciprocal(self.rstd[:], self.std[:]).then_inc(self.rstd_done, 1)
        dve.wait_ge(self.rstd_done, 1)

    def act_std(self, act, eps):
        act.wait_ge(self.kept, BATCH)
        self.nc.scalar.activation(self.std[:], self.mv_all[:, :, 1], ACT.Sqrt, bias=eps[:, 0:1])\
            .then_inc(self.std_done, 1)

    def dve_xn(self, dve, b, p):
        nc = self.nc
        shape = [P, TILES, D]
        rows = self.xflat[:, bass.ds(b * SEQ, SEQ)].rearrange("p (t d) -> p t d", d=D)
        mean = self.mv_all[:].rearrange("p t c -> p (t c)")[:, bass.ds(b * (2 * TILES), 2 * TILES)]\
            .rearrange("p (t c) -> p t c", c=2)[:, :, 0:1]
        nc.vector.tensor_tensor(self.centred[:], rows, mean.to_broadcast(shape), ALU.subtract)\
            .then_inc(self.centred_done, 1)
        dve.wait_ge(self.centred_done, b + 1)
        nc.vector.tensor_tensor(self.xn[p][:], self.centred[:],
                                self.rstd[:, bass.ds(b * TILES, TILES)].unsqueeze(2).to_broadcast(shape), ALU.mult)\
            .then_inc(self.xn_done, 1)
        dve.wait_ge(self.xn_done, b + 1)


def layernorm(nc, kit, sem, tag, x, ident, eps, xt_dram):
    with ExitStack() as ctx:
        k = kit.scope(ctx)
        norm = Norm(nc, k, sem, tag, x)
        xt = [k.sb(f"{tag}_xt{i}", [P, SEQ]) for i in range(2)]
        high = [k.sb(f"{tag}_high{i}", [P, SEQ], F32R) for i in range(2)]
        low = [k.sb(f"{tag}_low{i}", [P, SEQ], F32R) for i in range(2)]
        turned = [k.ps(f"{tag}_turned{i}", [P, SEQ]) for i in range(2)]
        turn_done, xt_done, high_done, low_done = (sem(f"{tag}_{n}") for n in ("turn", "xt", "high", "low"))
        stored = [sem(f"{tag}_stored{i}") for i in range(2)]

        def in_pairs(eng, step):
            with eng.Fori(0, BATCH // 2) as it:
                for p in range(2):
                    step(it, it * 2 + p, p)

        with nc.Block() as block:

            @block.vector
            def _(dve):
                dve.sem_inc(turn_done, 2)
                norm.dve_statistics(dve)

                def low_part(it, b, p):
                    dve.wait_ge(high_done, b + 3)
                    dve.wait_ge(stored[p], it * 48 + 48)
                    nc.vector.tensor_tensor(low[p][:], xt[p][:], high[p][:].bitcast(F32), ALU.subtract)\
                        .then_inc(low_done, 1)

                with dve.Fori(0, BATCH // 2) as it:
                    for p in range(2):
                        dve.wait_ge(turn_done, it * 2 + p + 1)
                        norm.dve_xn(dve, it * 2 + p, p)
                    for p in range(2):
                        low_part(it, it * 2 + p, p)

            @block.scalar
            def _(act):
                norm.act_std(act, eps)

                def step(it, b, p):
                    act.wait_ge(turn_done, b + 3)
                    act.wait_ge(stored[p], it * 48 + 48)
                    nc.scalar.copy(xt[p][:], turned[p][:]).then_inc(xt_done, 1)
                    nc.scalar.copy(high[p][:], turned[p][:]).then_inc(high_done, 1)

                in_pairs(act, step)

            @block.tensor
            def _(pe):
                pe.sem_inc(high_done, 2)

                def step(it, b, p):
                    pe.wait_ge(norm.xn_done, b + 1)
                    pe.wait_ge(high_done, b + 1)
                    for t in range(TILES):
                        last = nc.tensor.transpose(turned[p][:, t * P:(t + 1) * P], norm.xn[p][:, t, :], ident[:])
                    last.then_inc(turn_done, 1)

                in_pairs(pe, step)

            @block.sync
            def _(sp):
                for p in range(2):
                    sp.sem_inc(stored[p], 48)

                def step(it, b, p):
                    out = of(xt_dram, b)
                    sp.wait_ge(xt_done, b + 1)
                    sp.dma_start(out[0], xt[p][:]).then_inc(stored[p], 16)
                    sp.wait_ge(high_done, b + 3)
                    sp.dma_start(out[1], high[p][:].bitcast(F32)).then_inc(stored[p], 16)
                    sp.wait_ge(low_done, b + 1)
                    sp.dma_start(out[2], low[p][:].bitcast(F32)).then_inc(stored[p], 16)

                in_pairs(sp, step)
                for p in range(2):
                    sp.wait_ge(stored[p], 48 * (1 + BATCH // 2))


def chunk_plan():
    chunks, at = [], 0
    for half in range(2):
        for j in range(TILES):
            lead = max(0, j * P - half * HALF)
            if lead >= HALF:
                continue
            chunks.append((half, j, HALF - lead, at))
            at += 2 * (HALF - lead)
    return chunks, at


CHUNKS, P_COLS = chunk_plan()
NCH = len(CHUNKS)
GROUPS = [(0, 4), (4, 6), (6, 8), (8, 12)]
DIAGONAL_GROUPS = (0, 3)


def attention0(nc, kit, sem, x, xt_dram, w_dram, ones, scale, clamp):
    PAIRS = w_dram.shape[0]
    UNITS = BATCH * PAIRS
    assert PAIRS == TILES
    DH = P // 2
    SEQ_BITS = PAIRS.bit_length() - 1
    with ExitStack() as ctx:
        k = kit.scope(ctx)
        xt = k.sb("a0_xt", [P, SEQ])
        xh = k.sb("a0_xh", [P, 2 * SEQ], F32R)
        xl = k.sb("a0_xl", [P, 2 * SEQ], F32R)
        w = [k.sb(f"a0_w{i}", [P, 2, P]) for i in range(2)]
        wv = [k.sb(f"a0_wv{i}", [P, P]) for i in range(2)]
        wo = [k.sb(f"a0_wo{i}", [P, P]) for i in range(2)]
        wh = [k.sb(f"a0_wh{i}", [P, 2, P], F32R) for i in range(2)]
        wl = [k.sb(f"a0_wl{i}", [P, 2, P], F32R) for i in range(2)]
        stage = k.sb("a0_stage", [P, 2, 2, SEQ], F32R)
        q_st = [k.sb(f"a0_q{i}", [P, 2, SEQ], F32R) for i in range(2)]
        kh_st = [k.sb(f"a0_kh{i}", [P, 2, SEQ], F32R) for i in range(2)]
        kl_st = [k.sb(f"a0_kl{i}", [P, 2, SEQ], F32R) for i in range(2)]
        v = [k.sb(f"a0_v{i}", [P, TILES, P]) for i in range(2)]
        prob = [k.sb(f"a0_p{i}", [P, P_COLS]) for i in range(2)]
        part = k.sb("a0_part", [P, 2, SEQ])
        rsum = k.sb("a0_rsum", [P, HALF])
        rhl = k.sb("a0_rhl", [P, 2, HALF], F32R)
        spread = k.sb("a0_spread", [P, 2, P], F32R)
        ot = k.sb("a0_ot", [P, SEQ])
        score_ps = k.ps("a0_score", [P, 2, 2, HALF])
        out_ps = k.ps("a0_out", [P, 2, HALF])
        misc = k.ps("a0_misc", [P, 2, HALF])

        x_loaded = sem("a0_x_loaded")
        xt_loaded = sem("a0_xt_loaded")
        w_loaded = [sem(f"a0_w_loaded{i}") for i in range(2)]
        wv_loaded = [sem(f"a0_wv_loaded{i}") for i in range(2)]
        wo_loaded = [sem(f"a0_wo_loaded{i}") for i in range(2)]
        w_high, w_split = sem("a0_w_high"), sem("a0_w_split")
        NAMES = ["k0", "k1", "q0", "q1", "v0", "v1"]
        proj = {n: sem(f"a0_proj_{n}") for n in NAMES}
        evac = {n: sem(f"a0_evac_{n}") for n in NAMES}
        high = {n: sem(f"a0_high_{n}") for n in NAMES[:4]}
        stacked = sem("a0_stacked")
        scored, tanh_done, exp_done, masked = (sem(f"a0_{n}") for n in ("scored", "tanh", "exp", "masked"))
        pv_done = [sem(f"a0_pv{i}") for i in range(2)]
        added = sem("a0_added")
        summed, recip, r_high, r_split = (sem(f"a0_{n}") for n in ("summed", "recip", "r_high", "r_split"))
        spread_made = sem("a0_spread_made")
        out_evac = [sem(f"a0_out_evac{i}") for i in range(2)]
        bcast = [sem(f"a0_bcast{i}") for i in range(2)]
        normed = [sem(f"a0_normed{i}") for i in range(2)]
        wo_done = [sem(f"a0_wo{i}") for i in range(2)]
        x_added = [sem(f"a0_x_added{i}") for i in range(2)]
        QK_JOBS, V_JOBS = {0: "k0", 2: "q0", 3: "k1", 5: "q1"}, {4: 0, 7: 1}
        ADDS = NCH - 1
        STACK_DMAS = 12
        xflat = x[:].rearrange("p t d -> p (t d)")

        def exists(u):
            return not isinstance(u, int) or 0 <= u < UNITS

        def chunk_of(buffer, i, cols=None):
            _, _, width, at = CHUNKS[i]
            a, b = cols or (0, width)
            return buffer[:, at:at + 2 * width].rearrange("p (h q) -> p h q", h=2)[:, :, a:b]

        def load_unit(sp, n, p):
            if not exists(n):
                return
            kit.ge_apart(sp, w_split, n - 1)
            sp.dma_start(w[p][:], of(w_dram, n & (PAIRS - 1))[:, 0:2, :]).then_inc(w_loaded[p], 16)

        def load_x(sp, n):
            if not exists(n):
                return
            kit.ge_apart(sp, proj["q1"], n)
            kit.ge_apart(sp, x_loaded, n * 32 + 32)
            tile = n & (TILES - 1)
            src = of(xt_dram, ((n >> SEQ_BITS) + 1) & (BATCH - 1))
            to = ((n + TILES) & (2 * TILES - 1)) * P
            for part_, x_ in ((1, xh), (2, xl)):
                sp.dma_start(x_[:, bass.ds(to, P)].bitcast(F32), src[part_][:, bass.ds(tile * P, P)])\
                    .then_inc(x_loaded, 16)

        def load_xt(sp, n):
            if not exists(n):
                return
            kit.ge_apart(sp, proj["v1"], n)
            sp.dma_start(xt[:], of(xt_dram, (n >> SEQ_BITS) & (BATCH - 1))[0]).then_inc(xt_loaded, 16)

        def sp_step(sp, u, p):
            load_x(sp, u + 1)
            load_unit(sp, u + 2, p)
            if exists(u):
                kit.ge_apart(sp, wo_done[1], u - 1)
                sp.dma_start(wo[p][:], of(w_dram, u & (PAIRS - 1))[:, 3, :]).then_inc(wo_loaded[p], 16)
            n, pn = u + 1, 1 - p
            if exists(n):
                kit.ge_apart(sp, proj["v1"], n - 1)
                sp.dma_start(wv[pn][:], of(w_dram, n & (PAIRS - 1))[:, 2, :]).then_inc(wv_loaded[pn], 16)
                sg = stage[:].bitcast(F32)
                A, B = slice(0, DH), slice(DH, P)
                for what, first, second in (("k", "k0", "k1"), ("q", "q0", "q1")):
                    kit.ge_apart(sp, evac[first], n + 1)
                    kit.ge_apart(sp, evac[second], n + 1)
                    if what == "q":
                        moves = [(q_st[pn], A, 0, A, 0), (q_st[pn], B, 0, A, 1),
                                 (q_st[pn], A, 1, B, 1), (q_st[pn], B, 1, B, 0)]
                        row = 0
                    else:
                        moves = [(st[pn], half, h, (A, B)[h], part_)
                                 for st, part_ in ((kh_st, 0), (kl_st, 1)) for h in range(2) for half in (A, B)]
                        row = 1
                    for st, to, h, frm, hl in moves:
                        sp.dma_start(st[to, h, :].bitcast(F32), sg[frm, row, hl, :]).then_inc(stacked, 16)
            load_xt(sp, u + 1)

        def split_w(pool, n, p):
            if not exists(n):
                return
            kit.ge_apart(pool, w_loaded[p], 16 * (n >> 1) + 16)
            kit.ge_apart(pool, proj["q1"], n - 1)
            nc.gpsimd.tensor_copy(wh[p][:], w[p][:, 0:2, :]).then_inc(w_high, 1)
            kit.ge_apart(pool, w_high, n + 1)
            nc.gpsimd.tensor_tensor(wl[p][:], w[p][:, 0:2, :], wh[p][:].bitcast(F32),
                                    ALU.subtract).then_inc(w_split, 1)

        def pool_step(pool, u, p):
            for g in DIAGONAL_GROUPS:
                if exists(u):
                    kit.ge_apart(pool, exp_done, u * len(GROUPS) + g + 1)
                    for i in range(*GROUPS[g]):
                        blk = chunk_of(prob[p], i, (0, P))
                        last = nc.gpsimd.affine_select(out=blk, in_=blk, compare_op=ALU.is_ge, fill=0.0, base=0,
                                                       pattern=[[0, 2], [1, P]], channel_multiplier=-1)
                    last.then_inc(masked, 1)
                if g == 0:
                    split_w(pool, u + 2, p)

        def act_high(act, n, name):
            if not exists(n):
                return
            which, half = "qk".index(name[0]), int(name[1])
            act.wait_ge(proj[name], n + 1)
            if name == "k0":
                ge(act, stacked, n * (16 * STACK_DMAS))
            nc.scalar.copy(stage[:, which, 0, half * HALF:(half + 1) * HALF], misc[:, half, :])\
                .then_inc(high[name], 1)

        def act_v(act, u, p, half):
            act.wait_ge(proj[f"v{half}"], u + 1)
            if half == 0:
                ge(act, pv_done[1], u - 1)
            nc.scalar.copy(v[p][:, half * (TILES // 2):(half + 1) * (TILES // 2), :].rearrange("p t d -> p (t d)"),
                           misc[:, half, :]).then_inc(evac[f"v{half}"], 1)

        def act_out(act, m, half):
            if not exists(m):
                return
            act.wait_ge(pv_done[half], m + 1)
            ge(act, wo_done[half], m)
            nc.scalar.copy(ot[:, half * HALF:(half + 1) * HALF], out_ps[:, half, :]).then_inc(out_evac[half], 1)

        def act_step(act, u, p):
            act_out(act, u - 2, 1)
            if exists(u):
                ge(act, pv_done[1], u - 1)
                ge(act, added, (u - 1) * ADDS)
            g = 0
            for i, (_, _, width, at) in enumerate(CHUNKS):
                if exists(u):
                    act.wait_ge(scored, u * NCH + i + 1)
                    nc.scalar.activation(chunk_of(prob[p], i), score_ps[:, i % 2, :, 0:width], ACT.Tanh,
                                         scale=scale / clamp).then_inc(tanh_done, 1)
                if i in QK_JOBS:
                    act_high(act, u + 1, QK_JOBS[i])
                if i == 6:
                    act_out(act, u - 1, 0)
                if i in V_JOBS and exists(u):
                    act_v(act, u, p, V_JOBS[i])
                if i + 1 == GROUPS[g][1] and exists(u):
                    a = CHUNKS[GROUPS[g][0]][3]
                    act.wait_ge(tanh_done, u * NCH + i + 1)
                    nc.scalar.activation(prob[p][:, a:at + 2 * width], prob[p][:, a:at + 2 * width], ACT.Exp,
                                         scale=clamp).then_inc(exp_done, 1)
                    g += 1

        def pe_scores(pe, u, p, i):
            half, j, width, _ = CHUNKS[i]
            q0 = half * HALF + HALF - width
            if i == 0:
                pe.wait_ge(stacked, (u + 1) * (16 * STACK_DMAS))
            ge(pe, tanh_done, u * NCH + i - 1)
            for h in range(2):
                for st in (kh_st, kl_st):
                    last = nc.tensor.matmul(score_ps[:, i % 2, h, 0:width], st[p][:, h, j * P:(j + 1) * P],
                                            q_st[p][:, h, q0:q0 + width], start=st is kh_st, stop=st is kl_st)
            last.then_inc(scored, 1)

        def pe_pv(pe, m, p, i):
            half, j, width, _ = CHUNKS[i]
            g = [g for g, (a, b) in enumerate(GROUPS) if a == i]
            if g and g[0] in DIAGONAL_GROUPS:
                pe.wait_ge(masked, m * 2 + DIAGONAL_GROUPS.index(g[0]) + 1)
            elif g:
                pe.wait_ge(exp_done, m * len(GROUPS) + g[0] + 1)
            if j == 0:
                ge(pe, out_evac[half], m)
                ge(pe, evac["v1"], m + 1)
            last_j = max(c[1] for c in CHUNKS if c[0] == half)
            for h in range(2):
                mm = nc.tensor.matmul(out_ps[h * DH:(h + 1) * DH, half, HALF - width:HALF],
                                      v[p][:, j, h * DH:(h + 1) * DH], chunk_of(prob[p], i)[:, h, :],
                                      start=j == 0, stop=j == last_j)
            if j == last_j:
                mm.then_inc(pv_done[half], 1)

        def pe_qk(pe, n, p, name):
            which, half = "qk".index(name[0]), int(name[1])
            if name == "k0":
                pe.wait_ge(x_loaded, ((n >> SEQ_BITS) << (SEQ_BITS + 5)) + 32)
                pe.wait_ge(w_split, n + 1)
                ge(pe, x_added[0], n - 2)
            ge(pe, {"q0": evac["k0"], "q1": evac["k1"], "k1": x_added[1]}.get(name, evac["k0"]),
               {"q0": n + 1, "q1": n + 1, "k1": n - 2}.get(name, 0))
            cols = bass.ds(((n >> SEQ_BITS) & 1) * SEQ + half * HALF, HALF)
            terms = [(wh, xh), (wh, xl), (wl, xh)]
            for t, (ws, xs) in enumerate(terms):
                mm = nc.tensor.matmul(misc[:, half, :], ws[p][:, which, :], xs[:, cols],
                                      start=t == 0, stop=t == len(terms) - 1)
            mm.then_inc(proj[name], 1)

        def pe_v(pe, n, p, half):
            if exists(n + 1):
                pe.wait_ge(evac[f"q{half}"], n + 2)
            else:
                ge(pe, x_added[half], n - 1)
            if half == 0:
                pe.wait_ge(xt_loaded, n * 16 + 16)
                pe.wait_ge(wv_loaded[p], 16 * (n >> 1) + 16)
            for t in range(TILES // 2):
                tile = half * (TILES // 2) + t
                mm = nc.tensor.matmul(misc[:, half, t * P:(t + 1) * P], xt[:, tile * P:(tile + 1) * P],
                                      wv[p][:], start=True, stop=True)
            mm.then_inc(proj[f"v{half}"], 1)

        def pe_sum(pe, m):
            if exists(m + 1):
                pe.wait_ge(evac["v0"], m + 2)
            else:
                ge(pe, x_added[0], m)
            pe.wait_ge(added, m * ADDS + ADDS)
            for half in range(2):
                for h in range(2):
                    row = 32 * (2 * half + h)
                    mm = nc.tensor.matmul(misc[row:row + 32, 0, :], ones[:, 0:32],
                                          part[:, h, half * HALF:(half + 1) * HALF], start=True, stop=True)
            mm.then_inc(summed, 1)

        def pe_bcast(pe, m, half):
            pe.wait_ge(r_split, m + 1)
            if half == 1:
                if exists(m + 1):
                    pe.wait_ge(evac["v1"], m + 2)
                else:
                    ge(pe, x_added[1], m)
            if isinstance(m, int) and m == 0 and half == 0:
                pe.wait_ge(spread_made, 5)
            for t in range(2):
                mm = nc.tensor.matmul(misc[:, half, :], spread[:, half, :], rhl[:, t, :], start=t == 0, stop=t == 1)
            mm.then_inc(bcast[half], 1)

        def pe_wo(pe, m, p, half):
            if half == 0:
                pe.wait_ge(wo_loaded[p], 16 * (m >> 1) + 16)
            pe.wait_ge(normed[half], m + 1)
            for t in range(TILES // 2):
                tile = half * (TILES // 2) + t
                mm = nc.tensor.matmul(misc[:, half, t * P:(t + 1) * P], ot[:, tile * P:(tile + 1) * P],
                                      wo[p][:], start=True, stop=True)
            mm.then_inc(wo_done[half], 1)

        def pe_step(pe, u, p):
            nxt, prev, before = u + 1, u - 1, u - 2
            for i in range(NCH):
                if exists(u):
                    pe_scores(pe, u, p, i)
                if exists(prev):
                    pe_pv(pe, prev, 1 - p, i)
                if i in QK_JOBS and exists(nxt):
                    pe_qk(pe, nxt, 1 - p, QK_JOBS[i])
                if i in V_JOBS and exists(u):
                    pe_v(pe, u, p, V_JOBS[i])
                if i == 1 and exists(before):
                    pe_wo(pe, before, p, 1)
                if exists(prev):
                    if i == 5:
                        pe_sum(pe, prev)
                    if i in (9, 10):
                        pe_bcast(pe, prev, i - 9)
                    if i == 11:
                        pe_wo(pe, prev, 1 - p, 0)

        def dve_split(dve, n, name):
            which, half = "qk".index(name[0]), int(name[1])
            cols = slice(half * HALF, (half + 1) * HALF)
            dve.wait_ge(high[name], n + 1)
            nc.vector.tensor_tensor(stage[:, which, 1, cols], misc[:, half, :],
                                    stage[:, which, 0, cols].bitcast(F32), ALU.subtract).then_inc(evac[name], 1)

        def dve_adds(dve, m, p, g):
            if g in DIAGONAL_GROUPS:
                dve.wait_ge(masked, m * 2 + DIAGONAL_GROUPS.index(g) + 1)
            else:
                dve.wait_ge(exp_done, m * len(GROUPS) + g + 1)
            steps = []
            if g == 0:
                ge(dve, summed, m)
                steps.append(("copy", slice(0, P), chunk_of(prob[p], 0, (0, P)), None))
                steps.append(("add", slice(P, HALF), chunk_of(prob[p], 0, (P, HALF)), chunk_of(prob[p], 1)))
            elif g == 1:
                steps.append(("add", slice(HALF, SEQ), chunk_of(prob[p], 4), chunk_of(prob[p], 5)))
            for i in range(*GROUPS[g]):
                half, j, width, _ = CHUNKS[i]
                if j >= 2:
                    cols = slice(half * HALF + HALF - width, half * HALF + HALF)
                    steps.append(("acc", cols, part[:, :, cols], chunk_of(prob[p], i)))
            done = {0: 0, 1: 4, 2: 5, 3: 7}[g]
            for s, (kind, cols, a, b) in enumerate(steps):
                if kind == "acc":
                    dve.wait_ge(added, m * ADDS + done + s)
                if kind == "copy":
                    ins = nc.vector.tensor_copy(part[:, :, cols], a)
                else:
                    ins = nc.vector.tensor_tensor(part[:, :, cols], a, b, ALU.add)
                ins.then_inc(added, 1)

        def dve_recip(dve, m):
            dve.wait_ge(summed, m + 1)
            ge(dve, bcast[1], m)
            nc.vector.reciprocal(rsum[:], misc[:, 0, :]).then_inc(recip, 1)

        def dve_r_high(dve, m):
            dve.wait_ge(recip, m + 1)
            nc.vector.tensor_copy(rhl[:, 0, :], rsum[:]).then_inc(r_high, 1)

        def dve_r_low(dve, m):
            dve.wait_ge(r_high, m + 1)
            nc.vector.tensor_tensor(rhl[:, 1, :], rsum[:], rhl[:, 0, :].bitcast(F32), ALU.subtract)\
                .then_inc(r_split, 1)

        def dve_norm(dve, m, half):
            cols = slice(half * HALF, (half + 1) * HALF)
            dve.wait_ge(out_evac[half], m + 1)
            dve.wait_ge(bcast[half], m + 1)
            nc.vector.tensor_tensor(ot[:, cols], misc[:, half, :], ot[:, cols], ALU.mult)\
                .then_inc(normed[half], 1)

        def dve_x_add(dve, m, half):
            dve.wait_ge(wo_done[half], m + 1)
            ge(dve, x_added[half], m)
            at = ((m >> SEQ_BITS) & (BATCH - 1)) * SEQ + half * HALF
            rows = xflat[:, bass.ds(at, HALF)]
            nc.vector.tensor_tensor(rows, rows, misc[:, half, :], ALU.add).then_inc(x_added[half], 1)

        def dve_step(dve, u, p):
            nxt, prev, before = u + 1, u - 1, u - 2
            order = [("x", before, 0), ("norm", before, 1), ("split", nxt, "k0"), ("x", before, 1),
                     ("split", nxt, "q0"), ("split", nxt, "k1"), ("adds", prev, 3), ("split", nxt, "q1"),
                     ("recip", prev, None), ("r_high", prev, None), ("r_low", prev, None), ("adds", u, 0),
                     ("adds", u, 1), ("norm", prev, 0), ("adds", u, 2)]
            for what, m, arg in order:
                if not exists(m):
                    continue
                if what == "norm":
                    dve_norm(dve, m, arg)
                elif what == "split":
                    dve_split(dve, m, arg)
                elif what == "x":
                    dve_x_add(dve, m, arg)
                elif what == "adds":
                    dve_adds(dve, m, p if m is u else 1 - p, arg)
                elif what == "recip":
                    dve_recip(dve, m)
                elif what == "r_high":
                    dve_r_high(dve, m)
                else:
                    dve_r_low(dve, m)

        def steps(eng, step):
            for u in range(-1, 4):
                step(eng, u, u % 2)
            looped = (UNITS - 5) // 2
            with eng.Fori(0, looped) as it:
                for par in range(2):
                    step(eng, it * 2 + (4 + par), par)
            for u in range(4 + 2 * looped, UNITS + 2):
                step(eng, u, u % 2)

        with nc.Block() as block:

            @block.sync
            def _(sp):
                for part_, x_ in ((1, xh), (2, xl)):
                    sp.dma_start(x_[:, 0:SEQ].bitcast(F32), xt_dram[0, part_]).then_inc(x_loaded, 16)
                load_unit(sp, 0, 0)
                steps(sp, sp_step)
                sp.wait_ge(x_loaded, 32 * (UNITS + 1))

            @block.gpsimd
            def _(pool):
                split_w(pool, 0, 0)
                steps(pool, pool_step)

            @block.scalar
            def _(act):
                steps(act, act_step)

            @block.tensor
            def _(pe):
                steps(pe, pe_step)

            @block.vector
            def _(dve):
                nc.vector.memset(spread[:].bitcast(F32), 0.0).then_inc(spread_made, 1)
                dve.wait_ge(spread_made, 1)
                for half in range(2):
                    for h in range(2):
                        row = 32 * (2 * half + h)
                        nc.vector.memset(spread[row:row + 1, half, h * DH:(h + 1) * DH].bitcast(F32), 1.0)\
                            .then_inc(spread_made, 1)
                steps(dve, dve_step)


PAGE = 32
HEADS1, DH1 = 16, 8
QUAD = 4
QUADS = HEADS1 // QUAD
PARTS = 3
V_COLS = 32


def project1(nc, kit, sem, ident, xt_dram, wq_dram, wdown_dram, wk_dram, wv_dram, rope_dram, parts_dram, v_dram):
    with ExitStack() as ctx:
        k = kit.scope(ctx)
        L = wdown_dram.shape[1]
        wq = k.sb("p1_wq", [P, 2, P])
        wd = k.sb("p1_wd", [P, L])
        wk = k.sb("p1_wk", [L, 2, P])
        wv = k.sb("p1_wv", [L, P])
        rope = k.sb("p1_rope", [P, 2, SEQ])
        xt = k.sb("p1_xt", [P, 2 * SEQ])
        lat = k.sb("p1_lat", [L, SEQ])
        t_cos, t_sin = k.sb("p1_tcos", [P, SEQ]), k.sb("p1_tsin", [P, SEQ])
        rest = k.sb("p1_rest", [P, SEQ])
        part = [k.sb(f"p1_part{i}", [P, PARTS, SEQ], BF16) for i in range(2)]
        vp = k.sb("p1_v", [P, TILES, HEADS1, V_COLS])
        plain = k.ps("p1_plain", [P, SEQ])
        partner = k.ps("p1_partner", [P, SEQ])
        lat_ps = k.ps("p1_lat_ps", [L, SEQ])
        v_ps = k.ps("p1_v_ps", [P, SEQ])
        w_loaded, x_loaded, v_set = sem("p1_w_loaded"), sem("p1_x_loaded"), sem("p1_v_set")
        lat_done, lat_out, v_done, v_out = (sem(f"p1_{n}") for n in ("lat_done", "lat_out", "v_done", "v_out"))
        plain_done, cos_done, sin_done, rot_done = (sem(f"p1_{n}") for n in ("plain", "cos", "sin", "rot"))
        hi_done, rest_done, mid_done, lo_done = (sem(f"p1_{n}") for n in ("hi", "rest", "mid", "lo"))
        stored, x_free, part_free, v_free = (sem(f"p1_{n}") for n in ("stored", "x_free", "part_free", "v_free"))

        with nc.Block() as block:

            @block.sync
            def _(sp):
                for dst, src in ((wq, wq_dram), (wd, wdown_dram), (wk, wk_dram), (wv, wv_dram), (rope, rope_dram)):
                    sp.dma_start(dst[:], src).then_inc(w_loaded, 16)
                sp.sem_inc(part_free, 1)
                sp.sem_inc(plain_done, 1)
                sp.dma_start(xt[:, 0:SEQ], xt_dram[0, 0]).then_inc(x_loaded, 16)
                with sp.Fori(0, BATCH) as b:
                    kit.ge_apart(sp, plain_done, b * 2 + 1)
                    kit.ge_apart(sp, x_loaded, b * 16 + 16)
                    nxt = b + 1
                    sp.dma_start(xt[:, bass.ds((nxt & 1) * SEQ, SEQ)], of(xt_dram, nxt & (BATCH - 1))[0])\
                        .then_inc(x_loaded, 16)
                    for i in range(2):
                        sp.wait_ge(hi_done, b * 2 + i + 2)
                        sp.wait_ge(mid_done, b * 2 + i + 1)
                        kit.ge_apart(sp, lo_done, b * 2 + i + 2)
                        for a in range(PARTS):
                            dst = of(parts_dram, b)[i * PARTS + a]
                            sp.dma_start(dst, part[i][:, a, :]).then_inc(stored, 16)
                    sp.wait_ge(v_out, b + 2)
                    dst = of(v_dram, b)
                    for q in range(QUADS):
                        sp.dma_start(dst[q], vp[:, :, q * QUAD:(q + 1) * QUAD, :]).then_inc(stored, 16)
                    sp.wait_ge(stored, b * (16 * (2 * PARTS + QUADS)) + 16 * (2 * PARTS + QUADS))
                    sp.sem_inc(part_free, 1)
                sp.wait_ge(x_loaded, 16 * (BATCH + 1))

            @block.tensor
            def _(pe):
                pe.wait_ge(w_loaded, 16 * 5)
                with pe.Fori(0, BATCH) as b:
                    pe.wait_ge(x_loaded, b * 16 + 16)

                    def x_cols(half):
                        return xt[:, bass.ds((b & 1) * SEQ + half * HALF, HALF)]

                    for half in range(2):
                        mm = nc.tensor.matmul(lat_ps[:, half * HALF:(half + 1) * HALF], wd[:], x_cols(half),
                                              start=True, stop=True)
                    mm.then_inc(lat_done, 1)
                    for i in range(2):
                        pe.wait_ge(sin_done, b * 2 + i + 1)
                        if i == 1:
                            pe.wait_ge(lat_out, b + 1)
                        for to, which in ((plain, 0), (partner, 1)):
                            for half in range(2):
                                cols = slice(half * HALF, (half + 1) * HALF)
                                w_, x_ = (wq, x_cols(half)) if i == 0 else (wk, lat[:, cols])
                                mm = nc.tensor.matmul(to[:, cols], w_[:, which, :], x_, start=True, stop=True)
                        mm.then_inc(plain_done, 1)
                    pe.wait_ge(v_out, b + 1)
                    for t in range(TILES):
                        mm = nc.tensor.matmul(v_ps[:, t * P:(t + 1) * P], lat[:, t * P:(t + 1) * P], wv[:],
                                              start=True, stop=True)
                    mm.then_inc(v_done, 1)

            @block.scalar
            def _(act):
                act.wait_ge(v_set, 2)
                act.sem_inc(v_done, 1)
                act.sem_inc(v_out, 1)
                act.sem_inc(hi_done, 1)
                with act.Fori(0, BATCH) as b:
                    act.wait_ge(lat_done, b + 1)
                    act.wait_ge(v_done, b + 1)
                    nc.scalar.copy(lat[:], lat_ps[:]).then_inc(lat_out, 1)
                    act.wait_ge(part_free, b + 1)
                    for i in range(2):
                        act.wait_ge(rot_done, b * 2 + i + 1)
                        nc.scalar.copy(part[i][:, 0, :], t_cos[:]).then_inc(hi_done, 1)
                        act.wait_ge(rest_done, b * 2 + i + 1)
                        nc.scalar.copy(part[i][:, 1, :], rest[:]).then_inc(mid_done, 1)
                    act.wait_ge(v_done, b + 2)
                    nc.scalar.copy(vp[:, :, :, 0:DH1], v_ps[:].rearrange("p (t h d) -> p t h d", t=TILES, d=DH1))\
                        .then_inc(v_out, 1)

            @block.vector
            def _(dve):
                nc.vector.memset(vp[:], 0.0).then_inc(v_set, 1)
                dve.wait_ge(v_set, 1)
                nc.vector.memset(vp[:, :, :, DH1:DH1 + 1], 1.0).then_inc(v_set, 1)
                dve.wait_ge(w_loaded, 16 * 5)
                dve.sem_inc(sin_done, 1)
                dve.sem_inc(lo_done, 1)
                with dve.Fori(0, BATCH) as b:
                    for i in range(2):
                        n = b * 2 + i
                        dve.wait_ge(plain_done, n + 2)
                        dve.wait_ge(lo_done, n + 1)
                        dve.wait_ge(hi_done, n + 1)
                        nc.vector.tensor_tensor(t_cos[:], plain[:], rope[:, 0, :], ALU.mult).then_inc(cos_done, 1)
                        nc.vector.tensor_tensor(t_sin[:], partner[:], rope[:, 1, :], ALU.mult).then_inc(sin_done, 1)
                        dve.wait_ge(cos_done, n + 1)
                        dve.wait_ge(sin_done, n + 2)
                        nc.vector.tensor_tensor(t_cos[:], t_cos[:], t_sin[:], ALU.add).then_inc(rot_done, 1)
                        dve.wait_ge(hi_done, n + 2)
                        nc.vector.tensor_tensor(rest[:], t_cos[:], part[i][:, 0, :], ALU.subtract)\
                            .then_inc(rest_done, 1)
                        dve.wait_ge(mid_done, n + 1)
                        nc.vector.tensor_tensor(part[i][:, 2, :], rest[:], part[i][:, 1, :], ALU.subtract)\
                            .then_inc(lo_done, 1)


def attention1(nc, kit, sem, ident, parts_dram, v_dram, out, scale):
    UNITS = BATCH * QUADS
    ROWS = PARTS * PARTS * DH1
    ROWS_M = ROWS + PARTS
    SLOTS = 2 * NCH
    RING = 6
    PV_LAG = 2
    MAX_SLOTS = 15
    PIECES = [(h, t, c, c * HALF, min(HALF, (t + 1) * P - c * HALF))
              for h in range(QUAD) for t in range(TILES) for c in range(2) if (t + 1) * P > c * HALF]
    EARLY = len(PIECES) // QUAD
    BUFS = 3
    BANKS = 3
    with ExitStack() as ctx:
        k = kit.scope(ctx)
        q_st = [k.sb(f"a1_q{i}", [P, QUAD, SEQ], BF16) for i in range(BUFS)]
        k_st = [k.sb(f"a1_k{i}", [P, QUAD, SEQ], BF16) for i in range(BUFS)]
        v_st = [k.sb(f"a1_v{i}", [P, TILES, QUAD, V_COLS]) for i in range(BUFS)]
        prob = [k.sb(f"a1_p{i}", [P, 2, HALF]) for i in range(RING)]
        identb = k.sb("a1_identb", [P, P], BF16)
        page_mask = k.sb("a1_page_mask", [P, P], BF16)
        mx = [[k.sb(f"a1_mx{i}_{c}", [P, QUAD, TILES]) for c in range(2)] for i in range(BUFS)]
        ones_rows = k.sb("a1_ones_rows", [PARTS, QUAD, SEQ], BF16)
        neg = k.sb("a1_neg", [QUAD * TILES, P])
        neg_rest = k.sb("a1_neg_rest", [QUAD * TILES, P])
        neg_part = k.sb("a1_neg_part", [QUAD * TILES, PARTS, P], BF16)
        ot = k.sb("a1_ot", [P, 2, HALF])
        rs = k.sb("a1_rs", [P, TILES // 2, QUAD])
        score_ps = k.ps("a1_score", [P, 2, 2, HALF])
        out_ps = k.ps("a1_out", [P, HALF])
        misc = k.ps("a1_misc", [P, BANKS, HALF])

        st_loaded = [sem(f"a1_st_loaded{i}") for i in range(BUFS)]
        masks_made, ones_made, ones_loaded = (sem(f"a1_{n}") for n in ("masks_made", "ones_made", "ones_loaded"))
        cleared = [sem(f"a1_cleared{i}") for i in range(BUFS)]
        ready, free = sem("a1_misc_ready"), sem("a1_misc_free")
        combined, neg_done, hi_done, rest_done, mid_done, lo_done = \
            (sem(f"a1_{n}") for n in ("combined", "neg", "neg_hi", "neg_rest", "neg_mid", "neg_lo"))
        m_stacked = sem("a1_m_stacked")
        scored, exp_done, masked = (sem(f"a1_{n}") for n in ("scored", "exp", "masked"))
        pv_chunks = sem("a1_pv_chunks")
        HALF_END = [1 + max(i for i, c in enumerate(CHUNKS) if c[0] == half) for half in range(2)]
        out_evac = [sem(f"a1_out_evac{i}") for i in range(2)]
        rs_done = sem("a1_rs")
        ST_DMAS = 2 * PARTS * PARTS + 1
        DIAG = [i for i, (half, j, _, _) in enumerate(CHUNKS) if j // (TILES // 2) == half]

        def exists(u):
            return not isinstance(u, int) or 0 <= u < UNITS

        def uses(u):
            by_slot = {s: [] for s in range(SLOTS)}
            if exists(u + 1):
                left = PIECES if isinstance(u, int) and u == -1 else PIECES[EARLY:]
                for n, piece in enumerate(left):
                    by_slot[n * MAX_SLOTS // len(left)].append(("max", (1, *piece), n == len(left) - 1))
                by_slot[MAX_SLOTS + 2].append(("turn_max", None, None))
            if exists(u + 2):
                for n, piece in enumerate(PIECES[:EARLY]):
                    by_slot[MAX_SLOTS + n * (SLOTS - MAX_SLOTS) // EARLY].append(("max", (2, *piece), False))
            if exists(u - 1):
                by_slot[9].append(("turn_out", 1, None))
            if exists(u):
                by_slot[15].append(("turn_out", 0, None))
            n = sum(map(len, by_slot.values()))
            return by_slot, n

        FULL = len(PIECES) + 3

        def bank_of(u, at):
            short = FULL - uses(u)[1] if isinstance(u, int) and u < 1 else 0
            return (at + short) % BANKS

        def before(u):
            if isinstance(u, int):
                return sum(uses(s)[1] for s in range(-1, u))
            return before(1) + (u - 1) * FULL

        def wait_prob(eng, m, i, hp):
            if i in DIAG:
                eng.wait_ge(masked, m * (2 * len(DIAG)) + 2 * DIAG.index(i) + hp + 1)
            else:
                eng.wait_ge(exp_done, m * SLOTS + 2 * i + hp + 1)

        def load_unit(sp, n, b3, d3):
            if not exists(n):
                return
            kit.ge_apart(sp, pv_chunks, (n - BUFS + 1) * NCH)
            batch, quad = (n >> 2) & (BATCH - 1), n & (QUADS - 1)
            src = of(parts_dram, batch)
            for which, st in ((0, q_st), (1, k_st)):
                for a in range(PARTS):
                    row0 = a * (PARTS * DH1)
                    for b in range(PARTS):
                        part = a if which == 0 else b
                        rows = src[which * PARTS + part].rearrange("(g h d) t -> g d h t", g=QUADS, h=QUAD)
                        sp.dma_start(st[b3][row0 + b * DH1:row0 + (b + 1) * DH1, :, :], of(rows, quad))\
                            .then_inc(st_loaded[b3], 16)
            sp.dma_start(v_st[b3][:], of(of(v_dram, batch), quad)).then_inc(st_loaded[b3], 16)

        def sp_step(sp, u, b3, d3):
            if not (isinstance(u, int) and u == -1):
                load_unit(sp, u + 2, (b3 + 2) % BUFS, d3(2))
            n, bn = u + 1, (b3 + 1) % BUFS
            if exists(n):
                for a, done in enumerate((hi_done, mid_done, lo_done)):
                    sp.wait_ge(done, n + 1)
                    row = q_st[bn][ROWS + a:ROWS + a + 1, :, :].rearrange("o h (t c) -> o (h t) c", c=P)
                    sp.dma_start(row, neg_part[:, a, :]).then_inc(m_stacked, 16)

        def pool_step(pool, u, b3, d3):
            if not exists(u):
                return
            for i in DIAG:
                for hp in range(2):
                    slot = 2 * i + hp
                    kit.ge_apart(pool, exp_done, u * SLOTS + slot + 1)
                    blk = prob[slot % RING][:, :, 0:P].rearrange("p h (g q) -> p h g q", q=PAGE)
                    nc.gpsimd.affine_select(out=blk, in_=blk, compare_op=ALU.is_ge, fill=0.0, base=PAGE - 1,
                                            pattern=[[0, 2], [PAGE, P // PAGE], [0, PAGE]], channel_multiplier=-1)\
                        .then_inc(masked, 1)

        def act_out(act, m, half):
            if not exists(m):
                return
            act.wait_ge(pv_chunks, m * NCH + HALF_END[half])
            ge(act, rs_done, m * 2 + half)
            nc.scalar.copy(ot[:, half, :], out_ps[:]).then_inc(out_evac[half], 1)

        def act_step(act, u, b3, d3):
            for s in range(SLOTS):
                i = s // 2
                if exists(u):
                    width = CHUNKS[i][2]
                    ge(act, pv_chunks, u * NCH + (s // 2 - RING // 2 + 1))
                    act.wait_ge(scored, u * SLOTS + s + 1)
                    nc.scalar.activation(prob[s % RING][:, :, 0:width], score_ps[:, s % 2, :, 0:width], ACT.Exp,
                                         scale=scale).then_inc(exp_done, 1)
                if s == 2:
                    act_out(act, u - 1, 1)
                if s == 10:
                    act_out(act, u, 0)

        def pe_scores(pe, u, b3, s, h2):
            i, hp = s // 2, s % 2
            half, j, width, _ = CHUNKS[i]
            q0 = half * HALF + HALF - width
            if s == 0 and h2 == 0:
                pe.wait_ge(m_stacked, u * (16 * PARTS) + 16 * PARTS)
            if h2 == 0:
                ge(pe, exp_done, u * SLOTS + s - 1)
            h = 2 * hp + h2
            mm = nc.tensor.matmul(score_ps[:, s % 2, h2, 0:width], k_st[b3][:, h, j * P:(j + 1) * P],
                                  q_st[b3][:, h, q0:q0 + width], start=True, stop=True)
            if h2 == 1:
                mm.then_inc(scored, 1)

        def pe_pv(pe, m, b3, i):
            half, j, width, _ = CHUNKS[i]
            wait_prob(pe, m, i, 0)
            wait_prob(pe, m, i, 1)
            if j == 0:
                ge(pe, out_evac[1 - half], m + half)
            last_j = max(c[1] for c in CHUNKS if c[0] == half)
            for h in range(QUAD):
                slot = (2 * i + h // 2) % RING
                mm = nc.tensor.matmul(out_ps[h * V_COLS:(h + 1) * V_COLS, HALF - width:HALF],
                                      v_st[b3][:, j, h, :], prob[slot][:, h % 2, 0:width],
                                      start=j == 0, stop=j == last_j)
            mm.then_inc(pv_chunks, 1)

        def pe_use(pe, u, b3, kind, arg, number, at):
            bank = bank_of(u, at)
            ge(pe, free, number if isinstance(u, int) and at < BANKS else number - (BANKS - 1))
            if kind == "max":
                ahead, h, t, c, key0, keys = arg
                bn = (b3 + ahead) % BUFS
                diagonal = key0 + keys == (t + 1) * P
                mm = nc.tensor.matmul(misc[:, bank, 0:keys], q_st[bn][0:ROWS, h, t * P:(t + 1) * P],
                                      k_st[bn][0:ROWS, h, key0:key0 + keys], start=True, stop=not diagonal)
                if diagonal:
                    mm = nc.tensor.matmul(misc[:, bank, keys - P:keys], identb[:], page_mask[:],
                                          start=False, stop=True)
            elif kind == "turn_max":
                pe.wait_ge(combined, u + 2)
                mm = nc.tensor.transpose(misc[0:QUAD * TILES, bank, 0:P], mx[(b3 + 1) % BUFS][0][:].rearrange("p h t -> p (h t)"),
                                         ident[:])
            else:
                m = u if arg == 0 else u - 1
                pe.wait_ge(out_evac[arg], m + 1)
                for t in range(TILES // 2):
                    mm = nc.tensor.transpose(misc[:, bank, t * P:(t + 1) * P], ot[:, arg, t * P:(t + 1) * P], ident[:])
            mm.then_inc(ready, 1)

        def numbered(u):
            by_slot, _ = uses(u)
            first = before(u)
            at = 0
            result = {}
            for s in range(SLOTS):
                result[s] = []
                for kind, arg, last in by_slot[s]:
                    result[s].append((kind, arg, last, first + at, at))
                    at += 1
            return result

        def pe_step(pe, u, b3, d3):
            numb = numbered(u)
            if isinstance(u, int) and u == -1:
                pe.wait_ge(masks_made, 2 + P // PAGE - 1)
            if isinstance(u, int) and u == -1:
                pe.wait_ge(st_loaded[0], 16 * ST_DMAS)
            for s in range(SLOTS):
                if s == MAX_SLOTS and exists(u + 2):
                    pe.wait_ge(st_loaded[(b3 + 2) % BUFS], d3(2) * (16 * ST_DMAS) + 16 * ST_DMAS)
                todo = numb[s][:]
                for h2 in range(2):
                    if todo:
                        kind, arg, last, number, at = todo.pop(0)
                        pe_use(pe, u, b3, kind, arg, number, at)
                    if exists(u):
                        pe_scores(pe, u, b3, s, h2)
                if s % 2 == 0:
                    i = s // 2 - PV_LAG
                    m, c, bm = (u, i, b3) if i >= 0 else (u - 1, NCH + i, (b3 - 1) % BUFS)
                    if exists(m):
                        pe_pv(pe, m, bm, c)
                for kind, arg, last, number, at in todo:
                    pe_use(pe, u, b3, kind, arg, number, at)

        def dve_use(dve, u, b3, kind, arg, last, number, at):
            bank = bank_of(u, at)
            dve.wait_ge(ready, number + 1)
            n = u + 1
            if kind == "max":
                ahead, h, t, c, key0, keys = arg
                m = mx[(b3 + ahead) % BUFS]
                nc.vector.tensor_reduce(m[c][:, h, t:t + 1], misc[:, bank, 0:keys], AX_X, ALU.max).then_inc(free, 1)
                if last:
                    dve.wait_ge(free, number + 1)
                    upper = slice(TILES // 2, TILES)
                    nc.vector.tensor_tensor(m[0][:, :, upper], m[0][:, :, upper], m[1][:, :, upper], ALU.max)\
                        .then_inc(combined, 1)
            elif kind == "turn_max":
                ge(dve, m_stacked, n * (16 * PARTS))
                nc.vector.tensor_scalar(neg[:], misc[0:QUAD * TILES, bank, 0:P], -1.0, None, ALU.mult)\
                    .then_inc(free, 1)
                dve.wait_ge(free, number + 1)
                nc.vector.tensor_copy(neg_part[:, 0, :], neg[:]).then_inc(hi_done, 1)
                dve.wait_ge(hi_done, n + 1)
                nc.vector.tensor_tensor(neg_rest[:], neg[:], neg_part[:, 0, :], ALU.subtract).then_inc(rest_done, 1)
                dve.wait_ge(rest_done, n + 1)
                nc.vector.tensor_copy(neg_part[:, 1, :], neg_rest[:]).then_inc(mid_done, 1)
                dve.wait_ge(mid_done, n + 1)
                nc.vector.tensor_tensor(neg_part[:, 2, :], neg_rest[:], neg_part[:, 1, :], ALU.subtract)\
                    .then_inc(lo_done, 1)
            else:
                m = u if arg == 0 else u - 1
                order = m * 2 + arg
                turned = misc[:, bank, :].rearrange("p (t h c) -> p t h c", t=TILES // 2, h=QUAD)
                ge(dve, free, number)
                nc.vector.reciprocal(rs[:], turned[:, :, :, DH1]).then_inc(rs_done, 1)
                dve.wait_ge(rs_done, order + 2)
                col0 = (m & (QUADS - 1)) * (QUAD * DH1)
                to = out[:].rearrange("p t c -> p (t c)")
                for t in range(TILES // 2):
                    rows = to[:, bass.ds(((m >> 2) & (BATCH - 1)) * SEQ + (arg * (TILES // 2) + t) * P + col0, QUAD * DH1)]
                    ins = nc.vector.tensor_tensor(rows.rearrange("p (h d) -> p h d", d=DH1), turned[:, t, :, 0:DH1],
                                                  rs[:, t, :].unsqueeze(2).to_broadcast([P, QUAD, DH1]), ALU.mult)
                ins.then_inc(free, 1)

        def dve_step(dve, u, b3, d3):
            numb = numbered(u)
            for s in range(SLOTS):
                for kind, arg, last, number, at in numb[s]:
                    dve_use(dve, u, b3, kind, arg, last, number, at)

        def steps(eng, step):
            def plain(u):
                step(eng, u, u % BUFS, lambda k: (u + k) // BUFS)
            for u in (-1, 0):
                plain(u)
            looped = (UNITS - BUFS) // BUFS
            with eng.Fori(0, looped) as it:
                for i in range(BUFS):
                    step(eng, it * BUFS + (1 + i), (1 + i) % BUFS, lambda k, i=i: it + (1 + i + k) // BUFS)
            for u in range(1 + looped * BUFS, UNITS + 1):
                plain(u)

        with nc.Block() as block:

            @block.sync
            def _(sp):
                sp.wait_ge(ones_made, 1)
                for i in range(BUFS):
                    sp.wait_ge(cleared[i], 2)
                    sp.dma_start(k_st[i][ROWS:ROWS + PARTS, :, :], ones_rows[:]).then_inc(ones_loaded, 16)
                    if i < 2:
                        load_unit(sp, i, i, None)
                sp.wait_ge(ones_loaded, 16 * BUFS)
                steps(sp, sp_step)

            @block.gpsimd
            def _(pool):
                for i in range(1, BUFS):
                    for st in (q_st[i], k_st[i]):
                        nc.gpsimd.memset(st[:].bitcast(F32), 0.0).then_inc(cleared[i], 1)
                steps(pool, pool_step)

            @block.scalar
            def _(act):
                steps(act, act_step)

            @block.tensor
            def _(pe):
                steps(pe, pe_step)

            @block.vector
            def _(dve):
                for st in (q_st[0], k_st[0]):
                    nc.vector.memset(st[64:P, :, :].bitcast(F32), 0.0).then_inc(cleared[0], 1)
                nc.vector.memset(ones_rows[:], 1.0).then_inc(ones_made, 1)
                nc.vector.tensor_copy(identb[:], ident[:]).then_inc(masks_made, 1)
                nc.vector.memset(page_mask[:], 0.0).then_inc(masks_made, 1)
                dve.wait_ge(masks_made, 2)
                for g in range(P // PAGE - 1):
                    nc.vector.memset(page_mask[g * PAGE:(g + 1) * PAGE, (g + 1) * PAGE:], NEGATIVE)\
                        .then_inc(masks_made, 1)
                dve.sem_inc(rs_done, 1)
                steps(dve, dve_step)


NEGATIVE = -3e38


def project_out1(nc, kit, sem, ident, x, heads, wo_dram):
    with ExitStack() as ctx:
        k = kit.scope(ctx)
        wo = k.sb("po_wo", [P, D])
        turned = k.sb("po_turned", [P, SEQ])
        turned_ps = k.ps("po_turned_ps", [P, SEQ])
        y_ps = k.ps("po_y", [P, SEQ])
        w_loaded, turn_done, turn_out, y_done, added = (sem(f"po_{n}") for n in ("w", "turn", "turn_out", "y", "added"))
        staged = sem("po_staged")
        hflat = heads[:].rearrange("p t c -> p (t c)")
        xflat = x[:].rearrange("p t d -> p (t d)")
        here = k.sb("po_here", [P, SEQ])

        with nc.Block() as block:

            @block.sync
            def _(sp):
                sp.dma_start(wo[:], wo_dram).then_inc(w_loaded, 16)

            @block.tensor
            def _(pe):
                pe.wait_ge(w_loaded, 16)
                with pe.Fori(0, BATCH) as b:
                    pe.wait_ge(staged, b + 1)
                    for t in range(TILES):
                        mm = nc.tensor.transpose(turned_ps[:, t * P:(t + 1) * P], here[:, t * P:(t + 1) * P], ident[:])
                    mm.then_inc(turn_done, 1)
                    pe.wait_ge(turn_out, b + 1)
                    pe.wait_ge(added, b + 1)
                    for t in range(TILES):
                        mm = nc.tensor.matmul(y_ps[:, t * P:(t + 1) * P], turned[:, t * P:(t + 1) * P], wo[:],
                                              start=True, stop=True)
                    mm.then_inc(y_done, 1)

            @block.scalar
            def _(act):
                with act.Fori(0, BATCH) as b:
                    act.wait_ge(turn_done, b + 1)
                    nc.scalar.copy(turned[:], turned_ps[:]).then_inc(turn_out, 1)

            @block.vector
            def _(dve):
                nc.vector.tensor_copy(here[:], hflat[:, 0:SEQ]).then_inc(staged, 1)
                dve.sem_inc(added, 1)
                with dve.Fori(0, BATCH) as b:
                    nxt = (b + 1) & (BATCH - 1)
                    dve.wait_ge(turn_done, b + 1)
                    nc.vector.tensor_copy(here[:], hflat[:, bass.ds(nxt * SEQ, SEQ)]).then_inc(staged, 1)
                    dve.wait_ge(y_done, b + 1)
                    rows = xflat[:, bass.ds(b * SEQ, SEQ)]
                    nc.vector.tensor_tensor(rows, rows, y_ps[:], ALU.add).then_inc(added, 1)


def norm_and_gate(nc, kit, sem, tag, x, ident, eps, gate_dram, bias_dram, xn_all, xt_all, logits, sp_work,
                  pool_work, dve_work):
    E = gate_dram.shape[1]
    with ExitStack() as ctx:
        k = kit.scope(ctx)
        norm = Norm(nc, k, sem, tag, x)
        gate = k.sb(f"{tag}_gate", [P, E])
        biases = 0 if bias_dram is None else bias_dram.shape[1]
        bias = k.sb(f"{tag}_bias", [P, max(biases, 1), E])
        xt = [k.sb(f"{tag}_xt{i}", [P, SEQ]) for i in range(2)]
        turned = [k.ps(f"{tag}_turned{i}", [P, SEQ]) for i in range(2)]
        gate_ps = [k.ps(f"{tag}_gate_ps{i}", [P, TILES, E]) for i in range(2)]
        loaded, turn_done, xt_done, gated, biased, kept = \
            (sem(f"{tag}_{n}") for n in ("loaded", "turn", "xt", "gated", "biased", "kept"))
        gated_free = sem(f"{tag}_gated_free")
        LOADS = 1 + (biases > 0)
        STEPS = max(biases, 1)
        keeps = 1 + (xt_all is not None)
        lflat = logits[:].rearrange("p t e -> p (t e)")

        def dve_logits(dve, b, p):
            dve.wait_ge(gated, b + 1)
            rows = lflat[:, bass.ds(b * (TILES * E), TILES * E)].rearrange("p (t e) -> p t e", e=E)
            if biases == 0:
                nc.vector.tensor_copy(rows, gate_ps[p][:]).then_inc(biased, 1)
            for i in range(biases):
                if i > 0:
                    dve.wait_ge(biased, b * STEPS + 2 * STEPS + i)
                nc.vector.tensor_tensor(rows, gate_ps[p][:] if i == 0 else rows,
                                        bias[:, i:i + 1, :].to_broadcast([P, TILES, E]), ALU.add).then_inc(biased, 1)

        with nc.Block() as block:

            @block.sync
            def _(sp):
                sp.dma_start(gate[:], gate_dram).then_inc(loaded, 16)
                if biases:
                    sp.dma_start(bias[:], bias_dram).then_inc(loaded, 16)
                sp_work(sp)

            @block.gpsimd
            def _(pool):
                pool_work(pool)

            @block.vector
            def _(dve):
                dve.sem_inc(kept, 2 * keeps)
                dve.sem_inc(biased, 2 * STEPS)
                norm.dve_statistics(dve)
                dve_work(dve)
                dve.wait_ge(loaded, 16 * LOADS)
                with dve.Fori(0, BATCH // 2) as it:
                    for p in range(2):
                        b = it * 2 + p
                        dve.wait_ge(kept, b * keeps + keeps)
                        norm.dve_xn(dve, b, p)
                    for p in range(2):
                        dve_logits(dve, it * 2 + p, p)

            @block.scalar
            def _(act):
                norm.act_std(act, eps)
                with act.Fori(0, BATCH // 2) as it:
                    for p in range(2):
                        b = it * 2 + p
                        act.wait_ge(turn_done, b + 1)
                        act.wait_ge(gated_free, b + 1)
                        nc.scalar.copy(xt[p][:], turned[p][:]).then_inc(xt_done, 1)
                        nc.scalar.copy(xn_all[:, bass.ds(b * TILES, TILES), 0:D], norm.xn[p][:])\
                            .then_inc(kept, 1)
                        if xt_all is not None:
                            nc.scalar.copy(xt_all[:, bass.ds(b * SEQ, SEQ)], turned[p][:]).then_inc(kept, 1)

            @block.tensor
            def _(pe):
                pe.wait_ge(loaded, 16 * LOADS)
                pe.sem_inc(gated_free, 2)
                with pe.Fori(0, BATCH // 2) as it:
                    for p in range(2):
                        b = it * 2 + p
                        pe.wait_ge(norm.xn_done, b + 1)
                        pe.wait_ge(kept, b * keeps + keeps)
                        for t in range(TILES):
                            last = nc.tensor.transpose(turned[p][:, t * P:(t + 1) * P], norm.xn[p][:, t, :], ident[:])
                        last.then_inc(turn_done, 1)
                    for p in range(2):
                        b = it * 2 + p
                        pe.wait_ge(xt_done, b + 1)
                        pe.wait_ge(biased, b * STEPS + STEPS)
                        for t in range(TILES):
                            last = nc.tensor.matmul(gate_ps[p][:, t, :], xt[p][:, t * P:(t + 1) * P], gate[:],
                                                    start=True, stop=True)
                        last.then_inc(gated, 1)
                        pe.wait_ge(gated, b + 1)
                        pe.sem_inc(gated_free, 1)


PACK = 4


def route(nc, kit, sem, tag, logits, choices, starts_dram, rows_of, weights, tile_expert):
    E = logits.shape[2]
    ENTRIES = choices * ALL_TILES
    SLOT_TILES = PACK * tile_expert.shape[1]
    FAR = -3e38
    with ExitStack() as ctx:
        k = kit.scope(ctx)
        shape, wide_shape = [P, ALL_TILES, E], [P, ENTRIES, E]
        m = [k.sb(f"{tag}_m{i}", [P, ALL_TILES]) for i in range(2)]
        at_max = k.sb(f"{tag}_at_max", shape)
        first = k.sb(f"{tag}_first", [P, ALL_TILES])
        number = k.sb(f"{tag}_number", [P, 1, E])
        one = k.sb(f"{tag}_one", wide_shape)
        left = k.sb(f"{tag}_left", shape)
        ex = k.sb(f"{tag}_ex", shape)
        below = k.sb(f"{tag}_below", [P, P])
        full = k.sb(f"{tag}_full", [P, P])
        scan = [k.sb(f"{tag}_scan{i}", wide_shape) for i in range(2)]
        place = k.sb(f"{tag}_place", wide_shape)
        row = k.sb(f"{tag}_row", [P, ENTRIES])
        count_int = k.sb(f"{tag}_count_int", [P, E], I32)
        padded = k.sb(f"{tag}_padded", [P, 1, E])
        ends = [k.sb(f"{tag}_ends{i}", [P, 1, E]) for i in range(2)]
        starts = k.sb(f"{tag}_starts", [1, SLOT_TILES, E])
        passed = k.sb(f"{tag}_passed", [1, SLOT_TILES, E])
        tile_number = k.sb(f"{tag}_tile_number", [1, SLOT_TILES])
        rank_ps = k.ps(f"{tag}_rank", wide_shape)
        total_ps = k.ps(f"{tag}_total_ps", wide_shape)
        step, exp_done, exp_in, made = (sem(f"{tag}_{n}") for n in ("step", "exp", "exp_in", "made"))
        loaded, chosen, counted = sem(f"{tag}_starts_loaded"), sem(f"{tag}_chosen"), sem(f"{tag}_counted")

        with nc.Block() as block:

            @block.sync
            def _(sp):
                sp.dma_start(starts[:], starts_dram).then_inc(loaded, 16)

            @block.gpsimd
            def _(pool):
                nc.gpsimd.memset(full[:], 1.0).then_inc(made, 1)
                pool.wait_ge(made, 1)
                nc.gpsimd.affine_select(out=below[:], in_=full[:], compare_op=ALU.is_gt, fill=0.0, base=0,
                                        pattern=[[1, P]], channel_multiplier=-1).then_inc(made, 1)

            @block.tensor
            def _(pe):
                pe.wait_ge(made, 2)
                pe.wait_ge(chosen, 1)
                nc.tensor.matmul(total_ps[:], full[:], one[:], start=True, stop=True).then_inc(counted, 1)
                nc.tensor.matmul(rank_ps[:], below[:], one[:], start=True, stop=True).then_inc(counted, 1)

            @block.vector
            def _(dve):
                done = 0

                def in_turn(ins):
                    nonlocal done
                    ins.then_inc(step, 1)
                    done += 1
                    dve.wait_ge(step, done)

                V = nc.vector
                for e in range(E):
                    V.memset(number[:, :, e:e + 1], float(e - E)).then_inc(step, 1)
                done = E
                dve.wait_ge(step, done)
                of_choice = [one[:, c * ALL_TILES:(c + 1) * ALL_TILES, :] for c in range(choices)]

                def wide(a, shape=shape):
                    return a.unsqueeze(2).to_broadcast(shape)

                for c in range(choices):
                    src = logits if c == 0 else left
                    in_turn(V.tensor_reduce(m[c][:], src[:], AX_X, ALU.max))
                    in_turn(V.tensor_tensor(at_max[:], src[:], wide(m[c][:]), ALU.is_ge))
                    in_turn(V.tensor_tensor(at_max[:], at_max[:], number[:].to_broadcast(shape), ALU.mult))
                    in_turn(V.tensor_reduce(first[:], at_max[:], AX_X, ALU.min))
                    in_turn(V.tensor_tensor(of_choice[c], number[:].to_broadcast(shape), wide(first[:]), ALU.is_equal))
                    if c + 1 < choices:
                        in_turn(V.scalar_tensor_tensor(left[:], of_choice[c], FAR, logits[:], ALU.mult, ALU.add))
                dve.sem_inc(chosen, 1)
                if choices == 2:
                    in_turn(V.tensor_tensor(left[:], logits[:], wide(m[0][:]), ALU.subtract))
                    in_turn(V.tensor_tensor(first[:], m[1][:], m[0][:], ALU.subtract))
                    dve.sem_inc(exp_in, 1)

                dve.wait_ge(counted, 1)
                in_turn(V.tensor_copy(scan[0][:], total_ps[:]))
                now, gap = 0, 1
                while gap < ENTRIES:
                    a, b = scan[now], scan[1 - now]
                    V.tensor_copy(b[:, 0:gap, :], a[:, 0:gap, :]).then_inc(step, 1)
                    V.tensor_tensor(b[:, gap:, :], a[:, gap:, :], a[:, 0:ENTRIES - gap, :], ALU.add).then_inc(step, 1)
                    done += 2
                    dve.wait_ge(step, done)
                    now, gap = 1 - now, gap * 2
                inclusive, exclusive = scan[now], scan[1 - now]
                in_turn(V.tensor_tensor(exclusive[:], inclusive[:], total_ps[:], ALU.subtract))
                in_turn(V.tensor_scalar(padded[:], inclusive[:, ENTRIES - 1:, :], float(P - 1), None, ALU.add))
                in_turn(V.tensor_copy(count_int[:], padded[:, 0, :]))
                in_turn(V.tensor_scalar(count_int[:], count_int[:], -P, None, ALU.bitwise_and))
                in_turn(V.tensor_copy(padded[:, 0, :], count_int[:]))
                in_turn(V.tensor_copy(ends[0][:], padded[:]))
                now, gap = 0, 1
                while gap < E:
                    a, b = ends[now], ends[1 - now]
                    V.tensor_copy(b[:, :, 0:gap], a[:, :, 0:gap]).then_inc(step, 1)
                    V.tensor_tensor(b[:, :, gap:], a[:, :, gap:], a[:, :, 0:E - gap], ALU.add).then_inc(step, 1)
                    done += 2
                    dve.wait_ge(step, done)
                    now, gap = 1 - now, gap * 2
                end, base = ends[now], ends[1 - now]
                in_turn(V.tensor_tensor(base[:], end[:], padded[:], ALU.subtract))
                dve.wait_ge(counted, 2)
                in_turn(V.tensor_tensor(place[:], exclusive[:], rank_ps[:], ALU.add))
                in_turn(V.tensor_tensor(place[:], place[:], base[:].to_broadcast(wide_shape), ALU.add))
                in_turn(V.tensor_tensor(place[:], place[:], one[:], ALU.mult))
                in_turn(V.tensor_reduce(row[:], place[:], AX_X, ALU.add))
                in_turn(V.tensor_copy(rows_of[:], row[:]))
                dve.wait_ge(loaded, 16)
                in_turn(V.tensor_tensor(passed[:], starts[:], end[0:1].to_broadcast([1, SLOT_TILES, E]), ALU.is_ge))
                in_turn(V.tensor_reduce(tile_number[:], passed[:], AX_X, ALU.add))
                in_turn(V.tensor_scalar(tile_number[:], tile_number[:], float(E - 1), None, ALU.min))
                groups = tile_number[:].rearrange("o (g i) -> o g i", i=PACK)
                for i in range(PACK - 1, 0, -1):
                    in_turn(V.scalar_tensor_tensor(groups[:, :, i - 1], groups[:, :, i], float(E), groups[:, :, i - 1],
                                                   ALU.mult, ALU.add))
                in_turn(V.tensor_copy(tile_expert[:], groups[:, :, 0]))
                if choices == 2:
                    dve.wait_ge(exp_done, 2)
                    in_turn(V.tensor_reduce(m[0][:], ex[:], AX_X, ALU.add))
                    in_turn(V.reciprocal(weights[:, 0:ALL_TILES], m[0][:]))
                    in_turn(V.tensor_tensor(weights[:, ALL_TILES:], first[:], weights[:, 0:ALL_TILES], ALU.mult))

            @block.scalar
            def _(act):
                if choices == 2:
                    act.wait_ge(exp_in, 1)
                    nc.scalar.activation(ex[:], left[:], ACT.Exp).then_inc(exp_done, 1)
                    nc.scalar.activation(first[:], first[:], ACT.Exp).then_inc(exp_done, 1)


def scatter_rows(nc, pool, xn_all, rows_of, choices, shift, buffer_dram, scattered, renumbered):
    number = xn_all[:, :, D]
    for c in range(choices):
        if c > 0:
            pool.wait_ge(scattered, 16 * c * ALL_TILES)
            nc.gpsimd.tensor_tensor(number, number, shift[:], ALU.add).then_inc(renumbered, 1)
            pool.wait_ge(renumbered, c)
        for t in range(ALL_TILES):
            entry = c * ALL_TILES + t
            nc.gpsimd.indirect_dma_start(
                out=buffer_dram, out_offset=bass.IndirectOffsetOnAxis(ap=rows_of[:, entry:entry + 1], axis=0),
                in_=xn_all[:, t, :], in_offset=None).then_inc(scattered, 16)
    pool.wait_ge(scattered, 16 * choices * ALL_TILES)


def expert_tiles(nc, kit, sem, tag, ident, tile_expert, wa_all, wb_all, NC, gated, biased, x_rows, y_entries):
    E, A = wa_all.shape[1:]
    B = wb_all.shape[2]
    N = x_rows.shape[0]
    HID = NC * P
    START = 7
    assert E == 8
    XS, AHEAD = 4, 3
    with ExitStack() as ctx:
        k = kit.scope(ctx)
        wa = [k.sb(f"{tag}_wa{i}", [P, A]) for i in range(2)]
        wb = [k.sb(f"{tag}_wb{i}", [P, B]) for i in range(2)]
        xs = [k.sb(f"{tag}_xs{i}", [P, D + 1]) for i in range(XS)]
        entry = [k.sb(f"{tag}_entry{i}", [P, 1], U32) for i in range(XS)]
        xst = [k.sb(f"{tag}_xst{i}", [P, P]) for i in range(2)]
        silu = [k.sb(f"{tag}_silu{i}", [P, HID]) for i in range(2)] if gated else None
        ht = [k.sb(f"{tag}_ht{i}", [P, HID]) for i in range(2)]
        ys = [k.sb(f"{tag}_ys{i}", [P, D]) for i in range(XS)]
        turned = [k.ps(f"{tag}_turned{i}", [P, HALF]) for i in range(2)]
        y_ps = [k.ps(f"{tag}_y{i}", [P, HALF]) for i in range(2)]
        h_ps = [k.ps(f"{tag}_h{i}", [P, HALF]) for i in range(2)]
        g_ps = [k.ps(f"{tag}_g{i}", [P, HALF]) for i in range(2)] if gated else None
        x_loaded = [sem(f"{tag}_x_loaded{i}") for i in range(XS)]
        stored = [sem(f"{tag}_stored{i}") for i in range(XS)]
        entry_done = sem(f"{tag}_entry")
        turn_done, xst_done, wa_done, wb_done, h_done, silu_done, ht_done, y_done, y_out = \
            (sem(f"{tag}_{n}") for n in ("turn", "xst", "wa", "wb", "h", "silu", "ht", "y", "y_out"))
        wa_flat = wa_all[:].rearrange("p e c -> p (e c)")
        wb_flat = wb_all[:].rearrange("p e c -> p (e c)")

        def exists(u):
            return not isinstance(u, int) or 0 <= u < N

        def load(sp, n, q):
            if exists(n):
                kit.ge_apart(sp, turn_done, n - XS + 1)
                kit.ge_apart(sp, entry_done, n - XS + 1)
                sp.dma_start(xs[q][:], of(x_rows, n)).then_inc(x_loaded[q], 16)

        def sp_step(sp, u, q):
            load(sp, u + AHEAD, (q + AHEAD) % XS)

        def pool_step(pool, u, q):
            m, r = u - 1, (q - 1) % XS
            if exists(m):
                kit.ge_apart(pool, y_out, m + 1)
                kit.ge_apart(pool, entry_done, m + 1)
                nc.gpsimd.indirect_dma_start(
                    out=y_entries, out_offset=bass.IndirectOffsetOnAxis(ap=entry[r][:], axis=0),
                    in_=ys[r][:], in_offset=None).then_inc(stored[r], 16)

        def pe_step(pe, u, q):
            p = q % 2
            n, pn = u + 1, 1 - p
            if exists(n):
                pe.wait_ge(x_loaded[(q + 1) % XS], ((n >> 2) << 4) + 16)
                ge(pe, xst_done, n - 1)
                nc.tensor.transpose(turned[pn][:, 0:P], xs[(q + 1) % XS][:, 0:D], ident[:]).then_inc(turn_done, 1)
            if exists(u):
                pe.wait_ge(xst_done, u + 1)
                pe.wait_ge(wa_done, u + 1)
                ge(pe, ht_done, u - 1)
                for c in range(NC):
                    mm = nc.tensor.matmul(h_ps[p][:, c * P:(c + 1) * P], wa[p][:, c * P:(c + 1) * P], xst[p][:],
                                          start=True, stop=True)
                if gated:
                    for c in range(NC):
                        mm = nc.tensor.matmul(g_ps[p][:, c * P:(c + 1) * P], wa[p][:, HID + c * P:HID + (c + 1) * P],
                                              xst[p][:], start=True, stop=True)
                mm.then_inc(h_done, 1)
            m, pm = u - 1, 1 - p
            if exists(m):
                pe.wait_ge(ht_done, m + 1)
                pe.wait_ge(wb_done, m + 1)
                ge(pe, y_out, m - 1)
                for c in range(NC):
                    mm = nc.tensor.matmul(y_ps[pm][:, 0:D], ht[pm][:, c * P:(c + 1) * P],
                                          wb[pm][:, c * P:(c + 1) * P], start=c == 0, stop=c == NC - 1)
                mm.then_inc(y_done, 1)

        def y_evac(eng, m, pm, r):
            eng.wait_ge(y_done, m + 1)
            if exists(m - XS):
                ge(eng, stored[r], (m >> 2) << 4)
            y = y_ps[pm][:, 0:D]
            if biased:
                nc.vector.tensor_tensor(ys[r][:], y, wb[pm][:, HID:HID + D], ALU.add).then_inc(y_out, 1)
            else:
                nc.scalar.copy(ys[r][:], y).then_inc(y_out, 1)

        def act_step(act, u, q):
            p = q % 2
            n, pn = u + 1, 1 - p
            if exists(n):
                act.wait_ge(turn_done, n + 1)
                ge(act, h_done, n - 1)
                nc.scalar.copy(xst[pn][:], turned[pn][:, 0:P]).then_inc(xst_done, 1)
            if exists(u):
                act.wait_ge(h_done, u + 1)
                ge(act, y_done, u - 1)
                if gated:
                    nc.scalar.activation(silu[p][:], h_ps[p][:, 0:HID], ACT.Silu).then_inc(silu_done, 1)
                else:
                    for c in range(NC):
                        last = nc.scalar.activation(ht[p][:, c * P:(c + 1) * P], h_ps[p][:, c * P:(c + 1) * P],
                                                    ACT.Relu, bias=wa[p][:, HID + c:HID + c + 1])
                    last.then_inc(ht_done, 1)
            if exists(u - 1) and not biased:
                y_evac(act, u - 1, 1 - p, (q - 1) % XS)

        pack = []

        def load_pack(group):
            pack[:] = [nc.vector.value_load(tile_expert[0:1, bass.ds(group, 1)], min_val=0, max_val=E ** PACK - 1)]

        def dve_step(dve, u, q):
            p = q % 2
            n, pn = u + 1, 1 - p
            if exists(n):
                place = (q + 1) % PACK
                if place == 0:
                    load_pack(n // PACK if isinstance(n, int) else n >> 2)
                expert = (pack[0] >> (3 * place)) & (E - 1)
                ge(dve, h_done, n - 1)
                if not gated:
                    ge(dve, ht_done, n - 1)
                nc.vector.tensor_copy(wa[pn][:], wa_flat[:, bass.ds(expert * A, A)]).then_inc(wa_done, 1)
                r = (q + 1) % XS
                dve.wait_ge(x_loaded[r], ((n >> 2) << 4) + 16)
                if exists(n - XS):
                    ge(dve, stored[r], (n >> 2) << 4)
                nc.vector.tensor_copy(entry[r][:], xs[r][:, D:D + 1]).then_inc(entry_done, 1)
            if exists(u) and gated:
                dve.wait_ge(silu_done, u + 1)
                nc.vector.tensor_tensor(ht[p][:], silu[p][:], g_ps[p][:, 0:HID], ALU.mult).then_inc(ht_done, 1)
            if exists(u - 1) and biased:
                y_evac(dve, u - 1, 1 - p, (q - 1) % XS)
            if exists(n):
                ge(dve, y_done, n - 1)
                if biased:
                    ge(dve, y_out, n - 1)
                nc.vector.tensor_copy(wb[pn][:], wb_flat[:, bass.ds(expert * B, B)]).then_inc(wb_done, 1)

        def steps(eng, step):
            for u in range(-1, START):
                step(eng, u, u % XS)
            looped = (N - AHEAD - START) // XS
            with eng.Fori(0, looped) as it:
                for i in range(XS):
                    step(eng, it * XS + (START + i), (START + i) % XS)
            for u in range(START + XS * looped, N + 1):
                step(eng, u, u % XS)

        with nc.Block() as block:

            @block.sync
            def _(sp):
                for n in range(AHEAD - 1):
                    load(sp, n, n)
                steps(sp, sp_step)

            @block.gpsimd
            def _(pool):
                steps(pool, pool_step)
                for r in range(XS):
                    pool.wait_ge(stored[r], 16 * ((N + XS - 1 - r) // XS))

            @block.tensor
            def _(pe):
                steps(pe, pe_step)

            @block.scalar
            def _(act):
                steps(act, act_step)

            @block.vector
            def _(dve):
                steps(dve, dve_step)


def add_entries(nc, kit, sem, tag, x, weights, entries_dram, choices, out):
    RING = 4
    with ExitStack() as ctx:
        k = kit.scope(ctx)
        got = k.sb(f"{tag}_got", [P, RING, TILES, D])
        arrived = [sem(f"{tag}_arrived{i}") for i in range(RING)]
        added, stored = sem(f"{tag}_added"), sem(f"{tag}_stored")
        per_part = 1 if weights is None else 2
        parts = [(b, c) for b in range(BATCH) for c in range(choices)]

        with nc.Block() as block:

            @block.sync
            def _(sp):
                for n, (b, c) in enumerate(parts):
                    ge(sp, added, (n - RING + 1) * per_part)
                    first = (c * ALL_TILES + b * TILES) * P
                    sp.dma_start(got[:, n % RING, :, :],
                                 entries_dram[first:first + SEQ, :].rearrange("(t p) d -> p t d", p=P))\
                        .then_inc(arrived[n % RING], 16)

            @block.scalar
            def _(act):
                if out is not None:
                    for b in range(BATCH):
                        act.wait_ge(added, (b + 1) * choices * per_part)
                        act.dma_start(out[b].rearrange("(t p) d -> p t d", p=P), x[:, b * TILES:(b + 1) * TILES, :])\
                            .then_inc(stored, 16)
                    act.wait_ge(stored, 16 * BATCH)

            @block.vector
            def _(dve):
                for n, (b, c) in enumerate(parts):
                    dve.wait_ge(arrived[n % RING], 16 * (n // RING + 1))
                    part = got[:, n % RING, :, :]
                    if weights is not None:
                        first = c * ALL_TILES + b * TILES
                        nc.vector.tensor_tensor(part, part, weights[:, first:first + TILES].unsqueeze(2)
                                                .to_broadcast([P, TILES, D]), ALU.mult).then_inc(added, 1)
                        dve.wait_ge(added, n * per_part + 1)
                    to = x[:, b * TILES:(b + 1) * TILES, :]
                    nc.vector.tensor_tensor(to, to, part, ALU.add).then_inc(added, 1)


def shared_expert(nc, kit, sem, tag, x, xt_all, w1_dram, w3_dram, w2_dram, meanwhile):
    ROWS, NC = w2_dram.shape[:2]
    FF = w1_dram.shape[1]
    BLOCKS = TOKENS // HALF
    BT = HALF // P
    with ExitStack() as ctx:
        k = kit.scope(ctx)
        w1 = k.sb(f"{tag}_w1", [P, FF])
        w3 = k.sb(f"{tag}_w3", [P, FF])
        w2 = k.sb(f"{tag}_w2", [ROWS, NC, D])
        silu = [k.sb(f"{tag}_silu{i}", [ROWS, NC, HALF]) for i in range(2)]
        ht = [k.sb(f"{tag}_ht{i}", [ROWS, NC, HALF]) for i in range(2)]
        h_ps = k.ps(f"{tag}_h", [P, NC, HALF])
        g_ps = k.ps(f"{tag}_g", [P, NC, HALF])
        y_ps = k.ps(f"{tag}_y", [P, 2, HALF])
        loaded = sem(f"{tag}_loaded")
        h_done, ht_done, silu_done, y_done, added = (sem(f"{tag}_{n}") for n in ("h", "ht", "silu", "y", "added"))
        xflat = x[:].rearrange("p t d -> p (t d)")

        with nc.Block() as block:

            @block.sync
            def _(sp):
                sp.dma_start(w1[:], w1_dram).then_inc(loaded, 16)
                sp.dma_start(w3[:], w3_dram).then_inc(loaded, 16)
                sp.dma_start(w2[:], w2_dram).then_inc(loaded, 16)

            @block.gpsimd
            def _(pool):
                meanwhile(pool)

            @block.tensor
            def _(pe):
                def up(n):
                    for c in range(NC):
                        pe.wait_ge(ht_done, n * NC + c + 1)
                        rhs = xt_all[:, bass.ds(n * HALF, HALF)]
                        cols = slice(c * ROWS, (c + 1) * ROWS)
                        nc.tensor.matmul(h_ps[0:ROWS, c, :], w1[:, cols], rhs, start=True, stop=True)
                        nc.tensor.matmul(g_ps[0:ROWS, c, :], w3[:, cols], rhs, start=True, stop=True)\
                            .then_inc(h_done, 1)

                def down(n, par):
                    pe.wait_ge(ht_done, n * NC + 2 * NC)
                    pe.wait_ge(added, n + 1)
                    for t in range(BT):
                        for c in range(NC):
                            mm = nc.tensor.matmul(y_ps[:, par, t * P:(t + 1) * P], ht[par][:, c, t * P:(t + 1) * P],
                                                  w2[:, c, :], start=c == 0, stop=c == NC - 1)
                    mm.then_inc(y_done, 1)

                pe.wait_ge(loaded, 48)
                with pe.Fori(0, BLOCKS // 2) as it:
                    up(it * 2)
                    up(it * 2 + 1)
                    down(it * 2, 0)
                    down(it * 2 + 1, 1)

            @block.scalar
            def _(act):
                with act.Fori(0, BLOCKS // 2) as it:
                    for par in range(2):
                        n = it * 2 + par
                        for c in range(NC):
                            act.wait_ge(h_done, n * NC + c + 1)
                            act.wait_ge(ht_done, n * NC + c + 1)
                            nc.scalar.activation(silu[par][:, c, :], h_ps[0:ROWS, c, :], ACT.Silu)\
                                .then_inc(silu_done, 1)

            @block.vector
            def _(dve):
                dve.sem_inc(ht_done, NC)
                dve.sem_inc(added, 2)
                dve.sem_inc(y_done, 2)
                with dve.Fori(0, BLOCKS // 2) as it:
                    for par in range(2):
                        n = it * 2 + par
                        dve.wait_ge(y_done, n + 1)
                        for c in range(NC):
                            dve.wait_ge(silu_done, n * NC + c + 1)
                            nc.vector.tensor_tensor(ht[par][:, c, :], silu[par][:, c, :], g_ps[0:ROWS, c, :],
                                                    ALU.mult).then_inc(ht_done, 1)
                    for par in range(2):
                        n = it * 2 + par
                        dve.wait_ge(y_done, n + 3)
                        rows = xflat[:, bass.ds(n * HALF, HALF)]
                        nc.vector.tensor_tensor(rows, rows, y_ps[:, par, :], ALU.add).then_inc(added, 1)


def tiles_of_rows(choices, experts):
    return choices * ALL_TILES + experts - 1


def ffn0(nc, kit, sem, x, ident, eps, gate_dram, bias_dram, starts_dram, numbers_dram, wa_dram, wb_dram):
    E = gate_dram.shape[1]
    N = tiles_of_rows(1, E)
    x_rows = nc.dram_tensor("f0_x_rows", [N, P, D + 1], F32).ap()
    y_entries = nc.dram_tensor("f0_y_entries", [1 * TOKENS + N * P, D], F32).ap()
    with ExitStack() as ctx:
        k = kit.scope(ctx)
        rows_of = k.sb("f0_rows_of", [P, ALL_TILES], U32)
        tile_expert = k.sb("f0_tile_expert", [1, -(-N // PACK)], I32)
        wa_all = k.sb("f0_wa_all", wa_dram.shape)
        wb_all = k.sb("f0_wb_all", wb_dram.shape)
        with ExitStack() as gate_ctx:
            g = k.scope(gate_ctx)
            xn_all = g.sb("f0_xn_all", [P, ALL_TILES, D + 1])
            numbers = g.sb("f0_numbers", [P, ALL_TILES + N])
            logits = g.sb("f0_logits", [P, ALL_TILES, E])
            blank = g.sb("f0_blank", [P, N, D + 1])
            cleared, w_loaded = sem("f0_cleared"), sem("f0_w_loaded")
            numbers_loaded, numbered, blank_made = (sem(f"f0_{n}") for n in ("numbers_loaded", "numbered", "blank_made"))

            def sp_work(sp):
                sp.dma_start(numbers[:], numbers_dram).then_inc(numbers_loaded, 16)
                sp.dma_start(wa_all[:], wa_dram).then_inc(w_loaded, 16)
                sp.dma_start(wb_all[:], wb_dram).then_inc(w_loaded, 16)
                sp.wait_ge(blank_made, 2)
                sp.dma_start(x_rows.rearrange("n p d -> p n d"), blank[:]).then_inc(cleared, 16)
                sp.wait_ge(cleared, 16)
                sp.wait_ge(w_loaded, 32)

            def pool_work(pool):
                nc.gpsimd.memset(blank[:], 0.0).then_inc(blank_made, 1)
                pool.wait_ge(numbers_loaded, 16)
                pool.wait_ge(blank_made, 1)
                nc.gpsimd.tensor_copy(blank[:, :, D], numbers[:, ALL_TILES:]).then_inc(blank_made, 1)

            def dve_work(dve):
                dve.wait_ge(numbers_loaded, 16)
                nc.vector.tensor_copy(xn_all[:, :, D], numbers[:, 0:ALL_TILES]).then_inc(numbered, 1)

            norm_and_gate(nc, g, sem, "g0", x, ident, eps, gate_dram, bias_dram, xn_all, None, logits,
                          sp_work, pool_work, dve_work)
            route(nc, g, sem, "r0", logits, 1, starts_dram, rows_of, None, tile_expert)
            scattered = sem("f0_scattered")
            with nc.Block() as block:

                @block.gpsimd
                def _(pool):
                    scatter_rows(nc, pool, xn_all, rows_of, 1, None, x_rows.rearrange("n p d -> (n p) d"),
                                 scattered, None)

        expert_tiles(nc, k, sem, "e0", ident, tile_expert, wa_all, wb_all, 4, False, True, x_rows, y_entries)
        add_entries(nc, k, sem, "add0", x, None, y_entries, 1, None)


def ffn1(nc, kit, sem, x, ident, eps, gate_dram, starts_dram, numbers_dram, wa_dram, wb_dram, sw1_dram, sw3_dram, sw2_dram,
         out):
    E = gate_dram.shape[1]
    N = tiles_of_rows(2, E)
    x_rows = nc.dram_tensor("f1_x_rows", [N, P, D + 1], F32).ap()
    y_entries = nc.dram_tensor("f1_y_entries", [2 * TOKENS + N * P, D], F32).ap()
    with ExitStack() as ctx:
        k = kit.scope(ctx)
        rows_of = k.sb("f1_rows_of", [P, 2 * ALL_TILES], U32)
        weights = k.sb("f1_weights", [P, 2 * ALL_TILES])
        tile_expert = k.sb("f1_tile_expert", [1, -(-N // PACK)], I32)
        wa_all = k.sb("f1_wa_all", wa_dram.shape)
        wb_all = k.sb("f1_wb_all", wb_dram.shape)
        with ExitStack() as gate_ctx:
            g = k.scope(gate_ctx)
            xn_all = g.sb("f1_xn_all", [P, ALL_TILES, D + 1])
            numbers = g.sb("f1_numbers", [P, ALL_TILES + N])
            xt_all = g.sb("f1_xt_all", [P, TOKENS])
            logits = g.sb("f1_logits", [P, ALL_TILES, E])
            blank = g.sb("f1_blank", [P, N, D + 1])
            cleared, w_loaded = sem("f1_cleared"), sem("f1_w_loaded")
            numbers_loaded, numbered, blank_made = (sem(f"f1_{n}") for n in ("numbers_loaded", "numbered", "blank_made"))

            def sp_work(sp):
                sp.dma_start(numbers[:], numbers_dram).then_inc(numbers_loaded, 16)
                sp.dma_start(wa_all[:], wa_dram).then_inc(w_loaded, 16)
                sp.dma_start(wb_all[:], wb_dram).then_inc(w_loaded, 16)
                sp.wait_ge(blank_made, 2)
                sp.dma_start(x_rows.rearrange("n p d -> p n d"), blank[:]).then_inc(cleared, 16)
                sp.wait_ge(cleared, 16)
                sp.wait_ge(w_loaded, 32)

            def pool_work(pool):
                nc.gpsimd.memset(blank[:], 0.0).then_inc(blank_made, 1)
                pool.wait_ge(numbers_loaded, 16)
                pool.wait_ge(blank_made, 1)
                nc.gpsimd.tensor_copy(blank[:, :, D], numbers[:, ALL_TILES:]).then_inc(blank_made, 1)

            def dve_work(dve):
                dve.wait_ge(numbers_loaded, 16)
                nc.vector.tensor_copy(xn_all[:, :, D], numbers[:, 0:ALL_TILES]).then_inc(numbered, 1)

            norm_and_gate(nc, g, sem, "g1", x, ident, eps, gate_dram, None, xn_all, xt_all, logits,
                          sp_work, pool_work, dve_work)
            route(nc, g, sem, "r1", logits, 2, starts_dram, rows_of, weights, tile_expert)
            shift = g.sb("f1_shift", [P, ALL_TILES])
            scattered, shift_made, renumbered = (sem(f"f1_{n}") for n in ("scattered", "shift_made", "renumbered"))

            def meanwhile(pool):
                nc.gpsimd.memset(shift[:], float(TOKENS)).then_inc(shift_made, 1)
                pool.wait_ge(shift_made, 1)
                scatter_rows(nc, pool, xn_all, rows_of, 2, shift, x_rows.rearrange("n p d -> (n p) d"),
                             scattered, renumbered)

            shared_expert(nc, g, sem, "es", x, xt_all, sw1_dram, sw3_dram, sw2_dram, meanwhile)
        expert_tiles(nc, k, sem, "e1", ident, tile_expert, wa_all, wb_all, 3, True, False, x_rows, y_entries)
        add_entries(nc, k, sem, "add1", x, weights, y_entries, 2, out)


def transformer_kernel(nc, x_in, l0_attn_w, gate0, gate0_bias, starts0, numbers0, wa_0, wb_0,
                       wq, w_down, wk_up, wv_up, wo, rope, gate1, starts1, numbers1,
                       wa_1, wb_1, sw1, sw3, sw2, out):
    DH0, CLAMP = 64, 50.0
    with ExitStack() as ctx:
        kit = Kit(nc, ctx, ctx.enter_context(nc.semaphore("passed")))

        def in_stage(stage, *args):
            taken = []

            def sem(name):
                taken.append(nc.alloc_semaphore(name=name))
                return taken[-1]

            stage(nc, kit, sem, *args)
            nc.clear_and_free_semaphores(taken)
            nc.all_engine_barrier()

        x = kit.sb("x", [P, ALL_TILES, D])
        ident = kit.sb("ident", [P, P])
        ones = kit.sb("ones", [P, 32])
        eps = kit.sb("eps", [P, 1])
        xt0 = nc.dram_tensor("xt0", [BATCH, 3, P, SEQ], F32).ap()
        xt1 = nc.dram_tensor("xt1", [BATCH, 3, P, SEQ], F32).ap()
        parts = nc.dram_tensor("qk_parts", [BATCH, 2 * PARTS, P, SEQ], BF16).ap()
        values = nc.dram_tensor("values", [BATCH, QUADS, P, TILES, QUAD, V_COLS], F32).ap()

        in_stage(load_residual, x_in, x, ident, ones, eps)
        in_stage(layernorm, "ln0", x, ident, eps, xt0)
        in_stage(attention0, x, xt0, l0_attn_w, ones, DH0 ** -0.5, CLAMP)
        in_stage(ffn0, x, ident, eps, gate0, gate0_bias, starts0, numbers0, wa_0, wb_0)
        in_stage(layernorm, "ln1", x, ident, eps, xt1)
        in_stage(project1, ident, xt1, wq, w_down, wk_up, wv_up, rope, parts, values)
        with ExitStack() as heads_ctx:
            heads = kit.scope(heads_ctx).sb("heads", [P, ALL_TILES, D])
            in_stage(attention1, ident, parts, values, heads, DH1 ** -0.5)
            in_stage(project_out1, ident, x, heads, wo)
        in_stage(ffn1, x, ident, eps, gate1, starts1, numbers1, wa_1, wb_1, sw1, sw3, sw2, out)


def _rope_constants():
    import numpy as np
    theta = 10000.0
    inverse = 1.0 / theta ** (np.arange(0, DH1, 2, dtype=np.float32) / DH1)
    angle = np.outer(np.arange(SEQ, dtype=np.float32), inverse)
    table = np.empty((D, 2, SEQ), np.float32)
    for d in range(D):
        pair = d % DH1 // 2
        table[d, 0] = np.cos(angle[:, pair])
        table[d, 1] = np.sin(angle[:, pair]) * (-1 if d % 2 == 0 else 1)
    return table


def kernel(L0_attn_x, L0_attn_Wq, L0_attn_Wk, L0_attn_Wv, L0_attn_Wo, L0_ffn_gate_w, L0_ffn_gate_b,
           L0_ffn_expert_bias, L0_ffn_w1, L0_ffn_b1, L0_ffn_w2, L0_ffn_b2, L1_attn_wq, L1_attn_w_down,
           L1_attn_wk_up, L1_attn_wv_up, L1_attn_wo, L1_ffn_gate_w, L1_ffn_w1, L1_ffn_w2, L1_ffn_w3,
           L1_ffn_sw1, L1_ffn_sw2, L1_ffn_sw3):
    import numpy as np
    import concourse.bacc as bacc
    from concourse.bass_utils import run_bass_kernel_spmd

    a = np.asarray
    pairs = L0_attn_Wq.shape[0] // P

    def chunked(w, rows):
        w = a(w)
        n = -(-w.shape[1] // rows)
        w = np.pad(w, ((0, 0), (0, n * rows - w.shape[1]), (0, 0)))
        return w.reshape(w.shape[0], n, rows, D).transpose(2, 0, 1, 3).reshape(rows, w.shape[0], n * D)

    def whole_chunks(w):
        w = a(w).transpose(1, 0, 2)
        return np.pad(w, ((0, 0), (0, 0), (0, -w.shape[2] % P)))

    def starts(choices, experts):
        n = -(-tiles_of_rows(choices, experts) // PACK) * PACK
        return np.broadcast_to((np.arange(n, dtype=np.float32) * P)[None, :, None], (1, n, experts))

    def numbers(choices, experts):
        tiles = np.concatenate([np.arange(ALL_TILES), choices * ALL_TILES + np.arange(tiles_of_rows(choices, experts))])
        return (tiles[None] * P + np.arange(P)[:, None]).astype(np.float32)

    exchanged = np.arange(D) ^ 1
    by_pair = [a(w).reshape(pairs, P, D).transpose(0, 2, 1) for w in (L0_attn_Wq, L0_attn_Wk, L0_attn_Wv)]
    by_pair.append(a(L0_attn_Wo).T.reshape(pairs, P, D))
    experts = L0_ffn_gate_b.shape[0]
    shared_rows = L1_ffn_sw2.shape[0] // 2
    laid_out = {
        "x": a(L0_attn_x),
        "l0_attn_w": np.stack(by_pair, 2),
        "gate0": a(L0_ffn_gate_w).T,
        "gate0_bias": np.broadcast_to(np.stack([a(L0_ffn_gate_b), a(L0_ffn_expert_bias)]), (P, 2, experts)),
        "starts0": starts(1, experts),
        "numbers0": numbers(1, experts),
        "wa_0": np.concatenate([a(L0_ffn_w1).transpose(1, 0, 2),
                                a(L0_ffn_b1).reshape(experts, -1, P).transpose(2, 0, 1)], 2),
        "wb_0": np.concatenate([chunked(L0_ffn_w2, P), np.broadcast_to(a(L0_ffn_b2), (P, experts, D))], 2),
        "wq": np.stack([a(L1_attn_wq), a(L1_attn_wq)[:, exchanged]], 1),
        "w_down": a(L1_attn_w_down),
        "wk_up": np.stack([a(L1_attn_wk_up), a(L1_attn_wk_up)[:, exchanged]], 1),
        "wv_up": a(L1_attn_wv_up),
        "wo": a(L1_attn_wo),
        "rope": _rope_constants(),
        "gate1": a(L1_ffn_gate_w).T,
        "starts1": starts(2, experts),
        "numbers1": numbers(2, experts),
        "wa_1": np.concatenate([whole_chunks(L1_ffn_w1), whole_chunks(L1_ffn_w3)], 2),
        "wb_1": chunked(L1_ffn_w2, P),
        "sw1": a(L1_ffn_sw1),
        "sw3": a(L1_ffn_sw3),
        "sw2": chunked(a(L1_ffn_sw2)[None], shared_rows).reshape(shared_rows, -1, D),
    }
    nc = bacc.Bacc("TRN2", target_bir_lowering=False, num_devices=1)
    arrays, args = {}, []
    for name, array in laid_out.items():
        array = np.ascontiguousarray(array)
        arrays[f"in_{name}"] = array
        args.append(nc.dram_tensor(f"in_{name}", array.shape, mybir.dt.from_np(array.dtype), kind="ExternalInput").ap())
    out = nc.dram_tensor("out_x", (BATCH, SEQ, D), F32, kind="ExternalOutput").ap()
    transformer_kernel(nc, *args, out)
    result = run_bass_kernel_spmd(nc, [arrays], core_ids=[0])
    return result.results[0]["out_x"]
```
